# Optimizing a Trainium2 kernel written in Bass

```python
import numpy as np
import jax
import jax.numpy as jnp

def _softmax(x, axis=-1):
    return jax.nn.softmax(x, axis=axis)

def _gelu(x):
    return jax.nn.gelu(x, approximate=True)

def _silu(x):
    return jax.nn.silu(x)

def _sigmoid(x):
    return jax.nn.sigmoid(x)

def _layernorm(x, axis=-1, eps=1e-05):
    m = jnp.mean(x, axis=axis, keepdims=True)
    v = jnp.var(x, axis=axis, keepdims=True)
    return (x - m) / jnp.sqrt(v + eps)

def _scatter_add(tgt, idx, src, axis=0):
    return tgt.at[idx].add(src)

def _segment_sum(src, seg, n):
    return jax.ops.segment_sum(src, seg, n)
kernel_name = 'mk_perceiver_d4_seqx_r4_f70521'

def setup_inputs(seed: int=0):
    np.random.seed(seed)
    _w = jnp.asarray

    def _rec_inputs():
        import jax
        import jax.numpy as jnp
        _rk = jax.random.key(seed)
        x = 7.22e-05 + 1 * jax.random.normal(jax.random.fold_in(_rk, 1), (2, 256, 256), jnp.float32)
        _lenS = 256 - jax.random.randint(jax.random.fold_in(_rk, 7), (2,), 0, max(1, 256 // 4) + 1, jnp.int32)
        _lenS2 = 4096 - jax.random.randint(jax.random.fold_in(_rk, 8), (2,), 0, max(1, 4096 // 4) + 1, jnp.int32)
        fside_BxSxS_0 = 4.13588e-05 + 0.999923 * jax.random.normal(jax.random.fold_in(_rk, 11), (2, 256, 256), jnp.float32)
        _ctx_1024P = jax.random.normal(jax.random.fold_in(_rk, 12), (2, 16, 256), jnp.float32)
        _ctx_1024c = jax.random.dirichlet(jax.random.fold_in(_rk, 512), 0.3 * jnp.ones((16,), jnp.float32), (2, 4096))
        _ctx_1024t = jnp.einsum('bsk,bkd->bsd', _ctx_1024c, _ctx_1024P)
        _ctx_1024t = _ctx_1024t * jax.lax.rsqrt(jnp.mean(jnp.square(_ctx_1024t)) + 1e-12) * 0.953939
        ctx_1024 = -0.000761806 + 0.999296 * (_ctx_1024t + 0.3 * jax.random.normal(jax.random.fold_in(_rk, 612), (2, 4096, 256), jnp.float32))
        return (x, fside_BxSxS_0, ctx_1024)
    x, fside_BxSxS_0, ctx_1024 = _rec_inputs()

    def _L0_xattn_setup():
        import jax, jax.numpy as jnp
        import numpy as np
        DIM = 256
        HEADS = 16
        HEAD_DIM = DIM // HEADS
        B, N1, N2, SLOTS = (8, 256, 256, 64)
        key = jax.random.key(seed)
        ks = jax.random.split(key, 12)
        s = 1.0 / np.sqrt(DIM)
        return {'x1': jax.random.normal(ks[0], (B, N1, DIM), dtype=jnp.float32), 'x2': jax.random.normal(ks[1], (B, N2, DIM), dtype=jnp.float32), 'memory_k': jax.random.normal(ks[2], (B, SLOTS, DIM), dtype=jnp.float32), 'memory_v': jax.random.normal(ks[3], (B, SLOTS, DIM), dtype=jnp.float32), 'Wq': jax.random.normal(ks[4], (DIM, DIM), dtype=jnp.float32) * s, 'bq': jnp.zeros((DIM,), dtype=jnp.float32), 'Wk': jax.random.normal(ks[5], (DIM, DIM), dtype=jnp.float32) * s, 'bk': jnp.zeros((DIM,), dtype=jnp.float32), 'Wv': jax.random.normal(ks[6], (DIM, DIM), dtype=jnp.float32) * s, 'bv': jnp.zeros((DIM,), dtype=jnp.float32), 'Wp': jax.random.normal(ks[7], (DIM, DIM), dtype=jnp.float32) * s, 'bp': jnp.zeros((DIM,), dtype=jnp.float32)}
    _L0_xattn_all = _L0_xattn_setup()
    _L0_xattn_in = {k: v for k, v in _L0_xattn_all.items() if k in ('Wq', 'bq', 'Wk', 'bk', 'Wv', 'bv', 'Wp', 'bp')}
    del _L0_xattn_all

    def _L0_attn_setup():
        import jax, jax.numpy as jnp
        import numpy as np
        import math
        D_MODEL = 256
        N_HEADS = 16
        HEAD_DIM = D_MODEL // N_HEADS

        def get_slopes(n_heads: int) -> jnp.ndarray:

            def pow2_slopes(n):
                start = 2.0 ** (-8.0 / n)
                return np.array([start * start ** i for i in range(n)], dtype=np.float32)
            if math.log2(n_heads).is_integer():
                return jnp.asarray(pow2_slopes(n_heads))
            closest = 2 ** math.floor(math.log2(n_heads))
            base = pow2_slopes(closest)
            extra = pow2_slopes(2 * closest)[::2][:n_heads - closest]
            return jnp.asarray(np.concatenate([base, extra]))
        key = jax.random.key(seed)
        ks = jax.random.split(key, 9)
        s = 1.0 / math.sqrt(D_MODEL)
        x = jax.random.normal(ks[0], (2, 512, D_MODEL), dtype=jnp.float32)
        q_w = jax.random.uniform(ks[1], (D_MODEL, D_MODEL), jnp.float32, -s, s)
        q_b = jax.random.uniform(ks[2], (D_MODEL,), jnp.float32, -s, s)
        k_w = jax.random.uniform(ks[3], (D_MODEL, D_MODEL), jnp.float32, -s, s)
        k_b = jax.random.uniform(ks[4], (D_MODEL,), jnp.float32, -s, s)
        v_w = jax.random.uniform(ks[5], (D_MODEL, D_MODEL), jnp.float32, -s, s)
        v_b = jax.random.uniform(ks[6], (D_MODEL,), jnp.float32, -s, s)
        o_w = jax.random.uniform(ks[7], (D_MODEL, D_MODEL), jnp.float32, -s, s)
        o_b = jax.random.uniform(ks[8], (D_MODEL,), jnp.float32, -s, s)
        return {'x': x, 'q_w': q_w, 'q_b': q_b, 'k_w': k_w, 'k_b': k_b, 'v_w': v_w, 'v_b': v_b, 'o_w': o_w, 'o_b': o_b}
    _L0_attn_all = _L0_attn_setup()
    _L0_attn_in = {k: v for k, v in _L0_attn_all.items() if k in ('q_w', 'q_b', 'k_w', 'k_b', 'v_w', 'v_b', 'o_w', 'o_b')}
    del _L0_attn_all

    def _L0_ffn_setup():
        import jax, jax.numpy as jnp
        import numpy as np
        HIDDEN = 256
        INTER = 1024
        N_EXPERTS = 8

        def geglu(x, w1, w2, w3):
            return jax.nn.gelu(x @ w1, approximate=False) * (x @ w2) @ w3
        key = jax.random.key(seed)
        ks = jax.random.split(key, 8)
        s = 0.02
        x = jax.random.normal(ks[0], (2, 512, HIDDEN), dtype=jnp.float32)
        w1s = jax.random.normal(ks[1], (HIDDEN, INTER), dtype=jnp.float32) * s
        w2s = jax.random.normal(ks[2], (HIDDEN, INTER), dtype=jnp.float32) * s
        w3s = jax.random.normal(ks[3], (INTER, HIDDEN), dtype=jnp.float32) * s
        W1 = jax.random.normal(ks[4], (N_EXPERTS, HIDDEN, INTER), dtype=jnp.float32) * s
        W2 = jax.random.normal(ks[5], (N_EXPERTS, HIDDEN, INTER), dtype=jnp.float32) * s
        W3 = jax.random.normal(ks[6], (N_EXPERTS, INTER, HIDDEN), dtype=jnp.float32) * s
        Wg = jax.random.normal(ks[7], (HIDDEN, N_EXPERTS), dtype=jnp.float32) * s
        return {'x': x, 'w1s': w1s, 'w2s': w2s, 'w3s': w3s, 'W1': W1, 'W2': W2, 'W3': W3, 'Wg': Wg}
    _L0_ffn_all = _L0_ffn_setup()
    _L0_ffn_in = {k: v for k, v in _L0_ffn_all.items() if k in ('w1s', 'w2s', 'w3s', 'W1', 'W2', 'W3', 'Wg')}
    del _L0_ffn_all

    def _L1_xattn_setup():
        import jax, jax.numpy as jnp
        import numpy as np
        from math import sqrt
        D_MODEL = 256
        N_HEAD = 16
        D_HEAD = D_MODEL // N_HEAD

        def _split_heads(x):
            B, L, D = x.shape
            return x.reshape(B, L, N_HEAD, D_HEAD).transpose(0, 2, 1, 3)
        key = jax.random.key(seed)
        ks = jax.random.split(key, 11)
        B, L = (4, 512)
        s = 1.0 / sqrt(D_MODEL)
        inp = {'q': jax.random.normal(ks[0], (B, L, D_MODEL), jnp.float32), 'k': jax.random.normal(ks[1], (B, L, D_MODEL), jnp.float32), 'v': jax.random.normal(ks[2], (B, L, D_MODEL), jnp.float32), 'w_q': jax.random.normal(ks[3], (D_MODEL, D_MODEL), jnp.float32) * s, 'b_q': jax.random.normal(ks[4], (D_MODEL,), jnp.float32) * s, 'w_k': jax.random.normal(ks[5], (D_MODEL, D_MODEL), jnp.float32) * s, 'b_k': jax.random.normal(ks[6], (D_MODEL,), jnp.float32) * s, 'w_v': jax.random.normal(ks[7], (D_MODEL, D_MODEL), jnp.float32) * s, 'b_v': jax.random.normal(ks[8], (D_MODEL,), jnp.float32) * s, 'w_o': jax.random.normal(ks[9], (D_MODEL, D_MODEL), jnp.float32) * s, 'b_o': jax.random.normal(ks[10], (D_MODEL,), jnp.float32) * s}
        return inp
    _L1_xattn_all = _L1_xattn_setup()
    _L1_xattn_in = {k: v for k, v in _L1_xattn_all.items() if k in ('w_q', 'b_q', 'w_k', 'b_k', 'w_v', 'b_v', 'w_o', 'b_o')}
    del _L1_xattn_all

    def _L1_attn_setup():
        import math
        import jax, jax.numpy as jnp
        import numpy as np

        def _expmap0(u):
            u0 = u[..., :1]
            us = u[..., 1:]
            mink = -u0 * u0 + jnp.sum(us * us, axis=-1, keepdims=True)
            nomin = jnp.sqrt(jnp.maximum(mink, 1e-08))
            r = jnp.sinh(nomin) * u / nomin
            space = r[..., 1:]
            time = jnp.sqrt(1.0 + jnp.sum(space * space, axis=-1, keepdims=True))
            return jnp.concatenate([time, space], axis=-1)
        key = jax.random.key(seed)
        B, T, E, H = (2, 256, 256, 16)
        ks = jax.random.split(key, 8)
        s = 0.02
        return {'x': jax.random.normal(ks[0], (B, T, E), jnp.float32), 'Wqkv': jax.random.normal(ks[1], (3 * E, E), jnp.float32) * s, 'bqkv': jnp.zeros((3 * E,), jnp.float32), 'Wout': jax.random.normal(ks[2], (E, E), jnp.float32) * s, 'bout': jnp.zeros((E,), jnp.float32), 'Wimp': jax.random.normal(ks[3], (1, E), jnp.float32) * s, 'bimp': jnp.zeros((1,), jnp.float32), 'Walpha': jax.random.normal(ks[4], (H, E), jnp.float32) * s, 'balpha': jnp.zeros((H,), jnp.float32), 'spike_threshold': jnp.asarray(0.5, jnp.float32), 'log_k': jnp.full((H,), 0.54, jnp.float32), 'qk_scale': jnp.asarray(0.1, jnp.float32)}
    _L1_attn_all = _L1_attn_setup()
    _L1_attn_in = {k: v for k, v in _L1_attn_all.items() if k in ('Wqkv', 'bqkv', 'Wout', 'bout', 'Wimp', 'bimp', 'Walpha', 'balpha', 'spike_threshold', 'log_k', 'qk_scale')}
    del _L1_attn_all

    def _L1_ffn_setup():
        import jax, jax.numpy as jnp
        import numpy as np
        DIM = 256

        def _reference_tuple_inner(x, W_r, W_k, W_v, mu_r, mu_k):
            B, T, C = x.shape
            x_prev = jnp.concatenate([jnp.zeros((B, 1, C), x.dtype), x[:, :-1, :]], axis=1)
            xr = mu_r * x + (1.0 - mu_r) * x_prev
            xk = mu_k * x + (1.0 - mu_k) * x_prev
            r = jax.nn.sigmoid(jnp.einsum('btc,dc->btd', xr, W_r))
            k = jnp.einsum('btc,dc->btd', xk, W_k)
            k_act = jnp.square(jax.nn.relu(k))
            out = r * jnp.einsum('btc,dc->btd', k_act, W_v)
            new_state = x[:, -1, :]
            return (out, new_state)
        key = jax.random.key(seed)
        ks = jax.random.split(key, 6)
        B, T, C = (8, 512, DIM)
        x = jax.random.normal(ks[0], (B, T, C), dtype=jnp.float32)
        s = 1.0 / np.sqrt(C)
        W_r = jax.random.uniform(ks[1], (C, C), jnp.float32, -s, s)
        W_k = jax.random.uniform(ks[2], (C, C), jnp.float32, -s, s)
        W_v = jax.random.uniform(ks[3], (C, C), jnp.float32, -s, s)
        mu_r = jax.random.uniform(ks[4], (C,), jnp.float32)
        mu_k = jax.random.uniform(ks[5], (C,), jnp.float32)
        return {'x': x, 'W_r': W_r, 'W_k': W_k, 'W_v': W_v, 'mu_r': mu_r, 'mu_k': mu_k}
    _L1_ffn_all = _L1_ffn_setup()
    _L1_ffn_in = {k: v for k, v in _L1_ffn_all.items() if k in ('W_r', 'W_k', 'W_v', 'mu_r', 'mu_k')}
    del _L1_ffn_all

    def _L2_xattn_setup():
        import jax, jax.numpy as jnp
        import numpy as np
        N_EMBD = 256
        N_HEAD = 16
        R = 16
        SCALING = 1.0 / 16.0

        def lora_linear(x, W, b, A, B):
            return x @ W.T + b + x @ A.T @ B.T * SCALING
        key = jax.random.key(seed)
        ks = jax.random.split(key, 16)
        B, T, S, C = (8, 256, 64, N_EMBD)
        std = 0.02
        return {'x': jax.random.normal(ks[0], (B, T, C), jnp.float32), 'feature': jax.random.normal(ks[1], (B, S, C), jnp.float32), 'Wq': jax.random.normal(ks[2], (C, C), jnp.float32) * std, 'bq': jnp.zeros((C,), jnp.float32), 'Aq': jax.random.normal(ks[3], (R, C), jnp.float32) * std, 'Bq': jnp.zeros((C, R), jnp.float32), 'Wf': jax.random.normal(ks[4], (2 * C, C), jnp.float32) * std, 'bf': jnp.zeros((2 * C,), jnp.float32), 'Af': jax.random.normal(ks[5], (R, C), jnp.float32) * std, 'Bf': jnp.zeros((2 * C, R), jnp.float32), 'Wp': jax.random.normal(ks[6], (C, C), jnp.float32) * std, 'bp': jnp.zeros((C,), jnp.float32), 'Ap': jax.random.normal(ks[7], (R, C), jnp.float32) * std, 'Bp': jnp.zeros((C, R), jnp.float32)}
    _L2_xattn_all = _L2_xattn_setup()
    _L2_xattn_in = {k: v for k, v in _L2_xattn_all.items() if k in ('Wq', 'bq', 'Aq', 'Bq', 'Wf', 'bf', 'Af', 'Bf', 'Wp', 'bp', 'Ap', 'Bp')}
    del _L2_xattn_all

    def _L2_attn_setup():
        import jax, jax.numpy as jnp
        import numpy as np
        D_MODEL, D_STATE, D_CONV, EXPAND = (256, 16, 4, 2)
        D_INNER = D_MODEL * EXPAND
        key = jax.random.key(seed)
        ks = jax.random.split(key, 8)
        B, L = (4, 512)
        x = jax.random.normal(ks[0], (B, L, D_MODEL), dtype=jnp.float32)
        s = 0.02
        W_in = jax.random.normal(ks[1], (D_MODEL, 2 * D_INNER), dtype=jnp.float32) * s
        conv_w = jax.random.normal(ks[2], (D_INNER, 1, D_CONV), dtype=jnp.float32) * 0.2
        conv_b = jnp.zeros((D_INNER,), dtype=jnp.float32)
        W_x = jax.random.normal(ks[3], (D_INNER, 2 * D_STATE + 1), dtype=jnp.float32) * s
        W_dt = jax.random.normal(ks[4], (D_INNER, 1), dtype=jnp.float32) * 0.5
        b_dt = jax.random.normal(ks[5], (D_INNER,), dtype=jnp.float32) * 0.1
        A_log = jnp.log(jnp.arange(1, D_STATE + 1, dtype=jnp.float32))
        D = jnp.ones((D_INNER,), dtype=jnp.float32)
        W_out = jax.random.normal(ks[6], (D_INNER, D_MODEL), dtype=jnp.float32) * s
        return {'x': x, 'W_in': W_in, 'conv_w': conv_w, 'conv_b': conv_b, 'W_x': W_x, 'W_dt': W_dt, 'b_dt': b_dt, 'A_log': A_log, 'D': D, 'W_out': W_out}
    _L2_attn_all = _L2_attn_setup()
    _L2_attn_in = {k: v for k, v in _L2_attn_all.items() if k in ('W_in', 'conv_w', 'conv_b', 'W_x', 'W_dt', 'b_dt', 'A_log', 'D', 'W_out')}
    del _L2_attn_all

    def _L2_ffn_setup():
        import jax, jax.numpy as jnp
        import numpy as np
        B, L, H, E, FF, C = (4, 512, 256, 8, 1024, 2)
        key = jax.random.key(seed)
        ks = jax.random.split(key, 6)
        s = 0.02
        return {'x': jax.random.normal(ks[0], (B, L, H), dtype=jnp.float32), 'Wg': jax.random.normal(ks[1], (H, E), dtype=jnp.float32) * s, 'W1': jax.random.normal(ks[2], (E, H, FF), dtype=jnp.float32) * s, 'b1': jnp.zeros((E, FF), dtype=jnp.float32), 'W2': jax.random.normal(ks[3], (E, FF, H), dtype=jnp.float32) * s, 'b2': jnp.zeros((E, H), dtype=jnp.float32)}
    _L2_ffn_all = _L2_ffn_setup()
    _L2_ffn_in = {k: v for k, v in _L2_ffn_all.items() if k in ('Wg', 'W1', 'b1', 'W2', 'b2')}
    del _L2_ffn_all

    def _L3_xattn_setup():
        import jax, jax.numpy as jnp
        import numpy as np
        EPS = 1e-06

        def _rmsnorm(x, w, eps=EPS):
            x32 = x.astype(jnp.float32)
            var = jnp.mean(x32 * x32, axis=-1, keepdims=True)
            return (x32 * jax.lax.rsqrt(var + eps)).astype(x.dtype) * w
        key = jax.random.key(seed)
        ks = jax.random.split(key, 6)
        B, S, K, H = (4, 512, 64, 256)
        return {'hidden_states': jax.random.normal(ks[0], (B, S, H), jnp.float32), 'memory_state': jax.random.normal(ks[1], (B, K, H), jnp.float32), 'q_w': jax.random.normal(ks[2], (H, H), jnp.float32) * (1.0 / np.sqrt(H)), 'k_w': jax.random.normal(ks[3], (H, H), jnp.float32) * (1.0 / np.sqrt(H)), 'norm_w': jnp.ones((H,), jnp.float32), 'gate_w': jax.random.normal(ks[4], (H, H), jnp.float32) * 0.02, 'gate_b': jnp.zeros((H,), jnp.float32)}
    _L3_xattn_all = _L3_xattn_setup()
    _L3_xattn_in = {k: v for k, v in _L3_xattn_all.items() if k in ('q_w', 'k_w', 'norm_w', 'gate_w', 'gate_b')}
    del _L3_xattn_all

    def _L3_attn_setup():
        import jax, jax.numpy as jnp
        import numpy as np
        NUM_HEADS = 16
        key = jax.random.key(seed)
        ks = jax.random.split(key, 5)
        B, N, C = (2, 512, 256)
        x = jax.random.normal(ks[0], (B, N, C), dtype=jnp.float32)
        s_in = 1.0 / np.sqrt(C)
        Wq = jax.random.normal(ks[1], (C, 2 * C), dtype=jnp.float32) * s_in
        Wk = jax.random.normal(ks[2], (C, 2 * C), dtype=jnp.float32) * s_in
        Wv = jax.random.normal(ks[3], (C, 2 * C), dtype=jnp.float32) * s_in
        Wo = jax.random.normal(ks[4], (2 * C, C), dtype=jnp.float32) * (1.0 / np.sqrt(2 * C))
        return {'x': x, 'Wq': Wq, 'Wk': Wk, 'Wv': Wv, 'Wo': Wo}
    _L3_attn_all = _L3_attn_setup()
    _L3_attn_in = {k: v for k, v in _L3_attn_all.items() if k in ('Wq', 'Wk', 'Wv', 'Wo')}
    del _L3_attn_all

    def _L3_ffn_setup():
        import jax, jax.numpy as jnp
        import numpy as np
        D = 256
        H = 16
        DH = D // H
        DC = D // 4
        HID = 512
        G = 2
        EPG = 4
        E = G * EPG
        TOPK = 2
        EPS = 1e-06
        B, T = (2, 512)

        def _rope_sincos(t, dh):
            inv_freq = 1.0 / 10000.0 ** (jnp.arange(0, dh, 2, dtype=jnp.float32) / dh)
            ang = jnp.arange(t, dtype=jnp.float32)[:, None] * inv_freq[None, :]
            return (jnp.sin(ang), jnp.cos(ang))

        def _apply_rope(x, sin, cos):
            x1 = x[..., ::2]
            x2 = x[..., 1::2]
            r = jnp.stack([x1 * cos - x2 * sin, x1 * sin + x2 * cos], axis=-1)
            return r.reshape(x.shape)

        def _swiglu(x):
            a, b = jnp.split(x, 2, axis=-1)
            return jax.nn.silu(a) * b

        def _rmsnorm(x, w):
            return x * jax.lax.rsqrt(jnp.mean(x * x, axis=-1, keepdims=True) + EPS) * w
        key = jax.random.key(seed)
        ks = jax.random.split(key, 14)
        s = 0.02
        return {'src': jax.random.normal(ks[0], (B, T, D), jnp.float32), 'Wq': jax.random.normal(ks[1], (D, D), jnp.float32) * s, 'Wk_c': jax.random.normal(ks[2], (D, DC), jnp.float32) * s, 'Wv_c': jax.random.normal(ks[3], (D, DC), jnp.float32) * s, 'Wk': jax.random.normal(ks[4], (DC, D), jnp.float32) * s, 'Wv': jax.random.normal(ks[5], (DC, D), jnp.float32) * s, 'Wo': jax.random.normal(ks[6], (D, D), jnp.float32) * s, 'W_shared_in': jax.random.normal(ks[7], (D, 2 * HID), jnp.float32) * s, 'W_shared_out': jax.random.normal(ks[8], (HID, D), jnp.float32) * s, 'W1_shared': jax.random.normal(ks[9], (D, 2 * HID), jnp.float32) * s, 'W2_experts': jax.random.normal(ks[10], (E, HID, D), jnp.float32) * s, 'Wg_gate': jax.random.normal(ks[11], (D, G), jnp.float32) * s, 'We_gate': jax.random.normal(ks[12], (D, E), jnp.float32) * s, 'group_bias': jnp.zeros((G,), jnp.float32), 'expert_bias': jnp.zeros((E,), jnp.float32), 'norm1_w': jnp.ones((D,), jnp.float32), 'norm2_w': jnp.ones((D,), jnp.float32)}
    _L3_ffn_all = _L3_ffn_setup()
    _L3_ffn_in = {k: v for k, v in _L3_ffn_all.items() if k in ('Wq', 'Wk_c', 'Wv_c', 'Wk', 'Wv', 'Wo', 'W_shared_in', 'W_shared_out', 'W1_shared', 'W2_experts', 'Wg_gate', 'We_gate', 'group_bias', 'expert_bias', 'norm1_w', 'norm2_w')}
    del _L3_ffn_all
    return {'x': x, 'fside_BxSxS_0': fside_BxSxS_0, 'ctx_1024': ctx_1024, 'L0_xattn_Wq': _L0_xattn_in['Wq'], 'L0_xattn_bq': _L0_xattn_in['bq'], 'L0_xattn_Wk': _L0_xattn_in['Wk'], 'L0_xattn_bk': _L0_xattn_in['bk'], 'L0_xattn_Wv': _L0_xattn_in['Wv'], 'L0_xattn_bv': _L0_xattn_in['bv'], 'L0_xattn_Wp': _L0_xattn_in['Wp'], 'L0_xattn_bp': _L0_xattn_in['bp'], 'L0_attn_q_w': _L0_attn_in['q_w'], 'L0_attn_q_b': _L0_attn_in['q_b'], 'L0_attn_k_w': _L0_attn_in['k_w'], 'L0_attn_k_b': _L0_attn_in['k_b'], 'L0_attn_v_w': _L0_attn_in['v_w'], 'L0_attn_v_b': _L0_attn_in['v_b'], 'L0_attn_o_w': _L0_attn_in['o_w'], 'L0_attn_o_b': _L0_attn_in['o_b'], 'L0_ffn_w1s': _L0_ffn_in['w1s'], 'L0_ffn_w2s': _L0_ffn_in['w2s'], 'L0_ffn_w3s': _L0_ffn_in['w3s'], 'L0_ffn_W1': _L0_ffn_in['W1'], 'L0_ffn_W2': _L0_ffn_in['W2'], 'L0_ffn_W3': _L0_ffn_in['W3'], 'L0_ffn_Wg': _L0_ffn_in['Wg'], 'L1_xattn_w_q': _L1_xattn_in['w_q'], 'L1_xattn_b_q': _L1_xattn_in['b_q'], 'L1_xattn_w_k': _L1_xattn_in['w_k'], 'L1_xattn_b_k': _L1_xattn_in['b_k'], 'L1_xattn_w_v': _L1_xattn_in['w_v'], 'L1_xattn_b_v': _L1_xattn_in['b_v'], 'L1_xattn_w_o': _L1_xattn_in['w_o'], 'L1_xattn_b_o': _L1_xattn_in['b_o'], 'L1_attn_Wqkv': _L1_attn_in['Wqkv'], 'L1_attn_bqkv': _L1_attn_in['bqkv'], 'L1_attn_Wout': _L1_attn_in['Wout'], 'L1_attn_bout': _L1_attn_in['bout'], 'L1_attn_Wimp': _L1_attn_in['Wimp'], 'L1_attn_bimp': _L1_attn_in['bimp'], 'L1_attn_Walpha': _L1_attn_in['Walpha'], 'L1_attn_balpha': _L1_attn_in['balpha'], 'L1_attn_spike_threshold': _L1_attn_in['spike_threshold'], 'L1_attn_log_k': _L1_attn_in['log_k'], 'L1_attn_qk_scale': _L1_attn_in['qk_scale'], 'L1_ffn_W_r': _L1_ffn_in['W_r'], 'L1_ffn_W_k': _L1_ffn_in['W_k'], 'L1_ffn_W_v': _L1_ffn_in['W_v'], 'L1_ffn_mu_r': _L1_ffn_in['mu_r'], 'L1_ffn_mu_k': _L1_ffn_in['mu_k'], 'L2_xattn_Wq': _L2_xattn_in['Wq'], 'L2_xattn_bq': _L2_xattn_in['bq'], 'L2_xattn_Aq': _L2_xattn_in['Aq'], 'L2_xattn_Bq': _L2_xattn_in['Bq'], 'L2_xattn_Wf': _L2_xattn_in['Wf'], 'L2_xattn_bf': _L2_xattn_in['bf'], 'L2_xattn_Af': _L2_xattn_in['Af'], 'L2_xattn_Bf': _L2_xattn_in['Bf'], 'L2_xattn_Wp': _L2_xattn_in['Wp'], 'L2_xattn_bp': _L2_xattn_in['bp'], 'L2_xattn_Ap': _L2_xattn_in['Ap'], 'L2_xattn_Bp': _L2_xattn_in['Bp'], 'L2_attn_W_in': _L2_attn_in['W_in'], 'L2_attn_conv_w': _L2_attn_in['conv_w'], 'L2_attn_conv_b': _L2_attn_in['conv_b'], 'L2_attn_W_x': _L2_attn_in['W_x'], 'L2_attn_W_dt': _L2_attn_in['W_dt'], 'L2_attn_b_dt': _L2_attn_in['b_dt'], 'L2_attn_A_log': _L2_attn_in['A_log'], 'L2_attn_D': _L2_attn_in['D'], 'L2_attn_W_out': _L2_attn_in['W_out'], 'L2_ffn_Wg': _L2_ffn_in['Wg'], 'L2_ffn_W1': _L2_ffn_in['W1'], 'L2_ffn_b1': _L2_ffn_in['b1'], 'L2_ffn_W2': _L2_ffn_in['W2'], 'L2_ffn_b2': _L2_ffn_in['b2'], 'L3_xattn_q_w': _L3_xattn_in['q_w'], 'L3_xattn_k_w': _L3_xattn_in['k_w'], 'L3_xattn_norm_w': _L3_xattn_in['norm_w'], 'L3_xattn_gate_w': _L3_xattn_in['gate_w'], 'L3_xattn_gate_b': _L3_xattn_in['gate_b'], 'L3_attn_Wq': _L3_attn_in['Wq'], 'L3_attn_Wk': _L3_attn_in['Wk'], 'L3_attn_Wv': _L3_attn_in['Wv'], 'L3_attn_Wo': _L3_attn_in['Wo'], 'L3_ffn_Wq': _L3_ffn_in['Wq'], 'L3_ffn_Wk_c': _L3_ffn_in['Wk_c'], 'L3_ffn_Wv_c': _L3_ffn_in['Wv_c'], 'L3_ffn_Wk': _L3_ffn_in['Wk'], 'L3_ffn_Wv': _L3_ffn_in['Wv'], 'L3_ffn_Wo': _L3_ffn_in['Wo'], 'L3_ffn_W_shared_in': _L3_ffn_in['W_shared_in'], 'L3_ffn_W_shared_out': _L3_ffn_in['W_shared_out'], 'L3_ffn_W1_shared': _L3_ffn_in['W1_shared'], 'L3_ffn_W2_experts': _L3_ffn_in['W2_experts'], 'L3_ffn_Wg_gate': _L3_ffn_in['Wg_gate'], 'L3_ffn_We_gate': _L3_ffn_in['We_gate'], 'L3_ffn_group_bias': _L3_ffn_in['group_bias'], 'L3_ffn_expert_bias': _L3_ffn_in['expert_bias'], 'L3_ffn_norm1_w': _L3_ffn_in['norm1_w'], 'L3_ffn_norm2_w': _L3_ffn_in['norm2_w']}

def reference(x, fside_BxSxS_0, ctx_1024, L0_xattn_Wq, L0_xattn_bq, L0_xattn_Wk, L0_xattn_bk, L0_xattn_Wv, L0_xattn_bv, L0_xattn_Wp, L0_xattn_bp, L0_attn_q_w, L0_attn_q_b, L0_attn_k_w, L0_attn_k_b, L0_attn_v_w, L0_attn_v_b, L0_attn_o_w, L0_attn_o_b, L0_ffn_w1s, L0_ffn_w2s, L0_ffn_w3s, L0_ffn_W1, L0_ffn_W2, L0_ffn_W3, L0_ffn_Wg, L1_xattn_w_q, L1_xattn_b_q, L1_xattn_w_k, L1_xattn_b_k, L1_xattn_w_v, L1_xattn_b_v, L1_xattn_w_o, L1_xattn_b_o, L1_attn_Wqkv, L1_attn_bqkv, L1_attn_Wout, L1_attn_bout, L1_attn_Wimp, L1_attn_bimp, L1_attn_Walpha, L1_attn_balpha, L1_attn_spike_threshold, L1_attn_log_k, L1_attn_qk_scale, L1_ffn_W_r, L1_ffn_W_k, L1_ffn_W_v, L1_ffn_mu_r, L1_ffn_mu_k, L2_xattn_Wq, L2_xattn_bq, L2_xattn_Aq, L2_xattn_Bq, L2_xattn_Wf, L2_xattn_bf, L2_xattn_Af, L2_xattn_Bf, L2_xattn_Wp, L2_xattn_bp, L2_xattn_Ap, L2_xattn_Bp, L2_attn_W_in, L2_attn_conv_w, L2_attn_conv_b, L2_attn_W_x, L2_attn_W_dt, L2_attn_b_dt, L2_attn_A_log, L2_attn_D, L2_attn_W_out, L2_ffn_Wg, L2_ffn_W1, L2_ffn_b1, L2_ffn_W2, L2_ffn_b2, L3_xattn_q_w, L3_xattn_k_w, L3_xattn_norm_w, L3_xattn_gate_w, L3_xattn_gate_b, L3_attn_Wq, L3_attn_Wk, L3_attn_Wv, L3_attn_Wo, L3_ffn_Wq, L3_ffn_Wk_c, L3_ffn_Wv_c, L3_ffn_Wk, L3_ffn_Wv, L3_ffn_Wo, L3_ffn_W_shared_in, L3_ffn_W_shared_out, L3_ffn_W1_shared, L3_ffn_W2_experts, L3_ffn_Wg_gate, L3_ffn_We_gate, L3_ffn_group_bias, L3_ffn_expert_bias, L3_ffn_norm1_w, L3_ffn_norm2_w):
    import jax
    import jax.numpy as jnp

    def _L0_xattn_ref(x1, x2, memory_k, memory_v, Wq, bq, Wk, bk, Wv, bv, Wp, bp):
        import jax, jax.numpy as jnp
        import numpy as np
        DIM = 256
        HEADS = 16
        HEAD_DIM = DIM // HEADS
        B, N1, N2, SLOTS = (8, 256, 256, 64)
        Bn, Nq, C = x1.shape
        H, D = (HEADS, HEAD_DIM)
        scale = D ** (-0.5)
        q = (x1 @ Wq + bq).reshape(Bn, Nq, H, D).transpose(0, 2, 1, 3)
        k = x2 @ Wk + bk
        v = x2 @ Wv + bv
        k = jnp.concatenate([k, memory_k], axis=1)
        v = jnp.concatenate([v, memory_v], axis=1)
        Nkv = k.shape[1]
        k = k.reshape(Bn, Nkv, H, D).transpose(0, 2, 1, 3)
        v = v.reshape(Bn, Nkv, H, D).transpose(0, 2, 1, 3)
        attn = jnp.einsum('bhqd,bhkd->bhqk', q, k) * scale
        attn = jax.nn.softmax(attn, axis=-1)
        out = jnp.einsum('bhqk,bhkd->bhqd', attn, v)
        out = out.transpose(0, 2, 1, 3).reshape(Bn, Nq, C)
        return out @ Wp + bp

    def _L0_attn_ref(x, q_w, q_b, k_w, k_b, v_w, v_b, o_w, o_b):
        import jax, jax.numpy as jnp
        import numpy as np
        import math
        D_MODEL = 256
        N_HEADS = 16
        HEAD_DIM = D_MODEL // N_HEADS

        def get_slopes(n_heads: int) -> jnp.ndarray:

            def pow2_slopes(n):
                start = 2.0 ** (-8.0 / n)
                return np.array([start * start ** i for i in range(n)], dtype=np.float32)
            if math.log2(n_heads).is_integer():
                return jnp.asarray(pow2_slopes(n_heads))
            closest = 2 ** math.floor(math.log2(n_heads))
            base = pow2_slopes(closest)
            extra = pow2_slopes(2 * closest)[::2][:n_heads - closest]
            return jnp.asarray(np.concatenate([base, extra]))
        B, S, D = x.shape
        H, hd = (N_HEADS, HEAD_DIM)
        Q = (x @ q_w.T + q_b).reshape(B, S, H, hd).transpose(0, 2, 1, 3)
        K = (x @ k_w.T + k_b).reshape(B, S, H, hd).transpose(0, 2, 1, 3)
        V = (x @ v_w.T + v_b).reshape(B, S, H, hd).transpose(0, 2, 1, 3)
        scores = jnp.einsum('bhqd,bhkd->bhqk', Q, K) / math.sqrt(hd)
        pos = jnp.arange(S)
        rel = (pos[None, :] - pos[:, None]).astype(scores.dtype)
        slopes = get_slopes(H)
        scores = scores + slopes[None, :, None, None] * rel[None, None, :, :]
        causal = pos[None, :] <= pos[:, None]
        scores = jnp.where(causal[None, None], scores, -jnp.inf)
        attn = jax.nn.softmax(scores, axis=-1)
        out = jnp.einsum('bhqk,bhkd->bhqd', attn, V)
        out = out.transpose(0, 2, 1, 3).reshape(B, S, D)
        return out @ o_w.T + o_b

    def _L0_ffn_ref(x, w1s, w2s, w3s, W1, W2, W3, Wg):
        import jax, jax.numpy as jnp
        import numpy as np
        HIDDEN = 256
        INTER = 1024
        N_EXPERTS = 8

        def geglu(x, w1, w2, w3):
            return jax.nn.gelu(x @ w1, approximate=False) * (x @ w2) @ w3
        B, T, C = x.shape
        xf = x.reshape(-1, C)
        shared = geglu(xf, w1s, w2s, w3s)
        logits = xf @ Wg
        idx = jnp.argmax(logits, axis=-1)
        final = jnp.zeros_like(xf)
        for e in range(N_EXPERTS):
            y = geglu(xf, W1[e], W2[e], W3[e])
            final = final + jnp.where((idx == e)[:, None], y, 0.0)
        return (shared + final).reshape(B, T, C)

    def _L1_xattn_ref(q, k, v, w_q, b_q, w_k, b_k, w_v, b_v, w_o, b_o):
        import jax, jax.numpy as jnp
        import numpy as np
        from math import sqrt
        D_MODEL = 256
        N_HEAD = 16
        D_HEAD = D_MODEL // N_HEAD

        def _split_heads(x):
            B, L, D = x.shape
            return x.reshape(B, L, N_HEAD, D_HEAD).transpose(0, 2, 1, 3)
        qh = _split_heads(q @ w_q.T + b_q)
        kh = _split_heads(k @ w_k.T + b_k)
        vh = _split_heads(v @ w_v.T + b_v)
        scale = 1.0 / sqrt(D_HEAD)
        score = jnp.einsum('bhqd,bhkd->bhqk', qh, kh) * scale
        attn = jax.nn.softmax(score, axis=-1)
        out = jnp.einsum('bhqk,bhkd->bhqd', attn, vh)
        B, H, L, Dh = out.shape
        out = out.transpose(0, 2, 1, 3).reshape(B, L, D_MODEL)
        return out @ w_o.T + b_o

    def _L1_attn_ref(x, Wqkv, bqkv, Wout, bout, Wimp, bimp, Walpha, balpha, spike_threshold, log_k, qk_scale):
        import math
        import jax, jax.numpy as jnp
        import numpy as np

        def _expmap0(u):
            u0 = u[..., :1]
            us = u[..., 1:]
            mink = -u0 * u0 + jnp.sum(us * us, axis=-1, keepdims=True)
            nomin = jnp.sqrt(jnp.maximum(mink, 1e-08))
            r = jnp.sinh(nomin) * u / nomin
            space = r[..., 1:]
            time = jnp.sqrt(1.0 + jnp.sum(space * space, axis=-1, keepdims=True))
            return jnp.concatenate([time, space], axis=-1)
        B, T, C = x.shape
        H = log_k.shape[0]
        D = C // H
        importance = jax.nn.sigmoid(x @ Wimp.T + bimp)
        spikes = (importance > spike_threshold).astype(x.dtype)
        spike_mask = spikes.reshape(B, 1, T, 1)
        alpha = jax.nn.sigmoid(x @ Walpha.T + balpha)
        alpha = jnp.transpose(alpha, (0, 2, 1))[..., None]
        qkv = (x @ Wqkv.T + bqkv).reshape(B, T, 3, H, D)
        q = jnp.transpose(qkv[:, :, 0], (0, 2, 1, 3))
        k = jnp.transpose(qkv[:, :, 1], (0, 2, 1, 3))
        v = jnp.transpose(qkv[:, :, 2], (0, 2, 1, 3))
        scores_euclid = jnp.einsum('bhtd,bhsd->bhts', q, k) / math.sqrt(D)
        safe_scale = jax.nn.sigmoid(qk_scale) * 1.5
        qn = q / jnp.maximum(jnp.linalg.norm(q, axis=-1, keepdims=True), 1e-12) * safe_scale
        kn = k / jnp.maximum(jnp.linalg.norm(k, axis=-1, keepdims=True), 1e-12) * safe_scale
        q_hyp = _expmap0(qn)
        k_hyp = _expmap0(kn)
        inner = -jnp.einsum('bhti,bhsi->bhts', q_hyp[..., :1], k_hyp[..., :1]) + jnp.einsum('bhtd,bhsd->bhts', q_hyp[..., 1:], k_hyp[..., 1:])
        curv_k = (jax.nn.softplus(log_k) + 1e-06).reshape(1, H, 1, 1)
        mdot = jnp.maximum(-inner, 1.0 + 1e-06)
        dist = jnp.arccosh(mdot)
        scores_hyper = -(dist * dist) / curv_k
        scores = (1.0 - alpha) * scores_euclid + alpha * scores_hyper
        causal = jnp.tril(jnp.ones((T, T), bool))
        scores = jnp.where(causal[None, None], scores, -jnp.inf)
        attn = jax.nn.softmax(scores, axis=-1) * spike_mask
        y = jnp.einsum('bhts,bhsd->bhtd', attn, v)
        y = jnp.transpose(y, (0, 2, 1, 3)).reshape(B, T, C)
        return y @ Wout.T + bout

    def _L1_ffn_ref(x, W_r, W_k, W_v, mu_r, mu_k):
        import jax, jax.numpy as jnp
        import numpy as np
        DIM = 256

        def _reference_tuple_inner(x, W_r, W_k, W_v, mu_r, mu_k):
            B, T, C = x.shape
            x_prev = jnp.concatenate([jnp.zeros((B, 1, C), x.dtype), x[:, :-1, :]], axis=1)
            xr = mu_r * x + (1.0 - mu_r) * x_prev
            xk = mu_k * x + (1.0 - mu_k) * x_prev
            r = jax.nn.sigmoid(jnp.einsum('btc,dc->btd', xr, W_r))
            k = jnp.einsum('btc,dc->btd', xk, W_k)
            k_act = jnp.square(jax.nn.relu(k))
            out = r * jnp.einsum('btc,dc->btd', k_act, W_v)
            new_state = x[:, -1, :]
            return (out, new_state)
        return _reference_tuple_inner(x, W_r, W_k, W_v, mu_r, mu_k)[0]

    def _L2_xattn_ref(x, feature, Wq, bq, Aq, Bq, Wf, bf, Af, Bf, Wp, bp, Ap, Bp):
        import jax, jax.numpy as jnp
        import numpy as np
        N_EMBD = 256
        N_HEAD = 16
        R = 16
        SCALING = 1.0 / 16.0

        def lora_linear(x, W, b, A, B):
            return x @ W.T + b + x @ A.T @ B.T * SCALING
        Bsz, T, C = x.shape
        S = feature.shape[1]
        H = N_HEAD
        D = C // H
        q = lora_linear(x, Wq, bq, Aq, Bq).reshape(Bsz, T, H, D).transpose(0, 2, 1, 3)
        kv = lora_linear(feature, Wf, bf, Af, Bf)
        k, v = (kv[..., :C], kv[..., C:])
        k = k.reshape(Bsz, S, H, D).transpose(0, 2, 1, 3)
        v = v.reshape(Bsz, S, H, D).transpose(0, 2, 1, 3)
        att = jnp.einsum('bhtd,bhsd->bhts', q, k) * (1.0 / np.sqrt(D))
        mask = jnp.tril(jnp.ones((T, S), bool))
        att = jnp.where(mask, att, -jnp.inf)
        att = jax.nn.softmax(att, axis=-1)
        y = jnp.einsum('bhts,bhsd->bhtd', att, v)
        y = y.transpose(0, 2, 1, 3).reshape(Bsz, T, C)
        return lora_linear(y, Wp, bp, Ap, Bp)

    def _L2_attn_ref(x, W_in, conv_w, conv_b, W_x, W_dt, b_dt, A_log, D, W_out):
        import jax, jax.numpy as jnp
        import numpy as np
        D_MODEL, D_STATE, D_CONV, EXPAND = (256, 16, 4, 2)
        D_INNER = D_MODEL * EXPAND
        Bsz, L, _ = x.shape
        d_state = A_log.shape[0]
        xz = x @ W_in
        xi, z = jnp.split(xz, 2, axis=-1)
        xc = jnp.swapaxes(xi, 1, 2)
        k = conv_w.shape[-1]
        xc = jax.lax.conv_general_dilated(xc, conv_w, window_strides=(1,), padding=[(k - 1, 0)], dimension_numbers=('NCH', 'OIH', 'NCH'), feature_group_count=xc.shape[1]) + conv_b[None, :, None]
        xi = jax.nn.silu(jnp.swapaxes(xc, 1, 2))
        xp = xi @ W_x
        delta = jax.nn.softplus(xp[..., :1] @ W_dt.T + b_dt)
        Bp = xp[..., 1:d_state + 1]
        Cp = xp[..., d_state + 1:]
        A = -jnp.exp(A_log)

        def step(h, inp):
            x_t, dt, Bt, Ct = inp
            A_bar = jnp.exp(dt[..., None] * A)
            h = A_bar * h + dt[..., None] * Bt[:, None, :] * x_t[..., None]
            y_t = jnp.einsum('bds,bs->bd', h, Ct) + D * x_t
            return (h, y_t)
        h0 = jnp.zeros((Bsz, xi.shape[-1], d_state), dtype=x.dtype)
        xs = (jnp.swapaxes(xi, 0, 1), jnp.swapaxes(delta, 0, 1), jnp.swapaxes(Bp, 0, 1), jnp.swapaxes(Cp, 0, 1))
        _, ys = jax.lax.scan(step, h0, xs)
        y = jnp.swapaxes(ys, 0, 1)
        y = y * jax.nn.silu(z)
        return y @ W_out

    def _L2_ffn_ref(x, Wg, W1, b1, W2, b2):
        import jax, jax.numpy as jnp
        import numpy as np
        B, L, H, E, FF, C = (4, 512, 256, 8, 1024, 2)
        b, l, h = x.shape
        e = Wg.shape[1]
        n = b * l
        k = min(max(int(n * C / e), 1), n)
        xt = x.reshape(n, h)
        S = jax.nn.sigmoid(xt @ Wg).T
        G, I = jax.lax.top_k(S, k)
        ex = xt[I]
        hid = jax.nn.gelu(jnp.einsum('ekh,ehf->ekf', ex, W1) + b1[:, None, :], approximate=False)
        out = (jnp.einsum('ekf,efh->ekh', hid, W2) + b2[:, None, :]) * G[..., None]
        new_x = jnp.zeros_like(xt).at[I.reshape(-1)].add(out.reshape(-1, h))
        return new_x.reshape(b, l, h)

    def _L3_xattn_ref(hidden_states, memory_state, q_w, k_w, norm_w, gate_w, gate_b):
        import jax, jax.numpy as jnp
        import numpy as np
        EPS = 1e-06

        def _rmsnorm(x, w, eps=EPS):
            x32 = x.astype(jnp.float32)
            var = jnp.mean(x32 * x32, axis=-1, keepdims=True)
            return (x32 * jax.lax.rsqrt(var + eps)).astype(x.dtype) * w
        B, S, H = hidden_states.shape
        K = memory_state.shape[1]
        scale = 1.0 / np.sqrt(H)
        normed = _rmsnorm(hidden_states, norm_w)
        v_pool = jnp.concatenate([normed, memory_state], axis=1)
        q = jnp.einsum('bsh,oh->bso', normed, q_w)
        k = jnp.einsum('bth,oh->bto', v_pool, k_w)
        logits = jnp.einsum('bsd,btd->bst', q, k) * scale
        local = jnp.tril(jnp.ones((S, S), bool))
        mask = jnp.concatenate([local, jnp.ones((S, K), bool)], axis=1)
        logits = jnp.where(mask[None], logits, -jnp.inf)
        attn = jax.nn.softmax(logits, axis=-1)
        h_tilde = jnp.einsum('bst,bth->bsh', attn, v_pool)
        alpha = jax.nn.sigmoid(jnp.einsum('bsh,oh->bso', hidden_states, gate_w) + gate_b)
        return (1.0 - alpha) * hidden_states + alpha * h_tilde

    def _L3_attn_ref(x, Wq, Wk, Wv, Wo):
        import jax, jax.numpy as jnp
        import numpy as np
        NUM_HEADS = 16
        B, N, C = x.shape
        H = NUM_HEADS
        hd = C // H

        def proj(W):
            return (x @ W).reshape(B, N, H, 2 * hd).transpose(0, 2, 1, 3)
        q = proj(Wq)
        k = proj(Wk)
        v = proj(Wv)
        q_r, q_i = (q[..., :hd], q[..., hd:])
        k_r, k_i = (k[..., :hd], k[..., hd:])
        v_r, v_i = (v[..., :hd], v[..., hd:])
        scores = (jnp.einsum('bhnd,bhmd->bhnm', q_r, k_r) + jnp.einsum('bhnd,bhmd->bhnm', q_i, k_i)) / jnp.sqrt(jnp.float32(hd))
        causal = jnp.tril(jnp.ones((N, N), dtype=bool))
        scores = jnp.where(causal[None, None], scores, -jnp.inf)
        probs = jax.nn.softmax(scores, axis=-1)
        out_r = jnp.einsum('bhnm,bhmd->bhnd', probs, v_r)
        out_i = jnp.einsum('bhnm,bhmd->bhnd', probs, v_i)
        out = jnp.concatenate([out_r, out_i], axis=-1)
        out = out.transpose(0, 2, 1, 3).reshape(B, N, 2 * C)
        return out @ Wo

    def _L3_ffn_ref(src, Wq, Wk_c, Wv_c, Wk, Wv, Wo, W_shared_in, W_shared_out, W1_shared, W2_experts, Wg_gate, We_gate, group_bias, expert_bias, norm1_w, norm2_w):
        import jax, jax.numpy as jnp
        import numpy as np
        D = 256
        H = 16
        DH = D // H
        DC = D // 4
        HID = 512
        G = 2
        EPG = 4
        E = G * EPG
        TOPK = 2
        EPS = 1e-06
        B, T = (2, 512)

        def _rope_sincos(t, dh):
            inv_freq = 1.0 / 10000.0 ** (jnp.arange(0, dh, 2, dtype=jnp.float32) / dh)
            ang = jnp.arange(t, dtype=jnp.float32)[:, None] * inv_freq[None, :]
            return (jnp.sin(ang), jnp.cos(ang))

        def _apply_rope(x, sin, cos):
            x1 = x[..., ::2]
            x2 = x[..., 1::2]
            r = jnp.stack([x1 * cos - x2 * sin, x1 * sin + x2 * cos], axis=-1)
            return r.reshape(x.shape)

        def _swiglu(x):
            a, b = jnp.split(x, 2, axis=-1)
            return jax.nn.silu(a) * b

        def _rmsnorm(x, w):
            return x * jax.lax.rsqrt(jnp.mean(x * x, axis=-1, keepdims=True) + EPS) * w
        Bb, Tt, C = src.shape
        q = (src @ Wq).reshape(Bb, Tt, H, DH).transpose(0, 2, 1, 3)
        k = (src @ Wk_c @ Wk).reshape(Bb, Tt, H, DH).transpose(0, 2, 1, 3)
        v = (src @ Wv_c @ Wv).reshape(Bb, Tt, H, DH).transpose(0, 2, 1, 3)
        sin, cos = _rope_sincos(Tt, DH)
        q = _apply_rope(q, sin, cos)
        k = _apply_rope(k, sin, cos)
        attn = jnp.einsum('bhqd,bhkd->bhqk', q, k) / np.sqrt(DH).astype(np.float32)
        attn = jax.nn.softmax(attn, axis=-1)
        sa = jnp.einsum('bhqk,bhkd->bhqd', attn, v)
        sa = sa.transpose(0, 2, 1, 3).reshape(Bb, Tt, C) @ Wo
        x = _rmsnorm(src + sa, norm1_w)
        S = Bb * Tt
        flat = x.reshape(S, C)
        shared = _swiglu(flat @ W_shared_in) @ W_shared_out
        g_probs = jax.nn.softmax(flat @ Wg_gate + group_bias, -1)
        g_idx = jnp.argmax(g_probs, axis=-1)
        e_logits = flat @ We_gate + expert_bias
        e_group = jnp.arange(E) // EPG
        in_group = e_group[None, :] == g_idx[:, None]
        e_probs = jax.nn.softmax(jnp.where(in_group, e_logits, -jnp.inf), -1)
        g_prob = jnp.take_along_axis(g_probs, g_idx[:, None], axis=1)
        p_expert = e_probs * g_prob
        topv, topi = jax.lax.top_k(p_expert, TOPK)
        w = jnp.zeros((S, E), flat.dtype).at[jnp.arange(S)[:, None], topi].set(topv)
        h = _swiglu(flat @ W1_shared)
        routed = jnp.zeros_like(shared)
        for e in range(E):
            routed = routed + h @ W2_experts[e] * w[:, e:e + 1]
        out = x + (shared + routed).reshape(Bb, Tt, C)
        return _rmsnorm(out, norm2_w)
    x = x + _L0_xattn_ref(_layernorm(x, axis=-1), fside_BxSxS_0, ctx_1024, ctx_1024, L0_xattn_Wq, L0_xattn_bq, L0_xattn_Wk, L0_xattn_bk, L0_xattn_Wv, L0_xattn_bv, L0_xattn_Wp, L0_xattn_bp)
    x = x + _L0_attn_ref(_layernorm(x, axis=-1), L0_attn_q_w, L0_attn_q_b, L0_attn_k_w, L0_attn_k_b, L0_attn_v_w, L0_attn_v_b, L0_attn_o_w, L0_attn_o_b)
    x = x + _L0_ffn_ref(_layernorm(x, axis=-1), L0_ffn_w1s, L0_ffn_w2s, L0_ffn_w3s, L0_ffn_W1, L0_ffn_W2, L0_ffn_W3, L0_ffn_Wg)
    x = x + _L1_xattn_ref(_layernorm(x, axis=-1), ctx_1024, ctx_1024, L1_xattn_w_q, L1_xattn_b_q, L1_xattn_w_k, L1_xattn_b_k, L1_xattn_w_v, L1_xattn_b_v, L1_xattn_w_o, L1_xattn_b_o)
    x = x + _L1_attn_ref(_layernorm(x, axis=-1), L1_attn_Wqkv, L1_attn_bqkv, L1_attn_Wout, L1_attn_bout, L1_attn_Wimp, L1_attn_bimp, L1_attn_Walpha, L1_attn_balpha, L1_attn_spike_threshold, L1_attn_log_k, L1_attn_qk_scale)
    x = x + _L1_ffn_ref(_layernorm(x, axis=-1), L1_ffn_W_r, L1_ffn_W_k, L1_ffn_W_v, L1_ffn_mu_r, L1_ffn_mu_k)
    x = x + _L2_xattn_ref(_layernorm(x, axis=-1), ctx_1024, L2_xattn_Wq, L2_xattn_bq, L2_xattn_Aq, L2_xattn_Bq, L2_xattn_Wf, L2_xattn_bf, L2_xattn_Af, L2_xattn_Bf, L2_xattn_Wp, L2_xattn_bp, L2_xattn_Ap, L2_xattn_Bp)
    x = x + _L2_attn_ref(_layernorm(x, axis=-1), L2_attn_W_in, L2_attn_conv_w, L2_attn_conv_b, L2_attn_W_x, L2_attn_W_dt, L2_attn_b_dt, L2_attn_A_log, L2_attn_D, L2_attn_W_out)
    x = x + _L2_ffn_ref(_layernorm(x, axis=-1), L2_ffn_Wg, L2_ffn_W1, L2_ffn_b1, L2_ffn_W2, L2_ffn_b2)
    x = x + _L3_xattn_ref(_layernorm(x, axis=-1), ctx_1024, L3_xattn_q_w, L3_xattn_k_w, L3_xattn_norm_w, L3_xattn_gate_w, L3_xattn_gate_b)
    x = x + _L3_attn_ref(_layernorm(x, axis=-1), L3_attn_Wq, L3_attn_Wk, L3_attn_Wv, L3_attn_Wo)
    x = x + _L3_ffn_ref(_layernorm(x, axis=-1), L3_ffn_Wq, L3_ffn_Wk_c, L3_ffn_Wv_c, L3_ffn_Wk, L3_ffn_Wv, L3_ffn_Wo, L3_ffn_W_shared_in, L3_ffn_W_shared_out, L3_ffn_W1_shared, L3_ffn_W2_experts, L3_ffn_Wg_gate, L3_ffn_We_gate, L3_ffn_group_bias, L3_ffn_expert_bias, L3_ffn_norm1_w, L3_ffn_norm2_w)
    return x

_drawn_inputs = setup_inputs


def setup_inputs(seed=0):
    import zlib

    import numpy as np

    out = dict(_drawn_inputs(seed))
    spreads = {'L0_xattn_bq': (0.0, 0.1),
     'L0_xattn_bk': (0.0, 0.1),
     'L0_xattn_bv': (0.0, 0.1),
     'L0_xattn_bp': (0.0, 0.1),
     'L1_attn_bqkv': (0.0, 0.1),
     'L1_attn_bout': (0.0, 0.1),
     'L1_attn_balpha': (0.0, 0.1),
     'L1_attn_log_k': (0.5400000214576721, 0.2),
     'L2_xattn_bq': (0.0, 0.1),
     'L2_xattn_Bq': (0.0, 0.1),
     'L2_xattn_bf': (0.0, 0.1),
     'L2_xattn_Bf': (0.0, 0.1),
     'L2_xattn_bp': (0.0, 0.1),
     'L2_xattn_Bp': (0.0, 0.1),
     'L2_attn_conv_b': (0.0, 0.1),
     'L2_attn_D': (1.0, 0.2),
     'L2_ffn_b1': (0.0, 0.1),
     'L2_ffn_b2': (0.0, 0.1),
     'L3_xattn_norm_w': (1.0, 0.2),
     'L3_xattn_gate_b': (0.0, 0.1),
     'L3_ffn_group_bias': (0.0, 0.1),
     'L3_ffn_expert_bias': (0.0, 0.1),
     'L3_ffn_norm1_w': (1.0, 0.2),
     'L3_ffn_norm2_w': (1.0, 0.2)}
    factors = {}
    for name, (base, spread) in spreads.items():
        noise = np.random.default_rng([zlib.crc32(name.encode()), seed]).standard_normal(out[name].shape)
        drawn = base * np.exp(spread * noise) if base else spread * noise
        out[name] = jnp.asarray(drawn.astype(out[name].dtype))
    for name, factor in factors.items():
        out[name] = (out[name] * factor).astype(out[name].dtype)
    return out
```

```python
from contextlib import ExitStack, contextmanager

import concourse.bass as bass
import numpy as np
from concourse import mybir

F32 = mybir.dt.float32
ACT = mybir.ActivationFunctionType
ALU = mybir.AluOpType
AX = mybir.AxisListType
P = 128
B = 2
T = 256
C = 256
H = 16
KC = C // P
NT = B * T // P
NTOK = B * T
TB = T // P
S = 4096
ST = S // P
E = 8
FF = 1024
FC = FF // P
MASKED = -1.0e30


@contextmanager
def stage(nc, *names):
    with ExitStack() as es:
        sems = [es.enter_context(nc.semaphore(n)) for n in names]
        nums = [s.num for s in sems]
        with nc.Block() as block:
            yield (block, *sems)
        nc.all_engine_barrier(sems_to_clear=range(min(nums), max(nums) + 1))


class Steps:

    def __init__(self, engine, done):
        self.engine, self.done, self.n = engine, done, 0

    def __call__(self, instruction):
        self.n += 1
        instruction.then_inc(self.done, 1)
        self.engine.wait_ge(self.done, self.n)


class Pool:

    def __init__(self, nc, es, prefix):
        self.nc, self.es, self.prefix = nc, es, prefix

    def sb(self, name, shape, dt=F32):
        return self.es.enter_context(self.nc.sbuf_tensor(f"{self.prefix}_{name}", shape, dt))

    def ps(self, name, shape, dt=F32):
        return self.es.enter_context(self.nc.psum_tensor(f"{self.prefix}_{name}", shape, dt))


@contextmanager
def pool(nc, prefix):
    with ExitStack() as es:
        yield Pool(nc, es, prefix)


def load(nc, pairs):
    with stage(nc, "loaded_sp", "loaded_act") as (block, loaded_sp, loaded_act):
        @block.sync
        def _(sp):
            for dst, src in pairs[0::2]:
                sp.dma_start(dst, src).then_inc(loaded_sp, 16)
            sp.wait_ge(loaded_sp, 16 * len(pairs[0::2]))

        @block.scalar
        def _(act):
            for dst, src in pairs[1::2]:
                act.dma_start(dst, src).then_inc(loaded_act, 16)
            if pairs[1::2]:
                act.wait_ge(loaded_act, 16 * len(pairs[1::2]))


def normalize(nc, K, X, xn, xnT, eps, rms=False, w=None):
    with pool(nc, f"nrm{nc.next_id()}") as p:
        stats = p.sb("stats", [P, NT, 6])
        mv = p.sb("mv", [P, NT, 2])
        var = p.sb("var", [P, NT])
        sd = p.sb("sd", [P, NT])
        rstd = p.sb("rstd", [P, NT])
        shift = p.sb("shift", [P, NT])
        sq = p.sb("sq", [P, C])
        psT = p.ps("psT", [P, KC, 512])
        with stage(nc, "dve_step", "var_ready", "sd_ready", "rows_ready", "turned", "stored") as \
                (block, dve_step, var_ready, sd_ready, rows_ready, turned, stored):
            @block.vector
            def _(dve):
                step = Steps(dve, dve_step)
                for t in range(NT):
                    nc.vector.bn_stats(stats[:, t, :], X[:, t, :]).then_inc(dve_step, 1)
                step.n = NT
                dve.wait_ge(dve_step, step.n)
                for t in range(NT):
                    nc.vector.bn_aggr(mv[:, t, :], stats[:, t, :]).then_inc(dve_step, 1)
                step.n += NT
                dve.wait_ge(dve_step, step.n)
                if rms:
                    step(nc.vector.tensor_tensor(shift[:], mv[:, :, 0], mv[:, :, 0], ALU.mult))
                    step(nc.vector.tensor_tensor(shift[:], shift[:], mv[:, :, 1], ALU.add))
                    nc.vector.tensor_scalar(var[:], shift[:], eps, None, ALU.add).then_inc(var_ready, 1)
                else:
                    nc.vector.tensor_scalar(var[:], mv[:, :, 1], eps, None, ALU.add).then_inc(var_ready, 1)
                dve.wait_ge(sd_ready, 1)
                step(nc.vector.reciprocal(rstd[:], sd[:]))
                for t in range(NT):
                    if rms:
                        step(nc.vector.tensor_scalar(xn[:, t, :], X[:, t, :], rstd[:, t:t + 1], None, ALU.mult))
                        nc.vector.tensor_tensor(xn[:, t, :], xn[:, t, :], w[:, :], ALU.mult).then_inc(rows_ready, 1)
                    else:
                        nc.vector.tensor_scalar(xn[:, t, :], X[:, t, :], mv[:, t, 0:1], rstd[:, t:t + 1],
                                                ALU.subtract, ALU.mult).then_inc(rows_ready, 1)
                if xnT is not None:
                    dve.wait_ge(turned, 1)
                    nc.vector.tensor_copy(xnT[:, :, :], psT[:, :, :]).then_inc(stored, 1)

            @block.scalar
            def _(act):
                act.wait_ge(var_ready, 1)
                nc.scalar.activation(sd[:], var[:], ACT.Sqrt).then_inc(sd_ready, 1)

            @block.tensor
            def _(pe):
                if xnT is None:
                    return
                for t in range(NT):
                    pe.wait_ge(rows_ready, t + 1)
                    for k in range(KC):
                        last = nc.tensor.transpose(psT[:, k, t * P:(t + 1) * P], xn[:, t, k * P:(k + 1) * P], K["ident"])
                last.then_inc(turned, 1)


def gemms(nc, K, jobs, ring=4):
    with pool(nc, f"gem{nc.next_id()}") as p:
        banks = p.ps("banks", [P, ring, 512])
        turn = [sum(1 for j in jobs[:n] if j[4] == jobs[n][4]) for n in range(len(jobs))]
        with stage(nc, "product_ready", "dve_took", "act_took", "dve_step", "act_step") as \
                (block, product_ready, dve_took, act_took, dve_step, act_step):
            took = {"v": dve_took, "s": act_took}

            def view(n):
                return banks[0:jobs[n][0], n % ring, 0:jobs[n][1]]

            @block.tensor
            def _(pe):
                for n, (_, _, terms, _, _) in enumerate(jobs):
                    if n >= ring:
                        pe.wait_ge(took[jobs[n - ring][4]], turn[n - ring] + 1)
                    for i, term in enumerate(terms):
                        if term[0] == "turn":
                            _, rows, at = term
                            last = nc.tensor.transpose(view(n)[:, at:at + rows.shape[0]], rows, K["ident"])
                        elif len(term) > 2:
                            lhsT, rhs, at, first, final = term
                            last = nc.tensor.matmul(view(n)[:, at:at + rhs.shape[1]], lhsT, rhs, start=first, stop=final)
                        else:
                            last = nc.tensor.matmul(view(n), *term, start=i == 0, stop=i == len(terms) - 1)
                    last.then_inc(product_ready, 1)

            @block.vector
            def _(dve):
                step = Steps(dve, dve_step)
                for n, job in enumerate(jobs):
                    if job[4] == "v":
                        dve.wait_ge(product_ready, n + 1)
                        job[3](view(n), step).then_inc(dve_took, 1)

            @block.scalar
            def _(act):
                step = Steps(act, act_step)
                for n, job in enumerate(jobs):
                    if job[4] == "s":
                        act.wait_ge(product_ready, n + 1)
                        job[3](view(n), step).then_inc(act_took, 1)


def vcopy(nc, dst):
    return lambda ps, step: nc.vector.tensor_copy(dst, ps)


def scopy(nc, dst):
    return lambda ps, step: nc.scalar.copy(dst, ps)


def vadd(nc, dst, other):
    return lambda ps, step: nc.vector.tensor_tensor(dst, ps, other, ALU.add)


def vbias(nc, dst, bias):
    return lambda ps, step: nc.vector.tensor_scalar(dst, ps, bias, None, ALU.add)


def sbias(nc, dst, bias):
    return lambda ps, step: nc.scalar.activation(dst, ps, ACT.Identity, bias=bias)


def project_T(W, n_out, xT, evac, engine, cols=NTOK, kc=KC):
    return [(P, cols, [(W[:, k, m * P:(m + 1) * P], xT[:, k, 0:cols]) for k in range(kc)], evac(m), engine)
            for m in range(n_out // P)]


def project_rows(W, n_out, xT, evac, engine, bias=None, tiles=NT, kc=KC, ones=None):
    extra = [(ones, bias)] if bias is not None else []
    return [(P, n_out, [(xT[:, k, t * P:(t + 1) * P], W[:, k, 0:n_out]) for k in range(kc)] + extra, evac(t), engine)
            for t in range(tiles)]


def over_heads(x, nh):
    return x.unsqueeze(1).to_broadcast([P, nh, x.shape[1]])


def attention(nc, K, groups, nh, scale, key_tiles, mask):
    HP = P // nh
    D = HP // 2
    G = len(groups)
    PAIRS = nh // 2
    CB = key_tiles // 2
    UNITS = CB * PAIRS
    SLOTS = 3
    NP = 3
    with pool(nc, f"att{nc.next_id()}") as p:
        psS = p.ps("psS", [P, SLOTS, 2, 512])
        psO = p.ps("psO", [P, 512])
        psM = p.ps("psM", [P, 512])
        parts = p.sb("parts", [P, nh, 2 * CB])
        mpads = [p.sb(f"mpad{i}", [P, TB, P]) for i in range(2)]
        qB = p.sb("qB", [P, 2, T])
        probs = p.sb("probs", [P, NP, 2, 512])
        OT = p.sb("OT", [P, T])
        rec = p.sb("rec", [P, T])
        if mask:
            mska = p.sb("mska", [P, 2, 512])
            mskb = p.sb("mskb", [P, 2, 2, 512])
        with stage(nc, "dve_step", "scores_ready", "max_taken", "masked", "max_ready", "max_turned",
                   "shifted", "probs_ready", "probs_used", "o_copied", "sums_ready", "sums_used", "out_ready") as \
                (block, dve_step, scores_ready, max_taken, masked, max_ready, max_turned,
                 shifted, probs_ready, probs_used, o_copied, sums_ready, sums_used, out_ready):
            order = [(0, 0, u) for u in range(UNITS)]
            for g in range(G):
                if g + 1 < G:
                    order += [(0, g + 1, u) for u in range(UNITS)]
                order += [(1, g, u) for u in range(UNITS)]
            place = {unit: n for n, unit in enumerate(order)}

            @block.tensor
            def _(pe):
                def free_slot(n):
                    if n >= SLOTS:
                        kind, g, u = order[n - SLOTS]
                        pe.wait_ge(probs_ready if kind else max_taken, g * UNITS + u + 1)

                def maxima(g):
                    q, k, _, _ = groups[g]
                    for u in range(UNITS):
                        n = place[0, g, u]
                        free_slot(n)
                        for i in range(2):
                            t, c = (u // PAIRS * 2 + i) // CB, (u // PAIRS * 2 + i) % CB
                            for j in range(2):
                                h = u % PAIRS * 2 + j
                                r = slice(HP * h, HP * h + HP)
                                last = nc.tensor.matmul(psS[:, n % SLOTS, j, i * 256:(i + 1) * 256],
                                                        q[r, t * P:(t + 1) * P], k[r, c * 256:(c + 1) * 256],
                                                        start=True, stop=True)
                        last.then_inc(scores_ready, 1)

                def turn_maxima(g):
                    pe.wait_ge(max_ready, g + 1)
                    if g:
                        pe.wait_ge(sums_used, g)
                    for t in range(TB):
                        last = nc.tensor.transpose(psM[:, t * P:(t + 1) * P], mpads[g % 2][:, t, :], K["ident"])
                    last.then_inc(max_turned, 1)

                def probabilities(g):
                    _, k, v, _ = groups[g]
                    pe.wait_ge(shifted, g + 1)
                    for u in range(UNITS + 1):
                        if u < UNITS:
                            n = place[1, g, u]
                            free_slot(n)
                            for i in range(2):
                                kt = u // PAIRS * 2 + i
                                for j in range(2):
                                    h = u % PAIRS * 2 + j
                                    r = slice(HP * h, HP * h + HP)
                                    last = nc.tensor.matmul(psS[:, n % SLOTS, j, i * 256:(i + 1) * 256],
                                                            k[r, kt * P:(kt + 1) * P], qB[r, g % 2, :],
                                                            start=True, stop=True)
                            last.then_inc(scores_ready, 1)
                        if u >= 1:
                            w = g * UNITS + u - 1
                            if u == 1 and g:
                                pe.wait_ge(o_copied, g)
                            pe.wait_ge(probs_ready, w + 1)
                            for i in range(2):
                                kt = (u - 1) // PAIRS * 2 + i
                                for j in range(2):
                                    h = (u - 1) % PAIRS * 2 + j
                                    last = nc.tensor.matmul(psO[HP * h:HP * h + HP, 0:T],
                                                            v(kt)[:, HP * h:HP * h + HP],
                                                            probs[:, w % NP, j, i * 256:(i + 1) * 256],
                                                            start=kt == 0, stop=kt == key_tiles - 1)
                            last.then_inc(probs_used, 1)

                def sums(g):
                    pe.wait_ge(o_copied, g + 1)
                    nc.tensor.matmul(psM[:, 0:T], K["sel"][HP], OT[:], start=True, stop=True).then_inc(sums_ready, 1)

                maxima(0)
                for g in range(G):
                    if g + 1 < G:
                        maxima(g + 1)
                    if g:
                        sums(g - 1)
                    turn_maxima(g)
                    probabilities(g)
                sums(G - 1)

            @block.vector
            def _(dve):
                step = Steps(dve, dve_step)
                for m in mpads:
                    step(nc.vector.memset(m[:], 0.0))

                def take_maxima(g):
                    for u in range(UNITS):
                        n = place[0, g, u]
                        dve.wait_ge(scores_ready, n + 1)
                        src = psS[:, n % SLOTS, :, :]
                        if mask:
                            if g or u:
                                dve.wait_ge(max_taken, g * UNITS + u)
                            step(nc.vector.tensor_tensor(mska[:], src, over_heads(K["mask_q"].rearrange("p s n -> p (s n)"), 2), ALU.add))
                            src = mska[:]
                        h, s = u % PAIRS * 2, u // PAIRS * 2
                        nc.vector.tensor_reduce(parts[:, h:h + 2, s:s + 2], src.rearrange("p j (i n) -> p j i n", i=2),
                                                AX.X, ALU.max).then_inc(max_taken, 1)
                    dve.wait_ge(max_taken, (g + 1) * UNITS)
                    if g >= 2:
                        dve.wait_ge(max_turned, g - 1)
                    for t in range(TB):
                        dst = mpads[g % 2][:, t, :].rearrange("p (h d) -> p h d", h=nh)[:, :, D]
                        last = nc.vector.tensor_reduce(dst, parts[:, :, t * CB:(t + 1) * CB], AX.X, ALU.max, negate=True)
                        if t < TB - 1:
                            step(last)
                    last.then_inc(max_ready, 1)
                    dve.wait_ge(max_ready, g + 1)

                def shift(g):
                    dve.wait_ge(max_turned, g + 1)
                    nc.vector.tensor_tensor(qB[:, g % 2, :], psM[:, 0:T], groups[g][0], ALU.add).then_inc(shifted, 1)

                def add_mask(g):
                    for u in range(UNITS):
                        n, w = place[1, g, u], g * UNITS + u
                        dve.wait_ge(scores_ready, n + 1)
                        if w >= 2:
                            dve.wait_ge(probs_ready, w - 1)
                        nc.vector.tensor_tensor(mskb[:, w % 2, :, :], psS[:, n % SLOTS, :, :],
                                                over_heads(K["mask_k"].rearrange("p s n -> p (s n)"), 2), ALU.add).then_inc(masked, 1)

                def copy_o(g):
                    dve.wait_ge(probs_used, (g + 1) * UNITS)
                    if g:
                        dve.wait_ge(out_ready, g)
                    nc.vector.tensor_copy(OT[:], psO[:, 0:T]).then_inc(o_copied, 1)

                def divide(g):
                    dve.wait_ge(sums_ready, g + 1)
                    if g:
                        dve.wait_ge(out_ready, g)
                    nc.vector.reciprocal(rec[:], psM[:, 0:T]).then_inc(sums_used, 1)
                    dve.wait_ge(sums_used, g + 1)
                    nc.vector.tensor_tensor(groups[g][3], OT[:], rec[:], ALU.mult).then_inc(out_ready, 1)

                take_maxima(0)
                for g in range(G):
                    if g + 1 < G:
                        take_maxima(g + 1)
                    if g:
                        divide(g - 1)
                    shift(g)
                    if mask:
                        add_mask(g)
                    copy_o(g)
                divide(G - 1)

            @block.scalar
            def _(act):
                for g in range(G):
                    for u in range(UNITS):
                        n, w = place[1, g, u], g * UNITS + u
                        if w >= NP:
                            act.wait_ge(probs_used, w - NP + 1)
                        if mask:
                            act.wait_ge(masked, w + 1)
                            src = mskb[:, w % 2, :, :]
                        else:
                            act.wait_ge(scores_ready, n + 1)
                            src = psS[:, n % SLOTS, :, :]
                        nc.scalar.activation(probs[:, w % NP, :, :], src, ACT.Exp, scale=scale).then_inc(probs_ready, 1)


class Weights:

    def __init__(self, nc, p, name, arrays, specs):
        self.specs = specs[name]
        n = sum(int(np.prod(shape[1:])) for _, shape in self.specs.values())
        self.tile = p.sb("weights", [P, n])
        cut = [n * i // 4 for i in range(5)]
        load(nc, [(self.tile[:, a:b], arrays[name][:, a:b]) for a, b in zip(cut, cut[1:]) if b > a])

    def __getitem__(self, key):
        at, shape = self.specs[key]
        n = int(np.prod(shape[1:]))
        view = self.tile[0:shape[0], at:at + n]
        if len(shape) == 3:
            view = view.rearrange("p (k n) -> p k n", k=shape[1])
        return view


def add_to_residual(nc, K, X, W, attT, kc, bias):
    gemms(nc, K, project_rows(W, C, attT, lambda t: vadd(nc, X[:, t, :], X[:, t, :]), "v",
                           bias=bias, kc=kc, ones=K["ones"][0:1, :]))


def alibi_attention(nc, K, X, arrays, specs):
    with pool(nc, "l0a") as p:
        w = Weights(nc, p, "L0_attn", arrays, specs)
        xn = p.sb("xn", [P, NT, C])
        xnT = p.sb("xnT", [P, KC, NTOK])
        qT = p.sb("qT", [P, 4, NTOK])
        kT = p.sb("kT", [P, 4, NTOK])
        v = p.sb("v", [P, NT, 512])
        attT = p.sb("attT", [P, 4, NTOK])
        normalize(nc, K, X, xn, xnT, 1e-5)

        def with_table(dst, bias, table):
            return lambda m: (lambda ps, step: nc.vector.scalar_tensor_tensor(
                out=dst[:, m, :], in0=ps, scalar=bias[:, m:m + 1], in1=table[:, m, :], op0=ALU.add, op1=ALU.add))

        gemms(nc, K, project_T(w["q"], 512, xnT, with_table(qT, w["bq"], w["q_table"]), "v")
              + project_T(w["k"], 512, xnT, with_table(kT, w["bk"], w["k_table"]), "v")
              + project_rows(w["v"], 512, xnT, lambda t: scopy(nc, v[:, t, :]), "s", bias=w["bv"], ones=K["ones"][0:1, :]))
        self_attend(nc, K, qT, kT, v, attT, 4, True)
        add_to_residual(nc, K, X, w["o"], attT, 4, w["bo"])


def self_attend(nc, K, qT, kT, v, attT, nh, mask, k_tokens=T):
    chunks = H // nh
    groups = []
    for b in range(B):
        for c in range(chunks):
            def values(kt, b=b, c=c):
                return v[:, b * TB + kt, c * P:(c + 1) * P]
            groups.append((qT[:, c, b * T:(b + 1) * T], kT[:, c, b * T:(b + 1) * T], values, attT[:, c, b * T:(b + 1) * T]))
    attention(nc, K, groups, nh, float(C // H) ** -0.5, TB, mask)


def turn_all(K, rows, tiles, width, evac, engine):
    return [(P, P * min(4, tiles), [("turn", rows[:, t0 + t, k * P:(k + 1) * P], t * P) for t in range(min(4, tiles))],
             evac(k, t0), engine) for t0 in range(0, tiles, 4) for k in range(width // P)]


def cross_attention(nc, K, X, arrays, specs, name):
    raw = name == "L0_xattn"
    with pool(nc, name) as p:
        w = Weights(nc, p, name, arrays, specs)
        KT = ST + (TB if raw else 0)
        qT = p.sb("qT", [P, 4 * NTOK])
        attT = p.sb("attT", [P, 4 * NTOK])
        cx = p.sb("cx", [P, ST, C])
        qc = p.sb("qc", [P, T])
        oc = p.sb("oc", [P, T])
        kc = p.sb("kc", [P, KT * P])
        vc = p.sb("vc", [P, KT, P])
        with pool(nc, name + "q") as p1:
            xn = p1.sb("xn", [P, NT, C])
            xnT = p1.sb("xnT", [P, KC, NTOK])
            normalize(nc, K, X, xn, xnT, 1e-5)
            gemms(nc, K, project_T(w["q"], 512, xnT, lambda m: vbias(nc, qT[:, m * NTOK:(m + 1) * NTOK], w["bq"][:, m:m + 1]), "v"))
        if raw:
            sk = p.sb("sk", [P, 4 * NTOK])
            sv = p.sb("sv", [P, NT * 512])
            with pool(nc, name + "s") as p1:
                side = p1.sb("side", [P, NT, C])
                sideT = p1.sb("sideT", [P, KC, NTOK])
                load(nc, [(side[:, t, :], arrays["fside"][t // TB, (t % TB) * P:(t % TB + 1) * P, :]) for t in range(NT)])
                gemms(nc, K, turn_all(K, side, NT, C, lambda k, t0: vcopy(nc, sideT[:, k, :]), "v"))
                gemms(nc, K, project_T(w["k"], 512, sideT, lambda m: vbias(nc, sk[:, m * NTOK:(m + 1) * NTOK], w["bk"][:, m:m + 1]), "v")
                      + project_rows(w["v"], 512, sideT, lambda t: scopy(nc, sv[:, t * 512:(t + 1) * 512]), "s",
                                     bias=w["bv"], ones=K["ones"][0:1, :]))
        else:
            cxT = p.sb("cxT", [P, KC, S])
            wk = p.sb("wk", [P, KC, P])
            wv = p.sb("wv", [P, KC, P])
            bk = p.sb("bk", [P, 1])
            bv = p.sb("bv", [1, P])
        with stage(nc, "cleared") as (block, cleared):
            @block.vector
            def _(dve):
                nc.vector.memset(vc[:], 0.0).then_inc(cleared, 1)
                dve.wait_ge(cleared, 1)
                nc.vector.memset(vc[:].rearrange("p t (h d) -> p t h d", h=4)[:, :, :, 16], 1.0).then_inc(cleared, 1)
                dve.wait_ge(cleared, 2)
        with nc.Fori(0, B) as b:
            ctx_b = arrays["ctx"][bass.ds(b, 1)].rearrange("o (p n) c -> p (o n) c", p=P)
            load(nc, [(cx[:, n:n + 8, :], ctx_b[:, n:n + 8, :]) for n in range(0, ST, 8)])
            if not raw:
                gemms(nc, K, [job for n in range(0, ST, 4) for job in (
                    (P, 512, [("turn", cx[:, n + t, 0:P], t * P) for t in range(4)], vcopy(nc, cxT[:, 0, n * P:(n + 4) * P]), "v"),
                    (P, 512, [("turn", cx[:, n + t, P:C], t * P) for t in range(4)], scopy(nc, cxT[:, 1, n * P:(n + 4) * P]), "s"))])
            with nc.Fori(0, 4) as c:
                with stage(nc, "staged") as (block, staged):
                    @block.vector
                    def _(dve):
                        nc.vector.tensor_copy(qc[:], qT[:, bass.ds(c * NTOK + b * T, T)]).then_inc(staged, 1)
                        if raw:
                            nc.vector.tensor_copy(kc[:, S:S + T], sk[:, bass.ds(c * NTOK + b * T, T)]).then_inc(staged, 1)
                            for t in range(TB):
                                nc.vector.tensor_copy(vc[:, ST + t, :], sv[:, bass.ds((b * TB + t) * 512 + c * P, P)]).then_inc(staged, 1)
                            for j in range(4):
                                nc.vector.tensor_copy(vc[:, 0:ST, 32 * j:32 * j + 16],
                                                      cx[:, :, bass.ds(c * 64 + j * 16, 16)]).then_inc(staged, 1)
                            dve.wait_ge(staged, 8)
                        else:
                            for k in range(KC):
                                nc.vector.tensor_copy(wk[:, k, :], w["k"][:, k, bass.ds(c * P, P)]).then_inc(staged, 1)
                                nc.vector.tensor_copy(wv[:, k, :], w["v"][:, k, bass.ds(c * P, P)]).then_inc(staged, 1)
                            nc.vector.tensor_copy(bk[:], w["bk"][:, bass.ds(c, 1)]).then_inc(staged, 1)
                            nc.vector.tensor_copy(bv[:], w["bv"][:, bass.ds(c * P, P)]).then_inc(staged, 1)
                            dve.wait_ge(staged, 7)
                if raw:
                    gemms(nc, K, [(P, 512, [("turn", vc[:, n + t, :], t * P) for t in range(4)],
                                   (scopy if n % 8 else vcopy)(nc, kc[:, n * P:(n + 4) * P]), "s" if n % 8 else "v")
                                  for n in range(0, ST, 4)])
                else:
                    ones = K["ones"][0:1, :]
                    jobs = []
                    for n in range(0, ST, 4):
                        jobs.append((P, 512, [(wk[:, k, :], cxT[:, k, n * P:(n + 4) * P]) for k in range(KC)],
                                     sbias(nc, kc[:, n * P:(n + 4) * P], bk[:, 0:1]), "s"))
                        jobs.append((P, 512, [term for t in range(4) for term in (
                            (cxT[:, 0, (n + t) * P:(n + t + 1) * P], wv[:, 0, :], t * P, True, False),
                            (cxT[:, 1, (n + t) * P:(n + t + 1) * P], wv[:, 1, :], t * P, False, False),
                            (ones, bv[:], t * P, False, True))],
                            vcopy(nc, vc[:, n:n + 4, :].rearrange("p t d -> p (t d)")), "v"))
                    gemms(nc, K, jobs)
                attention(nc, K, [(qc[:], kc[:], lambda kt: vc[:, kt, :], oc[:])], 4, 0.25, KT, False)
                with stage(nc, "kept") as (block, kept):
                    @block.vector
                    def _(dve):
                        nc.vector.tensor_copy(attT[:, bass.ds(c * NTOK + b * T, T)], oc[:]).then_inc(kept, 1)
                        dve.wait_ge(kept, 1)
        add_to_residual(nc, K, X, w["o"], attT[:].rearrange("p (c n) -> p c n", c=4), 4, w["bo"])


def lora_attention(nc, K, X, arrays, specs):
    with pool(nc, "l2x") as p:
        w = Weights(nc, p, "L2_xattn", arrays, specs)
        xn = p.sb("xn", [P, NT, C])
        xnT = p.sb("xnT", [P, KC, NTOK])
        side = p.sb("side", [P, NT, C])
        sideT = p.sb("sideT", [P, KC, NTOK])
        qT = p.sb("qT", [P, 4, NTOK])
        kT = p.sb("kT", [P, 4, NTOK])
        v = p.sb("v", [P, NT, 512])
        attT = p.sb("attT", [P, 4, NTOK])
        lowq = p.sb("lowq", [16, NTOK])
        lowf = p.sb("lowf", [16, NTOK])
        lowp = p.sb("lowp", [16, NTOK])
        load(nc, [(side[:, t, :], arrays["ctx"][t // TB, (t % TB) * P:(t % TB + 1) * P, :]) for t in range(NT)])
        normalize(nc, K, X, xn, xnT, 1e-5)
        gemms(nc, K, turn_all(K, side, NT, C, lambda k, t0: vcopy(nc, sideT[:, k, :]), "v"))

        def low(dst, A, xT, kc):
            return (16, NTOK, [(A[:, k, :], xT[:, k, :]) for k in range(kc)],
                    lambda ps, step: nc.scalar.mul(dst[:], ps, 1.0 / 16.0), "s")

        gemms(nc, K, [low(lowq, w["Aq"], xnT, KC), low(lowf, w["Af"], sideT, KC)])
        jobs = []
        for W, Bm, lo, xT, dst, bias in ((w["q"], w["Bq"], lowq, xnT, qT, w["bq"]), (w["k"], w["Bk"], lowf, sideT, kT, w["bk"])):
            for m in range(4):
                s = slice(m * P, (m + 1) * P)
                jobs.append((P, NTOK, [(W[:, k, s], xT[:, k, :]) for k in range(KC)] + [(Bm[:, 0, s], lo[:])],
                             vbias(nc, dst[:, m, :], bias[:, m:m + 1]), "v"))
        for t in range(NT):
            s = slice(t * P, (t + 1) * P)
            jobs.append((P, 512, [(sideT[:, k, s], w["v"][:, k, :]) for k in range(KC)]
                         + [(lowf[:, s], w["Bv"][:, 0, :]), (K["ones"][0:1, :], w["bv"])], scopy(nc, v[:, t, :]), "s"))
        gemms(nc, K, jobs)
        self_attend(nc, K, qT, kT, v, attT, 4, True)
        gemms(nc, K, [low(lowp, w["Ap"], attT, 4)])
        gemms(nc, K, [(P, C, [(attT[:, k, t * P:(t + 1) * P], w["o"][:, k, :]) for k in range(4)]
                       + [(lowp[:, t * P:(t + 1) * P], w["Bp"][:, 0, :]), (K["ones"][0:1, :], w["bo"])],
                       vadd(nc, X[:, t, :], X[:, t, :]), "v") for t in range(NT)])


def complex_attention(nc, K, X, arrays, specs):
    with pool(nc, "l3a") as p:
        w = Weights(nc, p, "L3_attn", arrays, specs)
        xn = p.sb("xn", [P, NT, C])
        xnT = p.sb("xnT", [P, KC, NTOK])
        qT = p.sb("qT", [P, 8, NTOK])
        kT = p.sb("kT", [P, 8, NTOK])
        v = p.sb("v", [P, NT, 1024])
        attT = p.sb("attT", [P, 8, NTOK])
        normalize(nc, K, X, xn, xnT, 1e-5)
        gemms(nc, K, project_T(w["q"], 1024, xnT, lambda m: vcopy(nc, qT[:, m, :]), "v")
              + project_T(w["k"], 1024, xnT, lambda m: vbias(nc, kT[:, m, :], w["bk"][:, m:m + 1]), "v")
              + [(P, 512, [(xnT[:, k, t * P:(t + 1) * P], w["v"][:, k, n * 512:(n + 1) * 512]) for k in range(KC)]
                  + [(K["ones"][0:1, :], w["bv"][:, n * 512:(n + 1) * 512])], scopy(nc, v[:, t, n * 512:(n + 1) * 512]), "s")
                 for t in range(NT) for n in range(2)])
        self_attend(nc, K, qT, kT, v, attT, 2, True)
        gemms(nc, K, project_rows(w["o"], C, attT, lambda t: vadd(nc, X[:, t, :], X[:, t, :]), "v", kc=8))


def channel_mix(nc, K, X, arrays, specs):
    with pool(nc, "l1f") as p:
        w = Weights(nc, p, "L1_ffn", arrays, specs)
        xn = p.sb("xn", [P, NT, C])
        xnT = p.sb("xnT", [P, KC, NTOK])
        prev = p.sb("prev", [P, KC, NTOK])
        xr = p.sb("xr", [P, KC, NTOK])
        xk = p.sb("xk", [P, KC, NTOK])
        om = p.sb("om", [P, 2 * KC])
        r = p.sb("r", [P, NT, C])
        relu = p.sb("relu", [P, KC, NTOK])
        k2 = p.sb("k2", [P, KC, NTOK])
        gated = p.sb("gated", [P, NT, C])
        normalize(nc, K, X, xn, xnT, 1e-5)
        with stage(nc, "dve_step") as (block, dve_step):
            @block.vector
            def _(dve):
                step = Steps(dve, dve_step)
                step(nc.vector.memset(prev[:].rearrange("p k (b t) -> p k b t", b=B)[:, :, :, 0], 0.0))
                for k in range(KC):
                    step(nc.vector.tensor_copy(prev[:, k, :].rearrange("p (b t) -> p b t", b=B)[:, :, 1:T],
                                               xnT[:, k, :].rearrange("p (b t) -> p b t", b=B)[:, :, 0:T - 1]))
                step(nc.vector.tensor_scalar(om[:], w["mu"], -1.0, 1.0, ALU.mult, ALU.add))
                for dst, at in ((xr, 0), (xk, KC)):
                    for k in range(KC):
                        step(nc.vector.tensor_scalar(dst[:, k, :], prev[:, k, :], om[:, at + k:at + k + 1], None, ALU.mult))
                        step(nc.vector.scalar_tensor_tensor(out=dst[:, k, :], in0=xnT[:, k, :], scalar=w["mu"][:, at + k:at + k + 1],
                                                            in1=dst[:, k, :], op0=ALU.mult, op1=ALU.add))

        def square(m):
            def evac(ps, step):
                step(nc.vector.tensor_scalar(relu[:, m, :], ps, 0.0, None, ALU.max))
                return nc.vector.tensor_tensor(k2[:, m, :], relu[:, m, :], relu[:, m, :], ALU.mult)
            return evac

        gemms(nc, K, project_T(w["k"], C, xk, square, "v")
              + project_rows(w["r"], C, xr, lambda t: (lambda ps, step: nc.scalar.activation(r[:, t, :], ps, ACT.Sigmoid)), "s"))

        def gate(t):
            def evac(ps, step):
                step(nc.vector.tensor_tensor(gated[:, t, :], ps, r[:, t, :], ALU.mult))
                return nc.vector.tensor_tensor(X[:, t, :], X[:, t, :], gated[:, t, :], ALU.add)
            return evac

        gemms(nc, K, project_rows(w["v"], C, k2, gate, "v"))


def routed_geglu(nc, K, X, arrays, specs):
    with pool(nc, "l0f") as p:
        w = Weights(nc, p, "L0_ffn", arrays, specs)
        xn = p.sb("xn", [P, NT, C])
        xnT = p.sb("xnT", [P, KC, NTOK])
        W1 = [p.sb(f"W1_{i}", [P, KC, FF]) for i in range(2)]
        W2 = [p.sb(f"W2_{i}", [P, KC, FF]) for i in range(2)]
        W3 = [p.sb(f"W3_{i}", [P, FC, C]) for i in range(2)]
        logits = p.sb("logits", [P, NT, E])
        best = p.sb("best", [P, NT])
        at = p.sb("at", [P, NT, E])
        first = p.sb("first", [P, NT])
        chosen = p.sb("chosen", [P, (E + 1) * NT])
        here = p.sb("here", [P, 2, NT])
        gel = p.sb("gel", [P, 2, NTOK])
        hT = p.sb("hT", [P, FC, NTOK])

        def sources(e):
            one = bass.ds(e, 1)
            return [arrays["W1"][one].rearrange("o (k p) n -> p (o k) n", p=P),
                    arrays["W2"][one].rearrange("o (k p) n -> p (o k) n", p=P),
                    arrays["W3"][one].rearrange("o (k p) n -> p (o k) n", p=P)]

        load(nc, list(zip((W1[0][:], W2[0][:], W3[0][:]), sources(0))))
        normalize(nc, K, X, xn, xnT, 1e-5)
        gemms(nc, K, project_rows(w["gate"], E, xnT, lambda t: vcopy(nc, logits[:, t, :]), "v"))
        with stage(nc, "dve_step") as (block, dve_step):
            @block.vector
            def _(dve):
                step = Steps(dve, dve_step)
                step(nc.vector.tensor_reduce(best[:], logits[:], AX.X, ALU.max))
                step(nc.vector.tensor_tensor(at[:], logits[:], best[:].unsqueeze(2).to_broadcast([P, NT, E]), ALU.is_equal))
                step(nc.vector.tensor_tensor(at[:], at[:], w["iota_less"].to_broadcast([P, NT, E]), ALU.mult))
                step(nc.vector.tensor_reduce(first[:], at[:], AX.X, ALU.min))
                for e in range(E):
                    step(nc.vector.tensor_scalar(chosen[:, e * NT:(e + 1) * NT], first[:], float(e - E), None, ALU.is_equal))
                step(nc.vector.memset(chosen[:, E * NT:], 1.0))

        def experts(e, n):
            with pool(nc, f"exp{nc.next_id()}") as p2:
                psA = p2.ps("psA", [P, 2, 512])
                psG = p2.ps("psG", [P, 2, 512])
                psY = p2.ps("psY", [P, NT, 512])
                with stage(nc, "chosen_ready", "loaded1", "loaded0", "inner_ready", "gelu_ready", "hidden_ready",
                           "y_ready", "y_taken") as \
                        (block, chosen_ready, loaded1, loaded0, inner_ready, gelu_ready, hidden_ready, y_ready, y_taken):
                    @block.sync
                    def _(sp):
                        if n == 2:
                            for dst, src in zip((W1[1][:], W2[1][:], W3[1][:]), sources(e + 1)):
                                sp.dma_start(dst, src).then_inc(loaded1, 16)
                            sp.wait_ge(y_ready, NT)
                            for dst, src in zip((W1[0][:], W2[0][:], W3[0][:]), sources(e + 2)):
                                sp.dma_start(dst, src).then_inc(loaded0, 16)
                            sp.wait_ge(loaded1, 48)
                            sp.wait_ge(loaded0, 48)

                    @block.tensor
                    def _(pe):
                        for i in range(n):
                            if i:
                                pe.wait_ge(loaded1, 48)
                            for f in range(FC):
                                m = i * FC + f
                                s = slice(f * P, (f + 1) * P)
                                if m >= 2:
                                    pe.wait_ge(hidden_ready, m - 1)
                                for k in range(KC):
                                    last = nc.tensor.matmul(psA[:, m % 2, :], W1[i][:, k, s], xnT[:, k, :], start=k == 0, stop=k == KC - 1)
                                last.then_inc(inner_ready, 1)
                                for k in range(KC):
                                    last = nc.tensor.matmul(psG[:, m % 2, :], W2[i][:, k, s], xnT[:, k, :], start=k == 0, stop=k == KC - 1)
                                last.then_inc(inner_ready, 1)
                            pe.wait_ge(hidden_ready, (i + 1) * FC)
                            for t in range(NT):
                                if i:
                                    pe.wait_ge(y_taken, t + 1)
                                for f in range(FC):
                                    last = nc.tensor.matmul(psY[:, t, 0:C], hT[:, f, t * P:(t + 1) * P], W3[i][:, f, :],
                                                            start=f == 0, stop=f == FC - 1)
                                last.then_inc(y_ready, 1)
                    @block.scalar
                    def _(act):
                        for m in range(n * FC):
                            act.wait_ge(inner_ready, 2 * m + 1)
                            if m >= 2:
                                act.wait_ge(hidden_ready, m - 1)
                            nc.scalar.activation(gel[:, m % 2, :], psA[:, m % 2, :], ACT.Gelu).then_inc(gelu_ready, 1)

                    @block.vector
                    def _(dve):
                        for i in range(n):
                            nc.vector.tensor_copy(here[:, i, :], chosen[:, bass.ds((e + i) * NT, NT)]).then_inc(chosen_ready, 1)
                        dve.wait_ge(chosen_ready, n)
                        for i in range(n):
                            if i:
                                dve.wait_ge(y_ready, NT)
                            for f in range(FC):
                                m = i * FC + f
                                dve.wait_ge(gelu_ready, m + 1)
                                dve.wait_ge(inner_ready, 2 * m + 2)
                                nc.vector.tensor_tensor(hT[:, f, :], psG[:, m % 2, :], gel[:, m % 2, :], ALU.mult).then_inc(hidden_ready, 1)
                            for t in range(NT):
                                dve.wait_ge(y_ready, i * NT + t + 1)
                                if i:
                                    dve.wait_ge(y_taken, t + 1)
                                nc.vector.scalar_tensor_tensor(out=X[:, t, :], in0=psY[:, t, 0:C], scalar=here[:, i, t:t + 1],
                                                               in1=X[:, t, :], op0=ALU.mult, op1=ALU.add).then_inc(y_taken, 1)

        with nc.Fori(0, E // 2) as pair:
            experts(pair * 2, 2)
        experts(E, 1)


def hyperbolic_attention(nc, K, X, arrays, specs):
    NQ = 2 * H
    with pool(nc, "l1a") as p:
        w = Weights(nc, p, "L1_attn", arrays, specs)
        gates = p.sb("gates", [P, NT, H + 1])
        spikes = p.sb("spikes", [P, NT])
        coef = p.sb("coef", [P, NT, H])
        v = p.sb("v", [P, NT, C])
        y = p.sb("y", [P, NT, C])
        turned = {n: p.sb(f"T_{n}", [P, 4, NTOK]) for n in ("qE", "kE", "qH", "kH")}
        with pool(nc, "l1b") as p1:
            xn = p1.sb("xn", [P, NT, C])
            xnT = p1.sb("xnT", [P, KC, NTOK])
            qk = p1.sb("qk", [P, NT, NQ, 16])
            qn = p1.sb("qn", [P, NT, NQ, 16])
            sq = p1.sb("sq", [P, NT, NQ, 16])
            a = p1.sb("a", [P, NT, NQ])
            m = p1.sb("m", [P, NT, NQ])
            ratio = p1.sb("ratio", [P, NT, NQ])
            time = p1.sb("time", [P, NT, NQ])
            safe = p1.sb("safe", [P, 1])
            curv = p1.sb("curv", [P, H])
            soft = p1.sb("soft", [P, H])
            expm = p1.sb("expm", [P, H])
            om = p1.sb("om", [P, NT, H])
            rows = {n: p1.sb(f"R_{n}", [P, NT, 512]) for n in ("qE", "kE", "qH", "kH")}
            normalize(nc, K, X, xn, xnT, 1e-5)
            ones = K["ones"][0:1, :]
            gemms(nc, K, project_rows(w["gates"], H + 1, xnT, lambda t: (lambda ps, step: nc.scalar.activation(gates[:, t, :], ps, ACT.Sigmoid)),
                                      "s", bias=w["bgates"], ones=ones)
                  + project_rows(w["qk"], 512, xnT, lambda t: vcopy(nc, qk[:, t, :, :].rearrange("p h d -> p (h d)")), "v", bias=w["bqk"], ones=ones)
                  + project_rows(w["v"], C, xnT, lambda t: vcopy(nc, v[:, t, :]), "v", bias=w["bv"], ones=ones))

            def over(x):
                return x.unsqueeze(3).to_broadcast([P, NT, NQ, 16])

            def by_rows(x):
                return x.rearrange("p t h d -> p (t h) d")

            def heads(n):
                return rows[n][:].rearrange("p t (h d) -> p t h d", h=H)

            with stage(nc, "dve_step", "squares_ready", "norms_ready", "space_ready", "time_ready", "act_step", "soft_ready",
                       "log_ready", "safe_ready") as \
                    (block, dve_step, squares_ready, norms_ready, space_ready, time_ready, act_step, soft_ready, log_ready,
                     safe_ready):
                @block.scalar
                def _(act):
                    nc.scalar.activation(safe[:], w["qk_scale"], ACT.Sigmoid).then_inc(safe_ready, 1)
                    nc.scalar.activation(soft[:], w["log_k"], ACT.Abs).then_inc(soft_ready, 1)
                    act.wait_ge(soft_ready, 1)
                    nc.scalar.activation(expm[:], soft[:], ACT.Exp, scale=-1.0).then_inc(act_step, 1)
                    act.wait_ge(act_step, 1)
                    nc.scalar.activation(expm[:], expm[:], ACT.Ln, bias=K["ones"][:, 0:1]).then_inc(log_ready, 1)
                    act.wait_ge(squares_ready, 1)
                    nc.scalar.activation(a[:], a[:], ACT.Sqrt).then_inc(norms_ready, 1)
                    act.wait_ge(space_ready, 1)
                    nc.scalar.activation(time[:], time[:], ACT.Sqrt, bias=K["ones"][:, 0:1]).then_inc(time_ready, 1)

                @block.vector
                def _(dve):
                    step = Steps(dve, dve_step)
                    V = nc.vector
                    for n in rows:
                        step(V.memset(rows[n][:], 0.0))
                    step(V.tensor_tensor(sq[:], qk[:], qk[:], ALU.mult))
                    V.tensor_reduce(a[:], sq[:], AX.X, ALU.add).then_inc(squares_ready, 1)
                    step(V.tensor_scalar(spikes[:], gates[:, :, H], w["threshold"], None, ALU.is_gt))
                    dve.wait_ge(log_ready, 1)
                    step(V.tensor_scalar(curv[:], w["log_k"], 0.0, None, ALU.max))
                    step(V.tensor_tensor(curv[:], curv[:], expm[:], ALU.add))
                    step(V.tensor_scalar(curv[:], curv[:], 1e-6, None, ALU.add))
                    step(V.reciprocal(curv[:], curv[:]))
                    step(V.tensor_scalar(curv[:], curv[:], -1.0, None, ALU.mult))
                    step(V.tensor_tensor(coef[:], gates[:, :, 0:H], curv[:].unsqueeze(1).to_broadcast([P, NT, H]), ALU.mult))
                    step(V.tensor_scalar(om[:], gates[:, :, 0:H], -0.25, 0.25, ALU.mult, ALU.add))
                    for t in range(NT):
                        step(V.tensor_tensor(heads("qE")[:, t, :, 0:16], qk[:, t, 0:H, :], om[:, t, :].unsqueeze(2).to_broadcast([P, H, 16]), ALU.mult))
                        step(V.tensor_copy(heads("kE")[:, t, :, 0:16], qk[:, t, H:NQ, :]))
                    dve.wait_ge(safe_ready, 1)
                    dve.wait_ge(norms_ready, 1)
                    step(V.tensor_scalar(a[:], a[:], 1e-12, None, ALU.max))
                    step(V.reciprocal(m[:], a[:]))
                    step(V.tensor_scalar(m[:], m[:], safe[:, 0:1], 1.5, ALU.mult, ALU.mult))
                    step(V.tensor_tensor(by_rows(qn[:]), by_rows(qk[:]), m[:].rearrange("p t h -> p (t h)").unsqueeze(2).to_broadcast([P, NT * NQ, 16]), ALU.mult))
                    step(V.tensor_tensor(sq[:], qn[:], qn[:], ALU.mult))
                    step(V.tensor_reduce(m[:], by_rows(sq[:])[:, :, 1:16], AX.X, ALU.add))
                    step(V.tensor_tensor(m[:].rearrange("p t h -> p (t h)"), m[:].rearrange("p t h -> p (t h)"), by_rows(sq[:])[:, :, 0], ALU.subtract))
                    step(V.tensor_scalar(m[:], m[:], 1e-8, None, ALU.max))
                    coefs = [1.0]
                    for k in range(1, 9):
                        coefs.append(coefs[-1] / (2 * k * (2 * k + 1)))
                    step(V.tensor_scalar(ratio[:], m[:], coefs[8], coefs[7], ALU.mult, ALU.add))
                    for k in range(6, -1, -1):
                        step(V.tensor_tensor(ratio[:], ratio[:], m[:], ALU.mult))
                        step(V.tensor_scalar(ratio[:], ratio[:], coefs[k], None, ALU.add))
                    step(V.tensor_tensor(by_rows(qn[:]), by_rows(qn[:]), ratio[:].rearrange("p t h -> p (t h)").unsqueeze(2).to_broadcast([P, NT * NQ, 16]), ALU.mult))
                    step(V.tensor_tensor(sq[:], qn[:], qn[:], ALU.mult))
                    V.tensor_reduce(time[:], by_rows(sq[:])[:, :, 1:16], AX.X, ALU.add).then_inc(space_ready, 1)
                    dve.wait_ge(time_ready, 1)
                    for t in range(NT):
                        step(V.tensor_copy(heads("qH")[:, t, :, 1:16], qn[:, t, 0:H, 1:16]))
                        step(V.tensor_scalar(heads("kH")[:, t, :, 1:16], qn[:, t, H:NQ, 1:16], -1.0, None, ALU.mult))
                        step(V.tensor_copy(heads("qH")[:, t, :, 0], time[:, t, 0:H]))
                        step(V.tensor_copy(heads("kH")[:, t, :, 0], time[:, t, H:NQ]))
            gemms(nc, K, [job for n in rows for job in turn_all(K, rows[n], NT, 512, lambda k, t0, n=n: vcopy(nc, turned[n][:, k, :]), "v")])
        with pool(nc, "l1c") as p1:
            A = p1.sb("A", [P, H, 512])
            R = p1.sb("R", [P, H, 512])
            top = p1.sb("top", [P, H, TB])
            tot = p1.sb("tot", [P, H, TB])
            probsT = p1.sb("probsT", [P, H, TB, T])
            for b in range(B):
                def products(q, k, evac):
                    jobs = []
                    for h in range(H):
                        r = slice(32 * (h % 4), 32 * (h % 4) + 32)
                        jobs.append((P, 512, [(turned[q][r, h // 4, (b * TB + t) * P:(b * TB + t + 1) * P],
                                               turned[k][r, h // 4, b * T:(b + 1) * T], t * 256, True, True) for t in range(TB)],
                                     evac(h), "v"))
                    return jobs

                def less_one(h):
                    def evac(ps, step):
                        step(nc.vector.tensor_scalar(A[:, h, :], ps, float(np.float32(1.0 + 1e-6)), 1.0, ALU.max, ALU.add))
                        return nc.vector.scalar_tensor_tensor(out=R[:, h, :], in0=A[:, h, :], scalar=-2.0, in1=A[:, h, :],
                                                              op0=ALU.add, op1=ALU.mult)
                    return evac

                gemms(nc, K, products("qH", "kH", less_one))
                with stage(nc, "root_ready", "sum_ready", "log_ready", "dve_step") as (block, root_ready, sum_ready, log_ready, dve_step):
                    @block.scalar
                    def _(act):
                        for i in range(4):
                            nc.scalar.activation(R[:, 4 * i:4 * i + 4, :], R[:, 4 * i:4 * i + 4, :], ACT.Sqrt).then_inc(root_ready, 1)
                        for i in range(4):
                            act.wait_ge(sum_ready, i + 1)
                            nc.scalar.activation(A[:, 4 * i:4 * i + 4, :], A[:, 4 * i:4 * i + 4, :], ACT.Ln).then_inc(log_ready, 1)

                    @block.vector
                    def _(dve):
                        for i in range(4):
                            s = slice(4 * i, 4 * i + 4)
                            dve.wait_ge(root_ready, i + 1)
                            nc.vector.scalar_tensor_tensor(out=A[:, s, :], in0=A[:, s, :], scalar=-1.0, in1=R[:, s, :],
                                                           op0=ALU.add, op1=ALU.add).then_inc(sum_ready, 1)
                        for i in range(4):
                            s = slice(4 * i, 4 * i + 4)
                            dve.wait_ge(log_ready, i + 1)
                            nc.vector.tensor_tensor(R[:, s, :], A[:, s, :], A[:, s, :], ALU.mult).then_inc(dve_step, 1)
                        dve.wait_ge(dve_step, 4)

                def mix(h):
                    def evac(ps, step):
                        for t in range(TB):
                            s = slice(t * 256, (t + 1) * 256)
                            step(nc.vector.scalar_tensor_tensor(out=A[:, h, s], in0=R[:, h, s], scalar=coef[:, b * TB + t, h:h + 1],
                                                                in1=ps[:, s], op0=ALU.mult, op1=ALU.add))
                        step(nc.vector.tensor_tensor(A[:, h, :], A[:, h, :], K["mask_q"].rearrange("p s n -> p (s n)"), ALU.add))
                        return nc.vector.tensor_reduce(top[:, h, :], A[:, h, :].rearrange("p (s n) -> p s n", s=TB), AX.X, ALU.max)
                    return evac

                gemms(nc, K, products("qE", "kE", mix))
                with stage(nc, "shifted", "exp_ready", "dve_step") as (block, shifted, exp_ready, dve_step):
                    @block.vector
                    def _(dve):
                        for i in range(4):
                            s = A[:, 4 * i:4 * i + 4, :].rearrange("p h (s n) -> p (h s) n", s=TB)
                            m = top[:, 4 * i:4 * i + 4, :].rearrange("p h s -> p (h s)").unsqueeze(2).to_broadcast([P, 4 * TB, T])
                            nc.vector.tensor_tensor(s, s, m, ALU.subtract).then_inc(shifted, 1)
                        for i in range(4):
                            dve.wait_ge(exp_ready, i + 1)
                            s = A[:, 4 * i:4 * i + 4, :].rearrange("p h (s n) -> p (h s) n", s=TB)
                            nc.vector.tensor_reduce(tot[:, 4 * i:4 * i + 4, :].rearrange("p h s -> p (h s)"), s, AX.X, ALU.add).then_inc(dve_step, 1)
                        dve.wait_ge(dve_step, 4)
                        nc.vector.reciprocal(tot[:], tot[:]).then_inc(dve_step, 1)
                        dve.wait_ge(dve_step, 5)
                        for t in range(TB):
                            nc.vector.tensor_scalar(tot[:, :, t], tot[:, :, t], spikes[:, b * TB + t:b * TB + t + 1], None, ALU.mult).then_inc(dve_step, 1)
                        dve.wait_ge(dve_step, 7)

                    @block.scalar
                    def _(act):
                        for i in range(4):
                            act.wait_ge(shifted, i + 1)
                            nc.scalar.activation(A[:, 4 * i:4 * i + 4, :], A[:, 4 * i:4 * i + 4, :], ACT.Exp).then_inc(exp_ready, 1)
                gemms(nc, K, [(P, 512, [("turn", A[:, h, t * T + kt * P:t * T + (kt + 1) * P], kt * T + t * P) for kt in range(TB) for t in range(TB)],
                               (vcopy if h % 2 else scopy)(nc, probsT[:, h, :, :].rearrange("p k q -> p (k q)")), "v" if h % 2 else "s") for h in range(H)])

                def scaled(t):
                    def evac(ps, step):
                        f = tot[:, :, t].unsqueeze(2).to_broadcast([P, H, 16])
                        return nc.vector.tensor_tensor(y[:, b * TB + t, :].rearrange("p (h d) -> p h d", h=H),
                                                       ps.rearrange("p (h d) -> p h d", h=H), f, ALU.mult)
                    return evac

                gemms(nc, K, [(P, C, [(probsT[:, h, kt, t * P:(t + 1) * P], v[:, b * TB + kt, h * 16:(h + 1) * 16], h * 16, kt == 0, kt == TB - 1)
                                      for h in range(H) for kt in range(TB)], scaled(t), "v") for t in range(TB)])
            yT = p1.sb("yT", [P, KC, NTOK])
            gemms(nc, K, turn_all(K, y, NT, C, lambda k, t0: vcopy(nc, yT[:, k, :]), "v"))
            add_to_residual(nc, K, X, w["o"], yT, KC, w["bo"])


def pooled_attention(nc, K, X, arrays, specs):
    with pool(nc, "l3x") as p:
        w = Weights(nc, p, "L3_xattn", arrays, specs)
        NKT = TB + ST
        xn = p.sb("xn", [P, NT, C])
        xnT = p.sb("xnT", [P, KC, NTOK])
        XT = p.sb("XT", [P, KC, NTOK])
        q1 = p.sb("q1", [P, KC, NTOK])
        q2 = p.sb("q2", [P, KC, NTOK])
        alpha = p.sb("alpha", [P, NT, C])
        zn = p.sb("zn", [P, NT, C])
        znT = p.sb("znT", [P, KC, NTOK])
        normalize(nc, K, X, xn, xnT, 1e-5)
        normalize(nc, K, xn, zn, znT, 1e-6, rms=True, w=w["norm_w"])
        gemms(nc, K, project_T(w["q"], C, znT, lambda m: vcopy(nc, q1[:, m, :]), "v")
              + project_rows(w["gate"], C, xnT, lambda t: (lambda ps, step: nc.scalar.activation(alpha[:, t, :], ps, ACT.Sigmoid)), "s",
                             bias=w["gate_b"], ones=K["ones"][0:1, :]))
        gemms(nc, K, project_T(w["k"], C, q1, lambda m: vcopy(nc, q2[:, m, :]), "v"))
        cx = p.sb("cx", [P, ST, C])
        cxT = p.sb("cxT", [P, KC, S])
        sc = p.sb("sc", [P, NKT * P])
        pT = p.sb("pT", [P, NKT, P])
        top = p.sb("top", [P, 1])
        tot = p.sb("tot", [P, 1])
        ht = p.sb("ht", [P, C])
        for b in range(B):
            load(nc, [(cx[:, n:n + 8, :], arrays["ctx"][b].rearrange("(p n) c -> p n c", p=P)[:, n:n + 8, :]) for n in range(0, ST, 8)])
            gemms(nc, K, [job for n in range(0, ST, 4) for job in (
                (P, 512, [("turn", cx[:, n + t, 0:P], t * P) for t in range(4)], vcopy(nc, cxT[:, 0, n * P:(n + 4) * P]), "v"),
                (P, 512, [("turn", cx[:, n + t, P:C], t * P) for t in range(4)], scopy(nc, cxT[:, 1, n * P:(n + 4) * P]), "s"))])
            for t in range(TB):
                tt = b * TB + t
                qs = slice(tt * P, (tt + 1) * P)
                jobs = [(P, T, [(q2[:, k, qs], znT[:, k, b * T:(b + 1) * T]) for k in range(KC)],
                         vadd(nc, sc[:, S:S + T], K["mask_q"][:, t, :]), "v")]
                for n in range(0, S, 512):
                    jobs.append((P, 512, [(q2[:, k, qs], cxT[:, k, n:n + 512]) for k in range(KC)],
                                 (vcopy if n % 1024 else scopy)(nc, sc[:, n:n + 512]), "v" if n % 1024 else "s"))
                gemms(nc, K, jobs)
                with stage(nc, "top_ready", "exp_ready") as (block, top_ready, exp_ready):
                    @block.vector
                    def _(dve):
                        nc.vector.tensor_reduce(top[:], sc[:], AX.X, ALU.max, negate=True).then_inc(top_ready, 1)
                        dve.wait_ge(top_ready, 1)
                        nc.vector.tensor_scalar(top[:], top[:], 1.0 / 16.0, None, ALU.mult).then_inc(top_ready, 1)
                        dve.wait_ge(exp_ready, 1)
                        nc.vector.reciprocal(tot[:], tot[:]).then_inc(top_ready, 1)
                        dve.wait_ge(top_ready, 3)

                    @block.scalar
                    def _(act):
                        act.wait_ge(top_ready, 2)
                        nc.scalar.activation(sc[:], sc[:], ACT.Exp, bias=top[:, 0:1], scale=1.0 / 16.0, accum_out=tot[:]).then_inc(exp_ready, 1)
                        act.wait_ge(exp_ready, 1)
                jobs = []
                for i, n in enumerate(range(0, NKT, 4)):
                    m = min(4, NKT - n)
                    jobs.append((P, m * P, [("turn", sc[:, (n + j) * P:(n + j + 1) * P], j * P) for j in range(m)],
                                 (vcopy if i % 2 else scopy)(nc, pT[:, n:n + m, :].rearrange("p t q -> p (t q)")), "v" if i % 2 else "s"))
                gemms(nc, K, jobs)

                def blend(ps, step, tt=tt):
                    step(nc.vector.scalar_tensor_tensor(out=ht[:], in0=ps, scalar=tot[:, 0:1], in1=xn[:, tt, :], op0=ALU.mult, op1=ALU.subtract))
                    step(nc.vector.tensor_tensor(ht[:], ht[:], alpha[:, tt, :], ALU.mult))
                    step(nc.vector.tensor_tensor(ht[:], ht[:], xn[:, tt, :], ALU.add))
                    return nc.vector.tensor_tensor(X[:, tt, :], X[:, tt, :], ht[:], ALU.add)

                gemms(nc, K, [(P, C, [(pT[:, n, :], cx[:, n, :]) for n in range(ST)]
                               + [(pT[:, ST + n, :], zn[:, b * TB + n, :]) for n in range(TB)], blend, "v")])


def state_space(nc, K, X, arrays, specs):
    DI = 2 * C
    CH = DI // P
    NS = 16
    with pool(nc, "l2s") as p:
        w = Weights(nc, p, "L2_attn", arrays, specs)
        xn = p.sb("xn", [P, NT, C])
        xnT = p.sb("xnT", [P, KC, NTOK])
        xi = p.sb("xi", [P, CH, NTOK])
        z = p.sb("z", [P, CH, NTOK])
        conv = p.sb("conv", [P, CH, NTOK])
        xs = p.sb("xs", [P, CH, NTOK])
        xp = p.sb("xp", [2 * NS + 1, NTOK])
        raw = p.sb("raw", [P, CH, NTOK])
        delta = p.sb("delta", [P, CH, NTOK])
        dx = p.sb("dx", [P, CH, NTOK])
        A = p.sb("A", [P, NS])
        yT = p.sb("yT", [P, CH, NTOK])
        normalize(nc, K, X, xn, xnT, 1e-5)
        gemms(nc, K, project_T(w["in"], DI, xnT, lambda m: vcopy(nc, xi[:, m, :]), "v")
              + project_T(w["in"][:, :, DI:], DI, xnT, lambda m: (lambda ps, step: nc.scalar.activation(z[:, m, :], ps, ACT.Silu)), "s"))
        with stage(nc, "dve_step", "conv_ready", "act_step", "act_done") as (block, dve_step, conv_ready, act_step, act_done):
            @block.vector
            def _(dve):
                step = Steps(dve, dve_step)
                for m in range(CH):
                    step(nc.vector.tensor_scalar(conv[:, m, :], xi[:, m, :], w["conv_w"][:, m, 3:4], w["conv_b"][:, m:m + 1], ALU.mult, ALU.add))
                    out, src = (x[:, m, :].rearrange("p (b t) -> p b t", b=B) for x in (conv, xi))
                    for s in range(1, 4):
                        step(nc.vector.scalar_tensor_tensor(out=out[:, :, s:T], in0=src[:, :, 0:T - s], scalar=w["conv_w"][:, m, 3 - s:4 - s],
                                                            in1=out[:, :, s:T], op0=ALU.mult, op1=ALU.add))
                dve.sem_inc(conv_ready, 1)

            @block.scalar
            def _(act):
                act.wait_ge(conv_ready, 1)
                nc.scalar.activation(xs[:], conv[:], ACT.Silu).then_inc(act_done, 1)
                nc.scalar.activation(A[:], w["A_log"], ACT.Exp).then_inc(act_done, 1)
                act.wait_ge(act_done, 2)
                nc.scalar.mul(A[:], A[:], -1.0).then_inc(act_done, 1)
                act.wait_ge(act_done, 3)
        gemms(nc, K, [(2 * NS + 1, NTOK, [(w["x"][:, m, :], xs[:, m, :]) for m in range(CH)], vcopy(nc, xp[:]), "v")])
        gemms(nc, K, [(P, NTOK, [(w["dt"][:, m * P:(m + 1) * P], xp[0:1, :])], vbias(nc, raw[:, m, :], w["b_dt"][:, m:m + 1]), "v") for m in range(CH)])
        with stage(nc, "act_step", "soft_ready", "dve_step") as (block, act_step, soft_ready, dve_step):
            @block.scalar
            def _(act):
                step = Steps(act, act_step)
                step(nc.scalar.activation(delta[:], raw[:], ACT.Abs))
                step(nc.scalar.activation(delta[:], delta[:], ACT.Exp, scale=-1.0))
                nc.scalar.activation(delta[:], delta[:], ACT.Ln, bias=K["ones"][:, 0:1]).then_inc(soft_ready, 1)

            @block.vector
            def _(dve):
                step = Steps(dve, dve_step)
                dve.wait_ge(act_step, 1)
                step(nc.vector.tensor_scalar(raw[:], raw[:], 0.0, None, ALU.max))
                dve.wait_ge(soft_ready, 1)
                step(nc.vector.tensor_tensor(delta[:], delta[:], raw[:], ALU.add))
                step(nc.vector.tensor_tensor(dx[:], delta[:], xs[:], ALU.mult))
        with pool(nc, "l2t") as p2:
            psB = p2.ps("psB", [P, 2, 512])
            psC = p2.ps("psC", [P, 2, 512])
            psY = p2.ps("psY", [P, CH, 512])
            decay = p2.sb("decay", [P, 3, NTOK])
            u = p2.sb("u", [P, 2, NTOK])
            h = p2.sb("h", [P, 2, NTOK])
            hc = p2.sb("hc", [P, 3, NTOK])
            with stage(nc, "spread", "input_ready", "decay_ready", "states_ready", "read_ready", "summed", "dve_step") as \
                    (block, spread, input_ready, decay_ready, states_ready, read_ready, summed, dve_step):
                @block.tensor
                def _(pe):
                    def spread_rows(s):
                        if s >= 2:
                            pe.wait_ge(read_ready, (s - 1) * CH)
                        n = 2 * NS + 1
                        for ps, r in ((psB, 1 + s), (psC, 1 + NS + s)):
                            last = nc.tensor.matmul(ps[:, s % 2, :], K["ident"][0:n, r:r + 1].to_broadcast([n, P]), xp[:, :], start=True, stop=True)
                        last.then_inc(spread, 1)

                    spread_rows(0)
                    for s in range(NS):
                        if s + 1 < NS:
                            spread_rows(s + 1)
                        for m in range(CH):
                            i = s * CH + m
                            pe.wait_ge(read_ready, i + 1)
                            nc.tensor.matmul(psY[:, m, :], K["ident"], hc[:, i % 3, :], start=s == 0, stop=s == NS - 1).then_inc(summed, 1)

                @block.scalar
                def _(act):
                    for i in range(NS * CH):
                        if i >= 3:
                            act.wait_ge(states_ready, 2 * (i - 2))
                        nc.scalar.activation(decay[:, i % 3, :], delta[:, i % CH, :], ACT.Exp, scale=A[:, i // CH:i // CH + 1]).then_inc(decay_ready, 1)

                @block.vector
                def _(dve):
                    N = NS * CH

                    def inputs(i):
                        s, m = i // CH, i % CH
                        dve.wait_ge(spread, s + 1)
                        if i >= 2:
                            dve.wait_ge(states_ready, 2 * (i - 1))
                        nc.vector.tensor_tensor(u[:, i % 2, :], psB[:, s % 2, :], dx[:, m, :], ALU.mult).then_inc(input_ready, 1)

                    inputs(0)
                    for i in range(N):
                        s, m = i // CH, i % CH
                        if i + 1 < N:
                            inputs(i + 1)
                        dve.wait_ge(decay_ready, i + 1)
                        dve.wait_ge(input_ready, i + 1)
                        if i >= 2:
                            dve.wait_ge(read_ready, i - 1)
                        for b in range(B):
                            c = slice(b * T, (b + 1) * T)
                            nc.vector.tensor_tensor_scan(h[:, i % 2, c], decay[:, i % 3, c], u[:, i % 2, c], 0.0, ALU.mult, ALU.add).then_inc(states_ready, 1)
                        dve.wait_ge(states_ready, 2 * (i + 1))
                        if i >= 3:
                            dve.wait_ge(summed, i - 2)
                        nc.vector.tensor_tensor(hc[:, i % 3, :], psC[:, s % 2, :], h[:, i % 2, :], ALU.mult).then_inc(read_ready, 1)
                    dve.wait_ge(summed, N)
                    step = Steps(dve, dve_step)
                    for m in range(CH):
                        step(nc.vector.scalar_tensor_tensor(out=yT[:, m, :], in0=xs[:, m, :], scalar=w["D"][:, m:m + 1], in1=psY[:, m, :],
                                                            op0=ALU.mult, op1=ALU.add))
                        step(nc.vector.tensor_tensor(yT[:, m, :], yT[:, m, :], z[:, m, :], ALU.mult))
        gemms(nc, K, project_rows(w["out"], C, yT, lambda t: vadd(nc, X[:, t, :], X[:, t, :]), "v", kc=CH))


def expert_choice(nc, K, X, arrays, specs):
    with pool(nc, "l2f") as p:
        w = Weights(nc, p, "L2_ffn", arrays, specs)
        xn = p.sb("xn", [P, NT, C])
        xnT = p.sb("xnT", [P, KC, NTOK])
        W1 = [p.sb(f"W1_{i}", [P, KC, FF]) for i in range(2)]
        W2 = [p.sb(f"W2_{i}", [P, FC, C]) for i in range(2)]
        score = p.sb("score", [P, E, NT])
        rank = p.sb("rank", [P, E * NT])
        over = p.sb("over", [P, E, NT])
        same = p.sb("same", [P, E, NT])
        scores = p.sb("scores", [P, E, NTOK])
        junk = p.sb("junk", [P, 2, NTOK])

        def sources(e):
            one = bass.ds(e, 1)
            return [arrays["M1"][one].rearrange("o (k p) n -> p (o k) n", p=P), arrays["M2"][one].rearrange("o (k p) n -> p (o k) n", p=P)]

        load(nc, list(zip((W1[0][:], W2[0][:]), sources(0))))
        normalize(nc, K, X, xn, xnT, 1e-5)
        gemms(nc, K, project_rows(w["gate"], E, xnT, lambda t: (lambda ps, step: nc.scalar.activation(score[:, :, t], ps, ACT.Sigmoid)), "s"))
        gemms(nc, K, [(P, NTOK, [("turn", score[:, e, t:t + 1].to_broadcast([P, P]), t * P) for t in range(NT)], scopy(nc, scores[:, e, :]), "s")
                      for e in range(E)])
        with stage(nc, "dve_step", "counted") as (block, dve_step, counted):
            @block.vector
            def _(dve):
                step = Steps(dve, dve_step)
                for n in range(E * NT):
                    e, t = n // NT, n % NT
                    if n:
                        dve.wait_ge(counted, 2 * n)
                    nc.vector.tensor_scalar(junk[:, 0, :], scores[:, e, :], score[:, e, t:t + 1], 0.0, ALU.is_gt, ALU.add,
                                            accum_out=over[:, e, t:t + 1]).then_inc(counted, 1)
                    nc.vector.scalar_tensor_tensor(out=junk[:, 1, :], in0=scores[:, e, :], scalar=score[:, e, t:t + 1], in1=w["before"][:, t, :],
                                                   op0=ALU.is_equal, op1=ALU.mult, accum_out=same[:, e, t:t + 1]).then_inc(counted, 1)
                dve.wait_ge(counted, 2 * E * NT)
                step(nc.vector.tensor_tensor(rank[:], over[:].rearrange("p e t -> p (e t)"), same[:].rearrange("p e t -> p (e t)"), ALU.add))
        rk = p.sb("rk", [P, 2 * NT])
        sc = p.sb("sc", [P, 2 * NT])
        b1 = p.sb("b1", [P, 2 * FC])
        b2 = p.sb("b2", [1, 2 * C])
        place = p.sb("place", [P, NT, P])
        placeT = p.sb("placeT", [P, NT, P])
        exT = p.sb("exT", [P, KC, P])
        hT = p.sb("hT", [P, FC, P])
        rows = p.sb("rows", [P, C])
        flat_score = score[:].rearrange("p e t -> p (e t)")
        with nc.Fori(0, E // 2) as pair:
            e = pair * 2
            with pool(nc, "l2e") as p2:
                psX = p2.ps("psX", [P, KC, P])
                psP = p2.ps("psP", [P, NT, P])
                psH = p2.ps("psH", [P, 2, 4, P])
                psR = p2.ps("psR", [P, C])
                psY = p2.ps("psY", [P, 2, 512])
                with stage(nc, "picked", "placed", "gathered", "turned", "gathered_copied", "turned_copied", "inner_ready",
                           "gelu_ready", "rows_ready", "rows_copied", "y_ready", "y_taken", "loaded1", "loaded0") as \
                        (block, picked, placed, gathered, turned, gathered_copied, turned_copied, inner_ready,
                         gelu_ready, rows_ready, rows_copied, y_ready, y_taken, loaded1, loaded0):
                    @block.sync
                    def _(sp):
                        for dst, src in zip((W1[1][:], W2[1][:]), sources(e + 1)):
                            sp.dma_start(dst, src).then_inc(loaded1, 16)
                        sp.wait_ge(rows_ready, 1)
                        for dst, src in zip((W1[0][:], W2[0][:]), sources(e + 2)):
                            sp.dma_start(dst, src).then_inc(loaded0, 16)
                        sp.wait_ge(loaded1, 32)
                        sp.wait_ge(loaded0, 32)

                    @block.tensor
                    def _(pe):
                        for i in range(2):
                            pe.wait_ge(placed, NT * (i + 1))
                            for k in range(KC):
                                for t in range(NT):
                                    last = nc.tensor.matmul(psX[:, k, :], xn[:, t, k * P:(k + 1) * P], place[:, t, :], start=t == 0, stop=t == NT - 1)
                            last.then_inc(gathered, 1)
                            for t in range(NT):
                                last = nc.tensor.transpose(psP[:, t, :], place[:, t, :], K["ident"])
                            last.then_inc(turned, 1)
                            pe.wait_ge(gathered_copied, i + 1)
                            if i:
                                pe.wait_ge(loaded1, 32)
                            for f in range(FC):
                                if i:
                                    pe.wait_ge(gelu_ready, f // 4 * 4 + 4)
                                for k in range(KC):
                                    last = nc.tensor.matmul(psH[:, f // 4, f % 4, :], W1[i][:, k, f * P:(f + 1) * P], exT[:, k, :], start=k == 0, stop=k == KC - 1)
                                if f % 4 == 3:
                                    last.then_inc(inner_ready, 1)
                            pe.wait_ge(gelu_ready, FC * (i + 1))
                            for f in range(FC):
                                nc.tensor.matmul(psR[:, :], hT[:, f, :], W2[i][:, f, :], start=f == 0, stop=False)
                            nc.tensor.matmul(psR[:, :], K["ones"][0:1, :], b2[0:1, i * C:(i + 1) * C], start=False, stop=True).then_inc(rows_ready, 1)
                            pe.wait_ge(rows_copied, i + 1)
                            pe.wait_ge(turned_copied, i + 1)
                            for t in range(NT):
                                if i * NT + t >= 2:
                                    pe.wait_ge(y_taken, i * NT + t - 1)
                                nc.tensor.matmul(psY[:, t % 2, 0:C], placeT[:, t, :], rows[:], start=True, stop=True).then_inc(y_ready, 1)

                    @block.scalar
                    def _(act):
                        act.wait_ge(picked, 4)
                        for i in range(2):
                            act.wait_ge(turned, i + 1)
                            if i:
                                act.wait_ge(y_ready, NT)
                            nc.scalar.copy(placeT[:], psP[:]).then_inc(turned_copied, 1)
                            for f in range(FC):
                                act.wait_ge(inner_ready, 2 * i + f // 4 + 1)
                                if i:
                                    act.wait_ge(rows_ready, i)
                                nc.scalar.activation(hT[:, f, :], psH[:, f // 4, f % 4, :], ACT.Gelu,
                                                     bias=b1[:, i * FC + f:i * FC + f + 1]).then_inc(gelu_ready, 1)

                    @block.vector
                    def _(dve):
                        nc.vector.tensor_copy(rk[:], rank[:, bass.ds(e * NT, 2 * NT)]).then_inc(picked, 1)
                        nc.vector.tensor_copy(sc[:], flat_score[:, bass.ds(e * NT, 2 * NT)]).then_inc(picked, 1)
                        nc.vector.tensor_copy(b1[:], w["b1"][:, bass.ds(e * FC, 2 * FC)]).then_inc(picked, 1)
                        nc.vector.tensor_copy(b2[:], w["b2"][:, bass.ds(e * C, 2 * C)]).then_inc(picked, 1)
                        dve.wait_ge(picked, 4)
                        for i in range(2):
                            if i:
                                dve.wait_ge(gathered, i)
                                dve.wait_ge(turned, i)
                            for t in range(NT):
                                nc.vector.tensor_scalar(place[:, t, :], w["iota"], rk[:, i * NT + t:i * NT + t + 1], None, ALU.is_equal).then_inc(placed, 1)
                            dve.wait_ge(gathered, i + 1)
                            if i:
                                dve.wait_ge(inner_ready, 2 * i)
                            nc.vector.tensor_copy(exT[:], psX[:]).then_inc(gathered_copied, 1)
                            dve.wait_ge(rows_ready, i + 1)
                            if i:
                                dve.wait_ge(y_ready, NT * i)
                            nc.vector.tensor_copy(rows[:], psR[:]).then_inc(rows_copied, 1)
                            for t in range(NT):
                                n = i * NT + t
                                dve.wait_ge(y_ready, n + 1)
                                if n >= NT:
                                    dve.wait_ge(y_taken, n - NT + 1)
                                nc.vector.scalar_tensor_tensor(out=X[:, t, :], in0=psY[:, t % 2, 0:C], scalar=sc[:, n:n + 1], in1=X[:, t, :],
                                                               op0=ALU.mult, op1=ALU.add).then_inc(y_taken, 1)


def rope_and_groups(nc, K, X, arrays, specs):
    HID = 512
    HC = HID // P
    with pool(nc, "l3f") as p:
        w = Weights(nc, p, "L3_ffn", arrays, specs)
        xn = p.sb("xn", [P, NT, C])
        s1 = p.sb("s1", [P, NT, C])
        x1 = p.sb("x1", [P, NT, C])
        x1T = p.sb("x1T", [P, KC, NTOK])
        with pool(nc, "l3g") as p1:
            xnT = p1.sb("xnT", [P, KC, NTOK])
            lowk = p1.sb("lowk", [64, 1, NTOK])
            lowv = p1.sb("lowv", [64, 1, NTOK])
            qT = p1.sb("qT", [P, 4, NTOK])
            kT = p1.sb("kT", [P, 4, NTOK])
            v = p1.sb("v", [P, NT, 512])
            attT = p1.sb("attT", [P, 4, NTOK])
            other = p1.sb("other", [P, 8, NTOK])
            normalize(nc, K, X, xn, xnT, 1e-5)
            gemms(nc, K, [(64, NTOK, [(w[n][:, k, :], xnT[:, k, :]) for k in range(KC)], vcopy(nc, dst[:, 0, :]), "v")
                          for n, dst in (("kc", lowk), ("vc", lowv))])

            def straight(dst, bias):
                def at(m):
                    def evac(ps, step):
                        if bias is None:
                            return nc.vector.tensor_tensor(dst[:, m, :], ps, w["cos"], ALU.mult)
                        step(nc.vector.tensor_tensor(dst[:, m, :], ps, w["cos"], ALU.mult))
                        return nc.vector.tensor_scalar(dst[:, m, :], dst[:, m, :], bias, None, ALU.add)
                    return evac
                return at

            def crossed(dst, base):
                def at(m):
                    def evac(ps, step):
                        step(nc.vector.tensor_tensor(other[:, base + m, :], ps, w["sin"], ALU.mult))
                        return nc.vector.tensor_tensor(dst[:, m, :], dst[:, m, :], other[:, base + m, :], ALU.add)
                    return evac
                return at

            gemms(nc, K, project_T(w["q"], 512, xnT, straight(qT, None), "v") + project_T(w["k"], 512, lowk, straight(kT, w["ones_row"]), "v", kc=1)
                  + project_T(w["qx"], 512, xnT, crossed(qT, 0), "v") + project_T(w["kx"], 512, lowk, crossed(kT, 4), "v", kc=1)
                  + project_rows(w["v"], 512, lowv, lambda t: scopy(nc, v[:, t, :]), "s", kc=1, bias=w["bv"], ones=K["ones"][0:1, :]))
            self_attend(nc, K, qT, kT, v, attT, 4, False)
            gemms(nc, K, project_rows(w["o"], C, attT, lambda t: vadd(nc, s1[:, t, :], xn[:, t, :]), "v", kc=4))
        normalize(nc, K, s1, x1, x1T, 1e-6, rms=True, w=w["norm1_w"])
        acc = p.sb("acc", [P, NT, C])
        sil = p.sb("sil", [P, 2 * HC, NTOK])
        hT = p.sb("hT", [P, 2 * HC, NTOK])
        logit = p.sb("logit", [P, NT, 2 + E])
        gate = p.sb("gate", [P, NT, E])
        gemms(nc, K, [(P, NTOK, [(w[n][:, k, m * P:(m + 1) * P], x1T[:, k, :]) for k in range(KC)],
                       (lambda ps, step, i=i, m=m: nc.scalar.activation(sil[:, i * HC + m, :], ps, ACT.Silu)), "s")
                      for i, n in enumerate(("in", "w1")) for m in range(HC)]
              + project_rows(w["gates"], 2 + E, x1T, lambda t: vcopy(nc, logit[:, t, :]), "v", bias=w["bgates"], ones=K["ones"][0:1, :]))
        gemms(nc, K, [(P, NTOK, [(w[n][:, k, HID + m * P:HID + (m + 1) * P], x1T[:, k, :]) for k in range(KC)],
                       (lambda ps, step, i=i, m=m: nc.vector.tensor_tensor(hT[:, i * HC + m, :], ps, sil[:, i * HC + m, :], ALU.mult)), "v")
                      for i, n in enumerate(("in", "w1")) for m in range(HC)])
        group_weights(nc, p, logit, gate)
        gemms(nc, K, project_rows(w["out"], C, hT, lambda t: vadd(nc, acc[:, t, :], x1[:, t, :]), "v", kc=HC)
              + [(P, C, [(hT[:, HC + k, t * P:(t + 1) * P], w["w2"][:, e * HC + k, :]) for k in range(HC)],
                  (lambda ps, step, e=e, t=t: nc.vector.scalar_tensor_tensor(out=acc[:, t, :], in0=ps, scalar=gate[:, t, e:e + 1], in1=acc[:, t, :],
                                                                            op0=ALU.mult, op1=ALU.add)), "v")
                 for e in range(E) for t in range(NT)])
        normalize(nc, K, acc, s1, None, 1e-6, rms=True, w=w["norm2_w"])
        with stage(nc, "added") as (block, added):
            @block.vector
            def _(dve):
                nc.vector.tensor_tensor(X[:], X[:], s1[:], ALU.add).then_inc(added, 1)
                dve.wait_ge(added, 1)


def group_weights(nc, p, logit, gate):
    G, EG = 2, E // 2
    names = ("gmax", "gsum", "gp", "emax", "esum", "ep", "prob", "rank", "cmp")
    shapes = ((P, NT), (P, NT), (P, NT, G), (P, NT, G), (P, NT, G), (P, NT, E), (P, NT, E), (P, NT, E), (P, NT, E))
    gmax, gsum, gp, emax, esum, ep, prob, rank, cmp = (p.sb(n, list(s)) for n, s in zip(names, shapes))
    with stage(nc, "dve_step", "shifted", "exp_ready") as (block, dve_step, shifted, exp_ready):
        @block.scalar
        def _(act):
            act.wait_ge(shifted, 2)
            nc.scalar.activation(gp[:], gp[:], ACT.Exp).then_inc(exp_ready, 1)
            nc.scalar.activation(ep[:], ep[:], ACT.Exp).then_inc(exp_ready, 1)

        @block.vector
        def _(dve):
            V = nc.vector
            step = Steps(dve, dve_step)

            def by_group(x):
                return x[:].rearrange("p t (g e) -> p (t g) e", g=G)

            def each(x, n):
                return x.unsqueeze(2).to_broadcast([P, x.shape[1], n])

            def flat(x):
                return x[:].rearrange("p t g -> p (t g)")

            step(V.tensor_reduce(gmax[:], logit[:, :, 0:G], AX.X, ALU.max))
            V.tensor_tensor(gp[:], logit[:, :, 0:G], each(gmax[:], G), ALU.subtract).then_inc(shifted, 1)
            step(V.tensor_copy(ep[:], logit[:, :, G:G + E]))
            step(V.tensor_reduce(flat(emax), by_group(ep), AX.X, ALU.max))
            V.tensor_tensor(by_group(ep), by_group(ep), each(flat(emax), EG), ALU.subtract).then_inc(shifted, 1)
            dve.wait_ge(exp_ready, 2)
            step(V.tensor_reduce(gsum[:], gp[:], AX.X, ALU.add))
            step(V.reciprocal(gsum[:], gsum[:]))
            step(V.tensor_tensor(gp[:], gp[:], each(gsum[:], G), ALU.mult))
            step(V.tensor_reduce(flat(esum), by_group(ep), AX.X, ALU.add))
            step(V.reciprocal(esum[:], esum[:]))
            step(V.tensor_tensor(by_group(prob), by_group(ep), each(flat(esum), EG), ALU.mult))
            step(V.tensor_tensor(emax[:, :, 1], gp[:, :, 1], gp[:, :, 0], ALU.is_gt))
            step(V.tensor_scalar(emax[:, :, 0], emax[:, :, 1], -1.0, 1.0, ALU.mult, ALU.add))
            step(V.tensor_tensor(gp[:], gp[:], emax[:], ALU.mult))
            step(V.tensor_tensor(by_group(prob), by_group(prob), each(flat(gp), EG), ALU.mult))
            step(V.memset(rank[:], 0.0))
            for e in range(E):
                it = prob[:, :, e:e + 1].to_broadcast([P, NT, E])
                step(V.tensor_tensor(cmp[:], it, prob[:], ALU.is_gt))
                step(V.tensor_tensor(rank[:], rank[:], cmp[:], ALU.add))
                if e + 1 < E:
                    n = E - 1 - e
                    it = prob[:, :, e:e + 1].to_broadcast([P, NT, n])
                    step(V.tensor_tensor(cmp[:, :, e + 1:], it, prob[:, :, e + 1:], ALU.is_equal))
                    step(V.tensor_tensor(rank[:, :, e + 1:], rank[:, :, e + 1:], cmp[:, :, e + 1:], ALU.add))
            step(V.tensor_scalar(rank[:], rank[:], 2.0, None, ALU.is_lt))
            step(V.tensor_tensor(gate[:], prob[:], rank[:], ALU.mult))


LAYERS = [
    ("L0_xattn", lambda nc, K, X, a, s: cross_attention(nc, K, X, a, s, "L0_xattn")),
    ("L0_attn", alibi_attention),
    ("L0_ffn", routed_geglu),
    ("L1_xattn", lambda nc, K, X, a, s: cross_attention(nc, K, X, a, s, "L1_xattn")),
    ("L1_attn", hyperbolic_attention),
    ("L1_ffn", channel_mix),
    ("L2_xattn", lora_attention),
    ("L2_attn", state_space),
    ("L2_ffn", expert_choice),
    ("L3_xattn", pooled_attention),
    ("L3_attn", complex_attention),
    ("L3_ffn", rope_and_groups),
]


def build(nc, x, out, arrays, specs, layers=None):
    with pool(nc, "top") as p:
        X = p.sb("X", [P, NT, C])
        const = Weights(nc, p, "consts", arrays, specs)
        K = {k: const[k] for k in specs["consts"]}
        K["sel"] = {32: K["sel32"], 64: K["sel64"]}
        load(nc, [(X[:, t, :], x[t // TB, (t % TB) * P:(t % TB + 1) * P, :]) for t in range(NT)])
        for name, layer in LAYERS:
            if layers is None or name in layers:
                layer(nc, K, X, arrays, specs)
        with stage(nc, "stored") as (block, stored):
            @block.sync
            def _(sp):
                for t in range(NT):
                    sp.dma_start(out[t // TB, (t % TB) * P:(t % TB + 1) * P, :], X[:, t, :]).then_inc(stored, 16)
                sp.wait_ge(stored, 16 * NT)


def chunks(w):
    k, n = w.shape
    if k <= P:
        return w.reshape(k, 1, n)
    return w.reshape(k // P, P, n).transpose(1, 0, 2)


def pad_heads(w, d=16, fill=0.0):
    lead = w.shape[:-1]
    out = np.zeros(lead + (w.shape[-1] // d, 2 * d), np.float32)
    out[..., :d] = w.reshape(lead + (-1, d))
    out[..., d] = fill
    return out.reshape(lead + (-1,))


def column(v):
    return v.reshape(-1, P).T


def row(v):
    return v.reshape(1, -1)


def swap_pairs(w):
    return w.reshape(w.shape[0], -1, 2)[:, :, ::-1].reshape(w.shape)


def rotary_tables():
    inv = (1.0 / 10000.0 ** (np.arange(0, 16, 2, dtype=np.float32) / 16)).astype(np.float32)
    ang = (np.arange(T, dtype=np.float32)[None, :] * inv[:, None]).astype(np.float32)
    cos, sin = np.zeros((2, P // 32, 32, B, T), np.float32)
    cos[:, 0:16] = np.repeat(np.cos(ang), 2, axis=0)[None, :, None, :]
    sin[:, 0:16:2] = -np.sin(ang)[None, :, None, :]
    sin[:, 1:16:2] = np.sin(ang)[None, :, None, :]
    return cos.reshape(P, NTOK), sin.reshape(P, NTOK)


def everywhere(v):
    return np.broadcast_to(v.reshape(1, -1), (P, v.size))


def constants():
    i = np.arange(P)
    q, k = np.arange(T)[:, None], np.arange(T)[None, :]
    mask_q = np.where(k <= q, 0.0, MASKED).astype(np.float32)
    return {
        "ident": np.eye(P, dtype=np.float32),
        "sel32": (i[:, None] == i[None, :] // 32 * 32 + 16).astype(np.float32),
        "sel64": (i[:, None] == i[None, :] // 64 * 64 + 32).astype(np.float32),
        "ones": np.ones((P, P), np.float32),
        "mask_q": chunks(mask_q),
        "mask_k": chunks(np.ascontiguousarray(mask_q.T)),
    }


def alibi_tables():
    slopes = np.array([2.0 ** (-8.0 / H) * (2.0 ** (-8.0 / H)) ** i for i in range(H)], np.float32)
    pos = np.tile(np.arange(T, dtype=np.float32), B)
    q = np.zeros((H, 32, NTOK), np.float32)
    k = np.zeros((H, 32, NTOK), np.float32)
    q[:, 17] = 4 * slopes[:, None]
    k[:, 17] = pos
    q[:, 18] = -4 * slopes[:, None] * pos
    k[:, 18] = 1
    return chunks(q.reshape(-1, NTOK)), chunks(k.reshape(-1, NTOK))


def layouts(i):
    q_table, k_table = alibi_tables()
    cos, sin = rotary_tables()
    zero = np.zeros
    return {
        "consts": constants(),
        "L0_attn": {
            "q": chunks(pad_heads(i["L0_attn_q_w"].T)), "k": chunks(pad_heads(i["L0_attn_k_w"].T)),
            "v": chunks(pad_heads(i["L0_attn_v_w"].T)), "o": chunks(pad_heads(i["L0_attn_o_w"]).T),
            "bq": column(pad_heads(i["L0_attn_q_b"])), "bk": column(pad_heads(i["L0_attn_k_b"], fill=1.0)),
            "bv": row(pad_heads(i["L0_attn_v_b"], fill=1.0)), "bo": row(i["L0_attn_o_b"]),
            "q_table": q_table, "k_table": k_table,
        },
        "L0_xattn": {
            "q": chunks(pad_heads(i["L0_xattn_Wq"])), "k": chunks(pad_heads(i["L0_xattn_Wk"])),
            "v": chunks(pad_heads(i["L0_xattn_Wv"])), "o": chunks(pad_heads(i["L0_xattn_Wp"].T).T),
            "bq": column(pad_heads(i["L0_xattn_bq"])), "bk": column(pad_heads(i["L0_xattn_bk"], fill=1.0)),
            "bv": row(pad_heads(i["L0_xattn_bv"], fill=1.0)), "bo": row(i["L0_xattn_bp"]),
        },
        "L1_xattn": {
            "q": chunks(pad_heads(i["L1_xattn_w_q"].T)), "k": chunks(pad_heads(i["L1_xattn_w_k"].T)),
            "v": chunks(pad_heads(i["L1_xattn_w_v"].T)), "o": chunks(pad_heads(i["L1_xattn_w_o"]).T),
            "bq": column(pad_heads(i["L1_xattn_b_q"])), "bk": column(pad_heads(i["L1_xattn_b_k"], fill=1.0)),
            "bv": row(pad_heads(i["L1_xattn_b_v"], fill=1.0)), "bo": row(i["L1_xattn_b_o"]),
        },
        "L0_ffn": {
            "gate": chunks(i["L0_ffn_Wg"]), "iota_less": np.broadcast_to(np.arange(E, dtype=np.float32) - E, (P, 1, E)),
        },
        "L1_attn": {
            "qk": chunks(i["L1_attn_Wqkv"][:2 * C].T), "v": chunks(i["L1_attn_Wqkv"][2 * C:].T), "o": chunks(i["L1_attn_Wout"].T),
            "gates": chunks(np.concatenate([i["L1_attn_Walpha"], i["L1_attn_Wimp"]]).T),
            "bqk": row(i["L1_attn_bqkv"][:2 * C]), "bv": row(i["L1_attn_bqkv"][2 * C:]), "bo": row(i["L1_attn_bout"]),
            "bgates": row(np.concatenate([i["L1_attn_balpha"], i["L1_attn_bimp"]])),
            "threshold": everywhere(i["L1_attn_spike_threshold"]), "qk_scale": everywhere(i["L1_attn_qk_scale"]),
            "log_k": everywhere(i["L1_attn_log_k"]),
        },
        "L3_xattn": {
            "q": chunks(i["L3_xattn_q_w"].T), "k": chunks(i["L3_xattn_k_w"]), "gate": chunks(i["L3_xattn_gate_w"].T),
            "gate_b": row(i["L3_xattn_gate_b"]), "norm_w": everywhere(i["L3_xattn_norm_w"]),
        },
        "L2_attn": {
            "in": chunks(i["L2_attn_W_in"]), "x": chunks(i["L2_attn_W_x"]), "out": chunks(i["L2_attn_W_out"]),
            "conv_w": chunks(i["L2_attn_conv_w"][:, 0, :]), "conv_b": column(i["L2_attn_conv_b"]), "dt": row(i["L2_attn_W_dt"]),
            "b_dt": column(i["L2_attn_b_dt"]), "A_log": everywhere(i["L2_attn_A_log"]), "D": column(i["L2_attn_D"]),
        },
        "L2_ffn": {
            "gate": chunks(i["L2_ffn_Wg"]), "iota": everywhere(np.arange(P, dtype=np.float32)),
            "before": chunks((np.arange(NTOK)[None, :] < np.arange(NTOK)[:, None]).astype(np.float32)),
            "b1": i["L2_ffn_b1"].reshape(E * FC, P).T, "b2": row(i["L2_ffn_b2"]),
        },
        "L3_ffn": {
            "q": chunks(pad_heads(i["L3_ffn_Wq"])), "qx": chunks(pad_heads(swap_pairs(i["L3_ffn_Wq"]))),
            "kc": chunks(i["L3_ffn_Wk_c"]), "vc": chunks(i["L3_ffn_Wv_c"]),
            "k": chunks(pad_heads(i["L3_ffn_Wk"])), "kx": chunks(pad_heads(swap_pairs(i["L3_ffn_Wk"]))),
            "v": chunks(pad_heads(i["L3_ffn_Wv"])), "o": chunks(pad_heads(i["L3_ffn_Wo"].T).T),
            "bv": row(pad_heads(zero(256, np.float32), fill=1.0)), "cos": cos, "sin": sin,
            "ones_row": (np.arange(P) % 32 == 16).astype(np.float32)[:, None],
            "in": chunks(i["L3_ffn_W_shared_in"]), "w1": chunks(i["L3_ffn_W1_shared"]), "out": chunks(i["L3_ffn_W_shared_out"]),
            "w2": chunks(i["L3_ffn_W2_experts"].reshape(-1, C)),
            "gates": chunks(np.concatenate([i["L3_ffn_Wg_gate"], i["L3_ffn_We_gate"]], axis=1)),
            "bgates": row(np.concatenate([i["L3_ffn_group_bias"], i["L3_ffn_expert_bias"]])),
            "norm1_w": everywhere(i["L3_ffn_norm1_w"]), "norm2_w": everywhere(i["L3_ffn_norm2_w"]),
        },
        "L1_ffn": {
            "r": chunks(i["L1_ffn_W_r"].T), "k": chunks(i["L1_ffn_W_k"].T), "v": chunks(i["L1_ffn_W_v"].T),
            "mu": np.concatenate([column(i["L1_ffn_mu_r"]), column(i["L1_ffn_mu_k"])], axis=1),
        },
        "L2_xattn": {
            "q": chunks(pad_heads(i["L2_xattn_Wq"].T)), "k": chunks(pad_heads(i["L2_xattn_Wf"][:C].T)),
            "v": chunks(pad_heads(i["L2_xattn_Wf"][C:].T)), "o": chunks(pad_heads(i["L2_xattn_Wp"]).T),
            "bq": column(pad_heads(i["L2_xattn_bq"])), "bk": column(pad_heads(i["L2_xattn_bf"][:C], fill=1.0)),
            "bv": row(pad_heads(i["L2_xattn_bf"][C:], fill=1.0)), "bo": row(i["L2_xattn_bp"]),
            "Aq": chunks(i["L2_xattn_Aq"].T), "Af": chunks(i["L2_xattn_Af"].T), "Ap": chunks(pad_heads(i["L2_xattn_Ap"]).T),
            "Bq": chunks(pad_heads(i["L2_xattn_Bq"].T)), "Bk": chunks(pad_heads(i["L2_xattn_Bf"][:C].T)),
            "Bv": chunks(pad_heads(i["L2_xattn_Bf"][C:].T)), "Bp": chunks(i["L2_xattn_Bp"].T),
        },
        "L3_attn": {
            "q": chunks(pad_heads(i["L3_attn_Wq"], 32)), "k": chunks(pad_heads(i["L3_attn_Wk"], 32)),
            "v": chunks(pad_heads(i["L3_attn_Wv"], 32)), "o": chunks(pad_heads(i["L3_attn_Wo"].T, 32).T),
            "bk": column(pad_heads(zero(512, np.float32), 32, 1.0)), "bv": row(pad_heads(zero(512, np.float32), 32, 1.0)),
        },
    }


def pack(blocks):
    n = sum(int(np.prod(b.shape[1:])) for b in blocks.values())
    packed = np.zeros((P, n), np.float32)
    at, spec = 0, {}
    for name, b in blocks.items():
        m = int(np.prod(b.shape[1:]))
        packed[:b.shape[0], at:at + m] = b.reshape(b.shape[0], m)
        spec[name] = (at, b.shape)
        at += m
    return packed, spec


def lay_out(inputs, layers=None):
    arrays, specs = {}, {}
    for name, blocks in layouts(inputs).items():
        if layers is not None and name not in layers and name != "consts":
            continue
        arrays[name], specs[name] = pack(blocks)
    arrays.update(big_arrays(inputs))
    return arrays, specs


def big_arrays(i):
    return {
        "x": i["x"], "ctx": i["ctx_1024"], "fside": i["fside_BxSxS_0"],
        "W1": np.concatenate([i["L0_ffn_W1"], i["L0_ffn_w1s"][None]]),
        "W2": np.concatenate([i["L0_ffn_W2"], i["L0_ffn_w2s"][None]]),
        "W3": np.concatenate([i["L0_ffn_W3"], i["L0_ffn_w3s"][None]]),
        "M1": np.concatenate([i["L2_ffn_W1"], i["L2_ffn_W1"][:1]]),
        "M2": np.concatenate([i["L2_ffn_W2"], i["L2_ffn_W2"][:1]]),
    }


def kernel(**inputs):
    import numpy as _np
    import concourse.bacc as _bacc
    from concourse import mybir as _mybir
    from concourse.bass_utils import run_bass_kernel_spmd as _run

    nc = _bacc.Bacc("TRN2", target_bir_lowering=False, num_devices=1)
    arrays, specs = lay_out({k: _np.asarray(v) for k, v in inputs.items()})
    aps = {n: nc.dram_tensor(f"in_{n}", a.shape, _mybir.dt.float32, kind="ExternalInput").ap() for n, a in arrays.items()}
    out = nc.dram_tensor("out_x", (B, T, C), _mybir.dt.float32, kind="ExternalOutput").ap()
    build(nc, aps["x"], out, aps, specs)
    r = _run(nc, [{f"in_{n}": _np.ascontiguousarray(a) for n, a in arrays.items()}], core_ids=[0])
    return r.results[0]["out_x"]
```

```python
from contextlib import ExitStack, contextmanager

import concourse.bass as bass
import numpy as np
from concourse import mybir

F32 = mybir.dt.float32
ACT = mybir.ActivationFunctionType
ALU = mybir.AluOpType
AX = mybir.AxisListType
P = 128
B = 2
T = 256
C = 256
H = 16
KC = C // P
NT = B * T // P
NTOK = B * T
TB = T // P
S = 4096
ST = S // P
E = 8
FF = 1024
FC = FF // P
MASKED = -1.0e30


@contextmanager
def stage(nc, *names):
    with ExitStack() as es:
        sems = [es.enter_context(nc.semaphore(n)) for n in names]
        nums = [s.num for s in sems]
        with nc.Block() as block:
            yield (block, *sems)
        nc.all_engine_barrier(sems_to_clear=range(min(nums), max(nums) + 1))


class Steps:

    def __init__(self, engine, done):
        self.engine, self.done, self.n = engine, done, 0

    def __call__(self, instruction):
        self.n += 1
        instruction.then_inc(self.done, 1)
        self.engine.wait_ge(self.done, self.n)


class Pool:

    def __init__(self, nc, es, prefix):
        self.nc, self.es, self.prefix = nc, es, prefix

    def sb(self, name, shape, dt=F32):
        return self.es.enter_context(self.nc.sbuf_tensor(f"{self.prefix}_{name}", shape, dt))

    def ps(self, name, shape, dt=F32):
        return self.es.enter_context(self.nc.psum_tensor(f"{self.prefix}_{name}", shape, dt))


@contextmanager
def pool(nc, prefix):
    with ExitStack() as es:
        yield Pool(nc, es, prefix)


def load(nc, pairs):
    with stage(nc, "loaded_sp", "loaded_act") as (block, loaded_sp, loaded_act):
        @block.sync
        def _(sp):
            for dst, src in pairs[0::2]:
                sp.dma_start(dst, src).then_inc(loaded_sp, 16)
            sp.wait_ge(loaded_sp, 16 * len(pairs[0::2]))

        @block.scalar
        def _(act):
            for dst, src in pairs[1::2]:
                act.dma_start(dst, src).then_inc(loaded_act, 16)
            if pairs[1::2]:
                act.wait_ge(loaded_act, 16 * len(pairs[1::2]))


def normalize(nc, K, X, xn, xnT, eps, rms=False, w=None):
    with pool(nc, f"nrm{nc.next_id()}") as p:
        stats = p.sb("stats", [P, NT, 6])
        mv = p.sb("mv", [P, NT, 2])
        var = p.sb("var", [P, NT])
        sd = p.sb("sd", [P, NT])
        rstd = p.sb("rstd", [P, NT])
        shift = p.sb("shift", [P, NT])
        sq = p.sb("sq", [P, C])
        psT = p.ps("psT", [P, KC, 512])
        with stage(nc, "dve_step", "var_ready", "sd_ready", "rows_ready", "turned", "stored") as \
                (block, dve_step, var_ready, sd_ready, rows_ready, turned, stored):
            @block.vector
            def _(dve):
                step = Steps(dve, dve_step)
                for t in range(NT):
                    nc.vector.bn_stats(stats[:, t, :], X[:, t, :]).then_inc(dve_step, 1)
                step.n = NT
                dve.wait_ge(dve_step, step.n)
                for t in range(NT):
                    nc.vector.bn_aggr(mv[:, t, :], stats[:, t, :]).then_inc(dve_step, 1)
                step.n += NT
                dve.wait_ge(dve_step, step.n)
                if rms:
                    step(nc.vector.tensor_tensor(shift[:], mv[:, :, 0], mv[:, :, 0], ALU.mult))
                    step(nc.vector.tensor_tensor(shift[:], shift[:], mv[:, :, 1], ALU.add))
                    nc.vector.tensor_scalar(var[:], shift[:], eps, None, ALU.add).then_inc(var_ready, 1)
                else:
                    nc.vector.tensor_scalar(var[:], mv[:, :, 1], eps, None, ALU.add).then_inc(var_ready, 1)
                dve.wait_ge(sd_ready, 1)
                step(nc.vector.reciprocal(rstd[:], sd[:]))
                for t in range(NT):
                    if rms:
                        step(nc.vector.tensor_scalar(xn[:, t, :], X[:, t, :], rstd[:, t:t + 1], None, ALU.mult))
                        nc.vector.tensor_tensor(xn[:, t, :], xn[:, t, :], w[:, :], ALU.mult).then_inc(rows_ready, 1)
                    else:
                        nc.vector.tensor_scalar(xn[:, t, :], X[:, t, :], mv[:, t, 0:1], rstd[:, t:t + 1],
                                                ALU.subtract, ALU.mult).then_inc(rows_ready, 1)
                if xnT is not None:
                    dve.wait_ge(turned, 1)
                    nc.vector.tensor_copy(xnT[:, :, :], psT[:, :, :]).then_inc(stored, 1)

            @block.scalar
            def _(act):
                act.wait_ge(var_ready, 1)
                nc.scalar.activation(sd[:], var[:], ACT.Sqrt).then_inc(sd_ready, 1)

            @block.tensor
            def _(pe):
                if xnT is None:
                    return
                for t in range(NT):
                    pe.wait_ge(rows_ready, t + 1)
                    for k in range(KC):
                        last = nc.tensor.transpose(psT[:, k, t * P:(t + 1) * P], xn[:, t, k * P:(k + 1) * P], K["ident"])
                last.then_inc(turned, 1)


def gemms(nc, K, jobs, ring=4):
    with pool(nc, f"gem{nc.next_id()}") as p:
        banks = p.ps("banks", [P, ring, 512])
        turn = [sum(1 for j in jobs[:n] if j[4] == jobs[n][4]) for n in range(len(jobs))]
        with stage(nc, "product_ready", "dve_took", "act_took", "dve_step", "act_step") as \
                (block, product_ready, dve_took, act_took, dve_step, act_step):
            took = {"v": dve_took, "s": act_took}

            def view(n):
                return banks[0:jobs[n][0], n % ring, 0:jobs[n][1]]

            @block.tensor
            def _(pe):
                for n, (_, _, terms, _, _) in enumerate(jobs):
                    if n >= ring:
                        pe.wait_ge(took[jobs[n - ring][4]], turn[n - ring] + 1)
                    for i, term in enumerate(terms):
                        if term[0] == "turn":
                            _, rows, at = term
                            last = nc.tensor.transpose(view(n)[:, at:at + rows.shape[0]], rows, K["ident"])
                        elif len(term) > 2:
                            lhsT, rhs, at, first, final = term
                            last = nc.tensor.matmul(view(n)[:, at:at + rhs.shape[1]], lhsT, rhs, start=first, stop=final)
                        else:
                            last = nc.tensor.matmul(view(n), *term, start=i == 0, stop=i == len(terms) - 1)
                    last.then_inc(product_ready, 1)

            @block.vector
            def _(dve):
                step = Steps(dve, dve_step)
                for n, job in enumerate(jobs):
                    if job[4] == "v":
                        dve.wait_ge(product_ready, n + 1)
                        job[3](view(n), step).then_inc(dve_took, 1)

            @block.scalar
            def _(act):
                step = Steps(act, act_step)
                for n, job in enumerate(jobs):
                    if job[4] == "s":
                        act.wait_ge(product_ready, n + 1)
                        job[3](view(n), step).then_inc(act_took, 1)


def vcopy(nc, dst):
    return lambda ps, step: nc.vector.tensor_copy(dst, ps)


def scopy(nc, dst):
    return lambda ps, step: nc.scalar.copy(dst, ps)


def vadd(nc, dst, other):
    return lambda ps, step: nc.vector.tensor_tensor(dst, ps, other, ALU.add)


def vbias(nc, dst, bias):
    return lambda ps, step: nc.vector.tensor_scalar(dst, ps, bias, None, ALU.add)


def sbias(nc, dst, bias):
    return lambda ps, step: nc.scalar.activation(dst, ps, ACT.Identity, bias=bias)


def project_T(W, n_out, xT, evac, engine, cols=NTOK, kc=KC):
    return [(P, cols, [(W[:, k, m * P:(m + 1) * P], xT[:, k, 0:cols]) for k in range(kc)], evac(m), engine)
            for m in range(n_out // P)]


def project_rows(W, n_out, xT, evac, engine, bias=None, tiles=NT, kc=KC, ones=None):
    extra = [(ones, bias)] if bias is not None else []
    return [(P, n_out, [(xT[:, k, t * P:(t + 1) * P], W[:, k, 0:n_out]) for k in range(kc)] + extra, evac(t), engine)
            for t in range(tiles)]


def over_heads(x, nh):
    return x.unsqueeze(1).to_broadcast([P, nh, x.shape[1]])


def attention(nc, K, groups, nh, scale, key_tiles, mask):
    HP = P // nh
    D = HP // 2
    G = len(groups)
    PAIRS = nh // 2
    CB = key_tiles // 2
    UNITS = CB * PAIRS
    SLOTS = 3
    NP = 3
    with pool(nc, f"att{nc.next_id()}") as p:
        psS = p.ps("psS", [P, SLOTS, 2, 512])
        psO = p.ps("psO", [P, 512])
        psM = p.ps("psM", [P, 512])
        parts = p.sb("parts", [P, nh, 2 * CB])
        mpads = [p.sb(f"mpad{i}", [P, TB, P]) for i in range(2)]
        qB = p.sb("qB", [P, 2, T])
        probs = p.sb("probs", [P, NP, 2, 512])
        OT = p.sb("OT", [P, T])
        rec = p.sb("rec", [P, T])
        if mask:
            mska = p.sb("mska", [P, 2, 512])
            mskb = p.sb("mskb", [P, 2, 2, 512])
        with stage(nc, "dve_step", "scores_ready", "max_taken", "masked", "max_ready", "max_turned",
                   "shifted", "probs_ready", "probs_used", "o_copied", "sums_ready", "sums_used", "out_ready") as \
                (block, dve_step, scores_ready, max_taken, masked, max_ready, max_turned,
                 shifted, probs_ready, probs_used, o_copied, sums_ready, sums_used, out_ready):
            order = [(0, 0, u) for u in range(UNITS)]
            for g in range(G):
                if g + 1 < G:
                    order += [(0, g + 1, u) for u in range(UNITS)]
                order += [(1, g, u) for u in range(UNITS)]
            place = {unit: n for n, unit in enumerate(order)}

            @block.tensor
            def _(pe):
                def free_slot(n):
                    if n >= SLOTS:
                        kind, g, u = order[n - SLOTS]
                        pe.wait_ge(probs_ready if kind else max_taken, g * UNITS + u + 1)

                def maxima(g):
                    q, k, _, _ = groups[g]
                    for u in range(UNITS):
                        n = place[0, g, u]
                        free_slot(n)
                        for i in range(2):
                            t, c = (u // PAIRS * 2 + i) // CB, (u // PAIRS * 2 + i) % CB
                            for j in range(2):
                                h = u % PAIRS * 2 + j
                                r = slice(HP * h, HP * h + HP)
                                last = nc.tensor.matmul(psS[:, n % SLOTS, j, i * 256:(i + 1) * 256],
                                                        q[r, t * P:(t + 1) * P], k[r, c * 256:(c + 1) * 256],
                                                        start=True, stop=True)
                        last.then_inc(scores_ready, 1)

                def turn_maxima(g):
                    pe.wait_ge(max_ready, g + 1)
                    if g:
                        pe.wait_ge(sums_used, g)
                    for t in range(TB):
                        last = nc.tensor.transpose(psM[:, t * P:(t + 1) * P], mpads[g % 2][:, t, :], K["ident"])
                    last.then_inc(max_turned, 1)

                def probabilities(g):
                    _, k, v, _ = groups[g]
                    pe.wait_ge(shifted, g + 1)
                    for u in range(UNITS + 1):
                        if u < UNITS:
                            n = place[1, g, u]
                            free_slot(n)
                            for i in range(2):
                                kt = u // PAIRS * 2 + i
                                for j in range(2):
                                    h = u % PAIRS * 2 + j
                                    r = slice(HP * h, HP * h + HP)
                                    last = nc.tensor.matmul(psS[:, n % SLOTS, j, i * 256:(i + 1) * 256],
                                                            k[r, kt * P:(kt + 1) * P], qB[r, g % 2, :],
                                                            start=True, stop=True)
                            last.then_inc(scores_ready, 1)
                        if u >= 1:
                            w = g * UNITS + u - 1
                            if u == 1 and g:
                                pe.wait_ge(o_copied, g)
                            pe.wait_ge(probs_ready, w + 1)
                            for i in range(2):
                                kt = (u - 1) // PAIRS * 2 + i
                                for j in range(2):
                                    h = (u - 1) % PAIRS * 2 + j
                                    last = nc.tensor.matmul(psO[HP * h:HP * h + HP, 0:T],
                                                            v(kt)[:, HP * h:HP * h + HP],
                                                            probs[:, w % NP, j, i * 256:(i + 1) * 256],
                                                            start=kt == 0, stop=kt == key_tiles - 1)
                            last.then_inc(probs_used, 1)

                def sums(g):
                    pe.wait_ge(o_copied, g + 1)
                    nc.tensor.matmul(psM[:, 0:T], K["sel"][HP], OT[:], start=True, stop=True).then_inc(sums_ready, 1)

                maxima(0)
                for g in range(G):
                    if g + 1 < G:
                        maxima(g + 1)
                    if g:
                        sums(g - 1)
                    turn_maxima(g)
                    probabilities(g)
                sums(G - 1)

            @block.vector
            def _(dve):
                step = Steps(dve, dve_step)
                for m in mpads:
                    step(nc.vector.memset(m[:], 0.0))

                def take_maxima(g):
                    for u in range(UNITS):
                        n = place[0, g, u]
                        dve.wait_ge(scores_ready, n + 1)
                        src = psS[:, n % SLOTS, :, :]
                        if mask:
                            if g or u:
                                dve.wait_ge(max_taken, g * UNITS + u)
                            step(nc.vector.tensor_tensor(mska[:], src, over_heads(K["mask_q"].rearrange("p s n -> p (s n)"), 2), ALU.add))
                            src = mska[:]
                        h, s = u % PAIRS * 2, u // PAIRS * 2
                        nc.vector.tensor_reduce(parts[:, h:h + 2, s:s + 2], src.rearrange("p j (i n) -> p j i n", i=2),
                                                AX.X, ALU.max).then_inc(max_taken, 1)
                    dve.wait_ge(max_taken, (g + 1) * UNITS)
                    if g >= 2:
                        dve.wait_ge(max_turned, g - 1)
                    for t in range(TB):
                        dst = mpads[g % 2][:, t, :].rearrange("p (h d) -> p h d", h=nh)[:, :, D]
                        last = nc.vector.tensor_reduce(dst, parts[:, :, t * CB:(t + 1) * CB], AX.X, ALU.max, negate=True)
                        if t < TB - 1:
                            step(last)
                    last.then_inc(max_ready, 1)
                    dve.wait_ge(max_ready, g + 1)

                def shift(g):
                    dve.wait_ge(max_turned, g + 1)
                    nc.vector.tensor_tensor(qB[:, g % 2, :], psM[:, 0:T], groups[g][0], ALU.add).then_inc(shifted, 1)

                def add_mask(g):
                    for u in range(UNITS):
                        n, w = place[1, g, u], g * UNITS + u
                        dve.wait_ge(scores_ready, n + 1)
                        if w >= 2:
                            dve.wait_ge(probs_ready, w - 1)
                        nc.vector.tensor_tensor(mskb[:, w % 2, :, :], psS[:, n % SLOTS, :, :],
                                                over_heads(K["mask_k"].rearrange("p s n -> p (s n)"), 2), ALU.add).then_inc(masked, 1)

                def copy_o(g):
                    dve.wait_ge(probs_used, (g + 1) * UNITS)
                    if g:
                        dve.wait_ge(out_ready, g)
                    nc.vector.tensor_copy(OT[:], psO[:, 0:T]).then_inc(o_copied, 1)

                def divide(g):
                    dve.wait_ge(sums_ready, g + 1)
                    if g:
                        dve.wait_ge(out_ready, g)
                    nc.vector.reciprocal(rec[:], psM[:, 0:T]).then_inc(sums_used, 1)
                    dve.wait_ge(sums_used, g + 1)
                    nc.vector.tensor_tensor(groups[g][3], OT[:], rec[:], ALU.mult).then_inc(out_ready, 1)

                take_maxima(0)
                for g in range(G):
                    if g + 1 < G:
                        take_maxima(g + 1)
                    if g:
                        divide(g - 1)
                    shift(g)
                    if mask:
                        add_mask(g)
                    copy_o(g)
                divide(G - 1)

            @block.scalar
            def _(act):
                for g in range(G):
                    for u in range(UNITS):
                        n, w = place[1, g, u], g * UNITS + u
                        if w >= NP:
                            act.wait_ge(probs_used, w - NP + 1)
                        if mask:
                            act.wait_ge(masked, w + 1)
                            src = mskb[:, w % 2, :, :]
                        else:
                            act.wait_ge(scores_ready, n + 1)
                            src = psS[:, n % SLOTS, :, :]
                        nc.scalar.activation(probs[:, w % NP, :, :], src, ACT.Exp, scale=scale).then_inc(probs_ready, 1)


BF16 = mybir.dt.bfloat16
Q_PARTS = (0, 0, 0, 1, 1, 2)
K_PARTS = (0, 1, 2, 0, 1, 0)
D = C // H
STACK = 6 * D
SHIFT = STACK
PLAIN_ROWS = STACK + 3


def store_parts(nc, K, jobs):
    with pool(nc, f"prt{nc.next_id()}") as p:
        RING = 4
        banks = p.ps("banks", [P, RING, 512])
        left = p.sb("left", [P, RING, 512])
        parts = p.sb("parts", [P, RING, 3, 512], BF16)
        with stage(nc, "product_ready", "first_ready", "rest_ready", "second_ready", "third_ready",
                   "stored0", "stored1", "stored2", "stored3") as \
                (block, product_ready, first_ready, rest_ready, second_ready, third_ready, *stored):
            @block.tensor
            def _(pe):
                for n, (m, w, terms, _, _) in enumerate(jobs):
                    if n >= RING:
                        pe.wait_ge(rest_ready, n - RING + 1)
                    for i, term in enumerate(terms):
                        if term[0] == "turn":
                            _, rows, at = term
                            last = nc.tensor.transpose(banks[0:m, n % RING, at:at + rows.shape[0]], rows, K["ident"])
                        else:
                            last = nc.tensor.matmul(banks[0:m, n % RING, 0:w], *term, start=i == 0, stop=i == len(terms) - 1)
                    last.then_inc(product_ready, 1)

            @block.scalar
            def _(act):
                for n, (m, w, _, bias, _) in enumerate(jobs):
                    act.wait_ge(product_ready, n + 1)
                    if n >= RING:
                        act.wait_ge(stored[n % RING], 16 * (n // RING))
                    dst, src = parts[0:m, n % RING, 0, 0:w], banks[0:m, n % RING, 0:w]
                    if bias is None:
                        nc.scalar.copy(dst, src).then_inc(first_ready, 1)
                    else:
                        nc.scalar.activation(dst, src, ACT.Identity, bias=bias).then_inc(first_ready, 1)

            @block.vector
            def _(dve):
                def third(n):
                    m, w = jobs[n][0:2]
                    dve.wait_ge(second_ready, n + 1)
                    nc.vector.tensor_tensor(parts[0:m, n % RING, 2, 0:w], left[0:m, n % RING, 0:w], parts[0:m, n % RING, 1, 0:w],
                                            ALU.subtract).then_inc(third_ready, 1)

                for n, (m, w, _, bias, _) in enumerate(jobs):
                    dve.wait_ge(first_ready, n + 1)
                    if n >= RING:
                        dve.wait_ge(third_ready, n - RING + 1)
                    dst, src, first = left[0:m, n % RING, 0:w], banks[0:m, n % RING, 0:w], parts[0:m, n % RING, 0, 0:w]
                    if bias is None:
                        nc.vector.tensor_tensor(dst, src, first, ALU.subtract).then_inc(rest_ready, 1)
                    else:
                        nc.vector.scalar_tensor_tensor(out=dst, in0=src, scalar=bias, in1=first, op0=ALU.add, op1=ALU.subtract).then_inc(rest_ready, 1)
                    if n:
                        third(n - 1)
                third(len(jobs) - 1)

            @block.gpsimd
            def _(gp):
                for n, (m, w, _, _, _) in enumerate(jobs):
                    gp.wait_ge(rest_ready, n + 1)
                    nc.gpsimd.tensor_copy(parts[0:m, n % RING, 1, 0:w], left[0:m, n % RING, 0:w]).then_inc(second_ready, 1)

            @block.sync
            def _(sp):
                for n, (m, w, _, _, dst) in enumerate(jobs):
                    sp.wait_ge(third_ready, n + 1)
                    sp.dma_start(dst, parts[0:m, n % RING, :, 0:w]).then_inc(stored[n % RING], 16)
                for i in range(min(RING, len(jobs))):
                    sp.wait_ge(stored[i], 16 * len(range(i, len(jobs), RING)))


def key_pieces(dst, scratch, h, cols):
    return [(dst[i * D:(i + 1) * D], scratch[part, h * D:(h + 1) * D, cols]) for i, part in enumerate(K_PARTS)]


def query_pieces(dst, scratch, cols):
    return [(dst[i * D:(i + 1) * D], scratch[part, :, cols].rearrange("(h d) n -> d h n", d=D)) for i, part in enumerate(Q_PARTS)]


class LongItem:
    heads = 1

    def __init__(self, n, key_tiles, q, qB, k, v):
        self.n, self.key_tiles, self.q, self.qB, self.k, self.v = n, key_tiles, q, qB, k, v
        self.full = key_tiles // 8
        self.tail = key_tiles % 8
        self.units = -(-key_tiles // 4)
        self.parts = self.full + (1 if self.tail else 0)

    def maxima(self, s):
        if s < TB * self.full:
            t, c = s // self.full, s % self.full
            q = self.q[:, t * P:(t + 1) * P]
            mms = [(i * 512, q, self.k[:, c * 1024 + i * 512:c * 1024 + (i + 1) * 512]) for i in range(2)]
            return mms, (lambda ps: ps, lambda parts: parts[:, t, c:c + 1])
        w = self.tail * P
        mms = [(t * 512, self.q[:, t * P:(t + 1) * P], self.k[:, self.full * 1024:self.full * 1024 + w]) for t in range(TB)]
        return mms, (lambda ps: ps.rearrange("p (t n) -> p t n", t=TB)[:, :, 0:w], lambda parts: parts[:, :, self.full])

    def tiles(self, s):
        return range(4 * s, min(4 * s + 4, self.key_tiles))

    def scores(self, s):
        return [(i * T, self.k[:, kt * P:(kt + 1) * P], self.qB) for i, kt in enumerate(self.tiles(s))]

    def values(self, s):
        return [(i * T, self.v(kt), kt % 4, kt < 4, kt >= self.key_tiles - 4) for i, kt in enumerate(self.tiles(s))]

    def combine(self):
        return [("comb", self.n % 4)]


class PairItem:
    heads = 2
    units = 1
    parts = 1

    def __init__(self, n, q, qB, k, v):
        self.n, self.q, self.qB2, self.k, self.v = n, q, qB, k, v
        self.qB = qB

    def maxima(self, s):
        mms = [(j * 512 + t * T, self.q[:, j * T + t * P:j * T + (t + 1) * P], self.k[:, j * T:(j + 1) * T])
               for j in range(2) for t in range(TB)]
        return mms, (lambda ps: ps.rearrange("p (i n) -> p i n", n=T), lambda parts: parts[:, :, 0])

    def scores(self, s):
        return [(j * 512 + kt * T, self.k[:, j * T + kt * P:j * T + (kt + 1) * P], self.qB2[:, j * T:(j + 1) * T])
                for j in range(2) for kt in range(TB)]

    def values(self, s):
        return [(j * 512 + kt * T, self.v(j, kt), 2 * j + kt, True, True) for j in range(2) for kt in range(TB)]

    def combine(self):
        return [(f"comb{j}", (2 * self.n + j) % 4) for j in range(2)]


def stacked_attention(nc, K, items, outs, scale, mask=False, key_loads=None, lead=2):
    N, n = len(items), items[0].units
    G = N * n
    COLS = items[0].heads * TB
    PARTS = items[0].parts
    GROUP = 4 // items[0].heads
    R = items[0].qB.shape[0]
    SLOTS, NP, MR = 3, 3, 4
    ahead = n + lead
    order = [("max", a) for a in range(min(ahead, G))]
    for g in range(G):
        if g + ahead < G:
            order.append(("max", g + ahead))
        order.append(("score", g))
    place = {unit: i for i, unit in enumerate(order)}
    with pool(nc, f"sta{nc.next_id()}") as p:
        psS = p.ps("psS", [P, SLOTS, 1024])
        psO = p.ps("psO", [P, 2, T])
        psM = p.ps("psM", [P, 512])
        parts = p.sb("parts", [P, COLS, PARTS])
        neg = p.sb("neg", [P, COLS])
        rest = p.sb("rest", [P, COLS])
        split = p.sb("split", [P, MR, COLS, 3], BF16)
        probs = p.sb("probs", [P, NP, 1024])
        OT = p.sb("OT", [P, T])
        NT4 = p.sb("NT4", [P, T])
        rec = p.sb("rec", [P, T])
        if mask:
            mska = p.sb("mska", [P, 1024])
            mskb = p.sb("mskb", [P, 2, 1024])
        with stage(nc, "dve_step", "unit_ready", "max_taken", "masked", "max_split", "max_turned", "shifted", "probs_ready",
                   "probs_used", "o_copied", "combined", "n_copied", "sums_ready", "sums_read", "out_ready",
                   "keys0", "keys1", "keys2") as \
                (block, dve_step, unit_ready, max_taken, masked, max_split, max_turned, shifted, probs_ready,
                 probs_used, o_copied, combined, n_copied, sums_ready, sums_read, out_ready, *keys):

            def group_of(h):
                return h // GROUP

            @block.sync
            def _(sp):
                if key_loads is None:
                    return
                for i in range(N):
                    if i >= 3:
                        sp.wait_ge(unit_ready, place["score", (i - 2) * n - 1] + 1)
                    for dst, src in key_loads(i):
                        sp.dma_start(dst, src).then_inc(keys[i % 3], 16)

            @block.tensor
            def _(pe):
                def free_slot(at):
                    if at >= SLOTS:
                        kind, u = order[at - SLOTS]
                        pe.wait_ge(max_taken if kind == "max" else (masked if mask else probs_ready), u + 1)

                def emit(kind, u):
                    at = place[kind, u]
                    free_slot(at)
                    item, s = items[u // n], u % n
                    mms = item.maxima(s)[0] if kind == "max" else item.scores(s)
                    for col, lhsT, rhs in mms:
                        last = nc.tensor.matmul(psS[:, at % SLOTS, col:col + rhs.shape[1]], lhsT, rhs, start=True, stop=True)
                    last.then_inc(unit_ready, 1)

                def maxima(u):
                    if key_loads is not None and u % n == 0:
                        i = u // n
                        pe.wait_ge(keys[i % 3], 16 * len(key_loads(i)) * (i // 3 + 1))
                    emit("max", u)

                def values(u):
                    pe.wait_ge(probs_ready, u + 1)
                    for col, v, group, first, final in items[u // n].values(u % n):
                        last = nc.tensor.matmul(psO[32 * group:32 * group + 32, 0, :], v, probs[:, u % NP, col:col + T],
                                                start=first, stop=final)
                    last.then_inc(probs_used, 1)

                def combine(h):
                    pe.wait_ge(o_copied, h + 1)
                    for comb, row in items[h].combine():
                        last = nc.tensor.matmul(psO[32 * row:32 * row + 32, 1, :], K[comb], OT[:], start=True, stop=True)
                    last.then_inc(combined, 1)
                    if (h + 1) % GROUP == 0:
                        g = group_of(h)
                        pe.wait_ge(n_copied, g + 1)
                        pe.wait_ge(shifted, min(h + 2 + (n == 1), N))
                        nc.tensor.matmul(psM[:, 0:T], K["sel32"], NT4[:], start=True, stop=True).then_inc(sums_ready, 1)

                def turn(h):
                    pe.wait_ge(max_split, h + 1)
                    done = group_count(h - 1)
                    if done:
                        pe.wait_ge(sums_read, done)
                    if h:
                        pe.wait_ge(shifted, h)
                    for c in range(COLS):
                        last = nc.tensor.matmul(psM[SHIFT:SHIFT + 3, c * P:(c + 1) * P], split[:, h % MR, c, :], K["ident16"], start=True, stop=True)
                    last.then_inc(max_turned, 1)

                def group_count(h):
                    last_combined = ((h + 1) * n - 2) // n - 1 if h >= 0 else -1
                    return max(0, (last_combined + 1) // GROUP)

                for u in range(min(ahead, G)):
                    maxima(u)
                turn(0)
                for g in range(G):
                    if g + ahead < G:
                        maxima(g + ahead)
                    if g % n == 0:
                        pe.wait_ge(shifted, g // n + 1)
                    emit("score", g)
                    if g >= 1:
                        h = (g - 1) // n
                        if (g - 1) % n == 0 and h:
                            combine(h - 1)
                        values(g - 1)
                    if (g + 1) % n == 0 and (g + 1) // n < N:
                        turn((g + 1) // n)
                if n == 1 and N > 1:
                    combine(N - 2)
                values(G - 1)
                combine(N - 1)

            @block.vector
            def _(dve):
                step = Steps(dve, dve_step)

                def take(u):
                    at = place["max", u]
                    dve.wait_ge(unit_ready, at + 1)
                    item = items[u // n]
                    view, into = item.maxima(u % n)[1]
                    src = psS[:, at % SLOTS, :]
                    if mask:
                        if u:
                            dve.wait_ge(max_split, u)
                        nc.vector.tensor_tensor(mska[:].rearrange("p (j n) -> p j n", j=2), src.rearrange("p (j n) -> p j n", j=2),
                                                over_heads(K["mask_q"].rearrange("p s n -> p (s n)"), 2), ALU.add).then_inc(max_taken, 1)
                        dve.wait_ge(max_taken, u + 1)
                        src = mska[:]
                        step(nc.vector.tensor_reduce(into(parts), view(src), AX.X, ALU.max))
                    else:
                        nc.vector.tensor_reduce(into(parts), view(src), AX.X, ALU.max).then_inc(max_taken, 1)
                    if (u + 1) % n == 0:
                        h = u // n
                        dve.wait_ge(max_taken, u + 1)
                        if h >= MR:
                            dve.wait_ge(max_turned, h - MR + 1)
                        m = split[:, h % MR, :, :]
                        step(nc.vector.tensor_reduce(neg[:], parts[:], AX.X, ALU.max, negate=True))
                        step(nc.vector.tensor_copy(m[:, :, 0], neg[:]))
                        step(nc.vector.tensor_tensor(rest[:], neg[:], m[:, :, 0], ALU.subtract))
                        step(nc.vector.tensor_copy(m[:, :, 1], rest[:]))
                        nc.vector.tensor_tensor(m[:, :, 2], rest[:], m[:, :, 1], ALU.subtract).then_inc(max_split, 1)

                def shift(h):
                    dve.wait_ge(max_turned, h + 1)
                    nc.vector.tensor_copy(items[h].qB[SHIFT:SHIFT + 3, :], psM[SHIFT:SHIFT + 3, 0:COLS * P]).then_inc(shifted, 1)

                def copy_o(h):
                    dve.wait_ge(probs_used, (h + 1) * n)
                    if h:
                        dve.wait_ge(combined, h)
                    nc.vector.tensor_copy(OT[:], psO[:, 0, :]).then_inc(o_copied, 1)

                def divide(h):
                    g = group_of(h)
                    dve.wait_ge(combined, h + 1)
                    if g:
                        dve.wait_ge(out_ready, g)
                    nc.vector.tensor_copy(NT4[:], psO[:, 1, :]).then_inc(n_copied, 1)
                    dve.wait_ge(sums_ready, g + 1)
                    nc.vector.reciprocal(rec[:], psM[:, 0:T]).then_inc(sums_read, 1)
                    dve.wait_ge(sums_read, g + 1)
                    dve.wait_ge(n_copied, g + 1)
                    nc.vector.tensor_tensor(outs[g], NT4[:], rec[:], ALU.mult).then_inc(out_ready, 1)

                def mask_scores(g):
                    dve.wait_ge(unit_ready, place["score", g] + 1)
                    if g >= 2:
                        dve.wait_ge(probs_ready, g - 1)
                    nc.vector.tensor_tensor(mskb[:, g % 2, :].rearrange("p (j n) -> p j n", j=2),
                                            psS[:, place["score", g] % SLOTS, :].rearrange("p (j n) -> p j n", j=2),
                                            over_heads(K["mask_k"].rearrange("p s n -> p (s n)"), 2), ALU.add).then_inc(masked, 1)

                for u in range(min(ahead, G)):
                    take(u)
                shift(0)
                for g in range(G):
                    h = (g - 1) // n
                    ends = g >= 1 and (g - 1) % n == 0 and h
                    if ends:
                        copy_o(h - 1)
                    if g + ahead < G:
                        take(g + ahead)
                    if mask:
                        mask_scores(g)
                    if ends and h % GROUP == 0:
                        divide(h - 1)
                    if (g + 1) % n == 0 and (g + 1) // n < N:
                        shift((g + 1) // n)
                if n == 1 and N > 1:
                    copy_o(N - 2)
                    if (N - 1) % GROUP == 0:
                        divide(N - 2)
                copy_o(N - 1)
                divide(N - 1)

            @block.scalar
            def _(act):
                for g in range(G):
                    if g >= NP:
                        act.wait_ge(probs_used, g - NP + 1)
                    cols = T * len(items[g // n].values(g % n))
                    if mask:
                        act.wait_ge(masked, g + 1)
                        src = mskb[:, g % 2, 0:cols]
                    else:
                        act.wait_ge(unit_ready, place["score", g] + 1)
                        src = psS[:, place["score", g] % SLOTS, 0:cols]
                    nc.scalar.activation(probs[:, g % NP, 0:cols], src, ACT.Exp, scale=scale).then_inc(probs_ready, 1)


class Weights:

    def __init__(self, nc, p, name, arrays, specs):
        self.specs = specs[name]
        n = sum(int(np.prod(shape[1:])) for _, shape in self.specs.values())
        self.tile = p.sb("weights", [P, n])
        cut = [n * i // 4 for i in range(5)]
        load(nc, [(self.tile[:, a:b], arrays[name][:, a:b]) for a, b in zip(cut, cut[1:]) if b > a])

    def __getitem__(self, key):
        at, shape = self.specs[key]
        n = int(np.prod(shape[1:]))
        view = self.tile[0:shape[0], at:at + n]
        if len(shape) == 3:
            view = view.rearrange("p (k n) -> p k n", k=shape[1])
        return view


def add_to_residual(nc, K, X, W, attT, kc, bias):
    gemms(nc, K, project_rows(W, C, attT, lambda t: vadd(nc, X[:, t, :], X[:, t, :]), "v",
                           bias=bias, kc=kc, ones=K["ones"][0:1, :]))


def alibi_attention(nc, K, X, arrays, specs):
    with pool(nc, "l0a") as p:
        w = Weights(nc, p, "L0_attn", arrays, specs)
        xn = p.sb("xn", [P, NT, C])
        xnT = p.sb("xnT", [P, KC, NTOK])
        qT = p.sb("qT", [P, 4, NTOK])
        kT = p.sb("kT", [P, 4, NTOK])
        v = p.sb("v", [P, NT, 512])
        attT = p.sb("attT", [P, 4, NTOK])
        normalize(nc, K, X, xn, xnT, 1e-5)

        def with_table(dst, bias, table):
            return lambda m: (lambda ps, step: nc.vector.scalar_tensor_tensor(
                out=dst[:, m, :], in0=ps, scalar=bias[:, m:m + 1], in1=table[:, m, :], op0=ALU.add, op1=ALU.add))

        gemms(nc, K, project_T(w["q"], 512, xnT, with_table(qT, w["bq"], w["q_table"]), "v")
              + project_T(w["k"], 512, xnT, with_table(kT, w["bk"], w["k_table"]), "v")
              + project_rows(w["v"], 512, xnT, lambda t: scopy(nc, v[:, t, :]), "s", bias=w["bv"], ones=K["ones"][0:1, :]))
        self_attend(nc, K, qT, kT, v, attT, 4, True)
        add_to_residual(nc, K, X, w["o"], attT, 4, w["bo"])


def self_attend(nc, K, qT, kT, v, attT, nh, mask, k_tokens=T):
    chunks = H // nh
    groups = []
    for b in range(B):
        for c in range(chunks):
            def values(kt, b=b, c=c):
                return v[:, b * TB + kt, c * P:(c + 1) * P]
            groups.append((qT[:, c, b * T:(b + 1) * T], kT[:, c, b * T:(b + 1) * T], values, attT[:, c, b * T:(b + 1) * T]))
    attention(nc, K, groups, nh, float(C // H) ** -0.5, TB, mask)


def turn_all(K, rows, tiles, width, evac, engine):
    return [(P, P * min(4, tiles), [("turn", rows[:, t0 + t, k * P:(k + 1) * P], t * P) for t in range(min(4, tiles))],
             evac(k, t0), engine) for t0 in range(0, tiles, 4) for k in range(width // P)]


def cross_attention(nc, K, X, arrays, specs, name):
    raw = name == "L0_xattn"
    KT = ST + (TB if raw else 0)
    scrq = nc.dram_tensor(f"{name}_queries", (3, C, NTOK), BF16, kind="Internal").ap()
    scrk = nc.dram_tensor(f"{name}_keys", (3, C, KT * P), BF16, kind="Internal").ap()
    with pool(nc, name) as p:
        w = Weights(nc, p, name, arrays, specs)
        attT = p.sb("attT", [P, 4 * NTOK])
        V = p.sb("V", [P, KT, 512])
        V4 = V[:].rearrange("p t (h d) -> p t h d", h=H)
        qA = p.sb("qA", [PLAIN_ROWS, H, T], BF16)
        qB = p.sb("qB", [PLAIN_ROWS, H, T], BF16)
        oc = p.sb("oc", [P, 4, T])
        with pool(nc, name + "q") as p1:
            xn = p1.sb("xn", [P, NT, C])
            xnT = p1.sb("xnT", [P, KC, NTOK])
            normalize(nc, K, X, xn, xnT, 1e-5)
            store_parts(nc, K, [(P, NTOK, [(w["q"][:, k, m * P:(m + 1) * P], xnT[:, k, :]) for k in range(KC)], w["bq"][:, m:m + 1],
                                 scrq[:, m * P:(m + 1) * P, :].rearrange("s p n -> p s n")) for m in range(KC)])
        with stage(nc, "cleared", "qcleared") as (block, cleared, qcleared):
            @block.vector
            def _(dve):
                nc.vector.memset(V[:], 0.0).then_inc(cleared, 1)
                dve.wait_ge(cleared, 1)
                nc.vector.memset(V4[:, :, :, D], 1.0).then_inc(cleared, 1)
                dve.wait_ge(cleared, 2)

            @block.gpsimd
            def _(gp):
                nc.gpsimd.memset(qA[SHIFT:SHIFT + 3], 0.0).then_inc(qcleared, 1)
                gp.wait_ge(qcleared, 1)
        with nc.Fori(0, B) as b:
            with pool(nc, name + "b") as p1:
                cx = p1.sb("cx", [P, ST, C])
                ctx_b = arrays["ctx"][bass.ds(b, 1)].rearrange("o (p n) c -> p (o n) c", p=P)
                loads = [(cx[:, n:n + 8, :], ctx_b[:, n:n + 8, :]) for n in range(0, ST, 8)]
                if raw:
                    side = p1.sb("side", [P, TB, C])
                    sideT = p1.sb("sideT", [P, KC, T])
                    loads.append((side[:], arrays["fside"][bass.ds(b, 1)].rearrange("o (t p) c -> p (o t) c", p=P)))
                cols = bass.ds(b * T, T)
                load(nc, loads + query_pieces(qA, scrq, cols) + query_pieces(qB, scrq, cols))

                def keys_at(k, n, m):
                    return scrk[:, k * P:(k + 1) * P, n * P:(n + m) * P].rearrange("s p n -> p s n")

                def into_values(t):
                    return lambda ps, step: nc.vector.tensor_copy(V4[:, t, :, 0:D], ps.rearrange("p (h d) -> p h d", h=H))

                ones = K["ones"][0:1, :]
                if raw:
                    gemms(nc, K, turn_all(K, side, TB, C, lambda k, t0: vcopy(nc, sideT[:, k, :]), "v"))
                    gemms(nc, K, project_rows(w["v"], C, sideT, lambda t: into_values(ST + t), "v", bias=w["bv"], tiles=TB, ones=ones))
                    with stage(nc, "by_dve", "by_act", "by_pool") as (block, by_dve, by_act, by_pool):
                        cuts = (0, ST * 3 // 8, ST * 3 // 4, ST)

                        def piece(i):
                            s = slice(cuts[i], cuts[i + 1])
                            return V4[:, s, :, 0:D], cx[:, s, :].rearrange("p t (h d) -> p t h d", h=H)

                        @block.vector
                        def _(dve):
                            nc.vector.tensor_copy(*piece(0)).then_inc(by_dve, 1)
                            dve.wait_ge(by_dve, 1)

                        @block.scalar
                        def _(act):
                            nc.scalar.copy(*piece(1)).then_inc(by_act, 1)
                            act.wait_ge(by_act, 1)

                        @block.gpsimd
                        def _(gp):
                            nc.gpsimd.tensor_copy(*piece(2)).then_inc(by_pool, 1)
                            gp.wait_ge(by_pool, 1)
                    store_parts(nc, K, [(P, 512, [("turn", cx[:, n + t, k * P:(k + 1) * P], t * P) for t in range(4)], None, keys_at(k, n, 4))
                                        for n in range(0, ST, 4) for k in range(KC)]
                                + [(P, T, [(w["k"][:, k, m * P:(m + 1) * P], sideT[:, k, :]) for k in range(KC)], w["bk"][:, m:m + 1],
                                    keys_at(m, ST, TB)) for m in range(KC)])
                else:
                    cxT = p1.sb("cxT", [P, KC, S])
                    gemms(nc, K, [job for n in range(0, ST, 4) for job in (
                        (P, 512, [("turn", cx[:, n + t, 0:P], t * P) for t in range(4)], vcopy(nc, cxT[:, 0, n * P:(n + 4) * P]), "v"),
                        (P, 512, [("turn", cx[:, n + t, P:C], t * P) for t in range(4)], scopy(nc, cxT[:, 1, n * P:(n + 4) * P]), "s"))])
                    gemms(nc, K, project_rows(w["v"], C, cxT, into_values, "v", bias=w["bv"], tiles=ST, ones=ones))
                    store_parts(nc, K, [(P, 512, [(w["k"][:, k, m * P:(m + 1) * P], cxT[:, k, n * P:(n + 4) * P]) for k in range(KC)],
                                         w["bk"][:, m:m + 1], keys_at(m, n, 4)) for n in range(0, ST, 4) for m in range(KC)])
            with pool(nc, name + "a") as p1:
                kst = [p1.sb(f"kst{i}", [PLAIN_ROWS, KT * P], BF16) for i in range(3)]
                with stage(nc, "ones_ready") as (block, ones_ready):
                    @block.gpsimd
                    def _(gp):
                        for t in kst:
                            nc.gpsimd.memset(t[SHIFT:SHIFT + 3], 1.0).then_inc(ones_ready, 1)
                        gp.wait_ge(ones_ready, 3)
                items = [LongItem(h, KT, qA[:, h, :], qB[:, h, :], kst[h % 3],
                                  lambda kt, h=h: V[:, kt, 32 * h:32 * h + 32]) for h in range(H)]
                stacked_attention(nc, K, items, [oc[:, g, :] for g in range(4)], 0.25,
                                  key_loads=lambda i: key_pieces(kst[i % 3], scrk, i, slice(0, KT * P)))
            with stage(nc, "kept") as (block, kept):
                @block.vector
                def _(dve):
                    for g in range(4):
                        nc.vector.tensor_copy(attT[:, bass.ds(b * T + g * NTOK, T)], oc[:, g, :]).then_inc(kept, 1)
                    dve.wait_ge(kept, 4)
        add_to_residual(nc, K, X, w["o"], attT[:].rearrange("p (c n) -> p c n", c=4), 4, w["bo"])


def lora_attention(nc, K, X, arrays, specs):
    with pool(nc, "l2x") as p:
        w = Weights(nc, p, "L2_xattn", arrays, specs)
        xn = p.sb("xn", [P, NT, C])
        xnT = p.sb("xnT", [P, KC, NTOK])
        side = p.sb("side", [P, NT, C])
        sideT = p.sb("sideT", [P, KC, NTOK])
        qT = p.sb("qT", [P, 4, NTOK])
        kT = p.sb("kT", [P, 4, NTOK])
        v = p.sb("v", [P, NT, 512])
        attT = p.sb("attT", [P, 4, NTOK])
        lowq = p.sb("lowq", [16, NTOK])
        lowf = p.sb("lowf", [16, NTOK])
        lowp = p.sb("lowp", [16, NTOK])
        load(nc, [(side[:, t, :], arrays["ctx"][t // TB, (t % TB) * P:(t % TB + 1) * P, :]) for t in range(NT)])
        normalize(nc, K, X, xn, xnT, 1e-5)
        gemms(nc, K, turn_all(K, side, NT, C, lambda k, t0: vcopy(nc, sideT[:, k, :]), "v"))

        def low(dst, A, xT, kc):
            return (16, NTOK, [(A[:, k, :], xT[:, k, :]) for k in range(kc)],
                    lambda ps, step: nc.scalar.mul(dst[:], ps, 1.0 / 16.0), "s")

        gemms(nc, K, [low(lowq, w["Aq"], xnT, KC), low(lowf, w["Af"], sideT, KC)])
        jobs = []
        for W, Bm, lo, xT, dst, bias in ((w["q"], w["Bq"], lowq, xnT, qT, w["bq"]), (w["k"], w["Bk"], lowf, sideT, kT, w["bk"])):
            for m in range(4):
                s = slice(m * P, (m + 1) * P)
                jobs.append((P, NTOK, [(W[:, k, s], xT[:, k, :]) for k in range(KC)] + [(Bm[:, 0, s], lo[:])],
                             vbias(nc, dst[:, m, :], bias[:, m:m + 1]), "v"))
        for t in range(NT):
            s = slice(t * P, (t + 1) * P)
            jobs.append((P, 512, [(sideT[:, k, s], w["v"][:, k, :]) for k in range(KC)]
                         + [(lowf[:, s], w["Bv"][:, 0, :]), (K["ones"][0:1, :], w["bv"])], scopy(nc, v[:, t, :]), "s"))
        gemms(nc, K, jobs)
        self_attend(nc, K, qT, kT, v, attT, 4, True)
        gemms(nc, K, [low(lowp, w["Ap"], attT, 4)])
        gemms(nc, K, [(P, C, [(attT[:, k, t * P:(t + 1) * P], w["o"][:, k, :]) for k in range(4)]
                       + [(lowp[:, t * P:(t + 1) * P], w["Bp"][:, 0, :]), (K["ones"][0:1, :], w["bo"])],
                       vadd(nc, X[:, t, :], X[:, t, :]), "v") for t in range(NT)])


def complex_attention(nc, K, X, arrays, specs):
    with pool(nc, "l3a") as p:
        w = Weights(nc, p, "L3_attn", arrays, specs)
        xn = p.sb("xn", [P, NT, C])
        xnT = p.sb("xnT", [P, KC, NTOK])
        qT = p.sb("qT", [P, 8, NTOK])
        kT = p.sb("kT", [P, 8, NTOK])
        v = p.sb("v", [P, NT, 1024])
        attT = p.sb("attT", [P, 8, NTOK])
        normalize(nc, K, X, xn, xnT, 1e-5)
        gemms(nc, K, project_T(w["q"], 1024, xnT, lambda m: vcopy(nc, qT[:, m, :]), "v")
              + project_T(w["k"], 1024, xnT, lambda m: vbias(nc, kT[:, m, :], w["bk"][:, m:m + 1]), "v")
              + [(P, 512, [(xnT[:, k, t * P:(t + 1) * P], w["v"][:, k, n * 512:(n + 1) * 512]) for k in range(KC)]
                  + [(K["ones"][0:1, :], w["bv"][:, n * 512:(n + 1) * 512])], scopy(nc, v[:, t, n * 512:(n + 1) * 512]), "s")
                 for t in range(NT) for n in range(2)])
        self_attend(nc, K, qT, kT, v, attT, 2, True)
        gemms(nc, K, project_rows(w["o"], C, attT, lambda t: vadd(nc, X[:, t, :], X[:, t, :]), "v", kc=8))


def channel_mix(nc, K, X, arrays, specs):
    with pool(nc, "l1f") as p:
        w = Weights(nc, p, "L1_ffn", arrays, specs)
        xn = p.sb("xn", [P, NT, C])
        xnT = p.sb("xnT", [P, KC, NTOK])
        prev = p.sb("prev", [P, KC, NTOK])
        xr = p.sb("xr", [P, KC, NTOK])
        xk = p.sb("xk", [P, KC, NTOK])
        om = p.sb("om", [P, 2 * KC])
        r = p.sb("r", [P, NT, C])
        relu = p.sb("relu", [P, KC, NTOK])
        k2 = p.sb("k2", [P, KC, NTOK])
        gated = p.sb("gated", [P, NT, C])
        normalize(nc, K, X, xn, xnT, 1e-5)
        with stage(nc, "dve_step") as (block, dve_step):
            @block.vector
            def _(dve):
                step = Steps(dve, dve_step)
                step(nc.vector.memset(prev[:].rearrange("p k (b t) -> p k b t", b=B)[:, :, :, 0], 0.0))
                for k in range(KC):
                    step(nc.vector.tensor_copy(prev[:, k, :].rearrange("p (b t) -> p b t", b=B)[:, :, 1:T],
                                               xnT[:, k, :].rearrange("p (b t) -> p b t", b=B)[:, :, 0:T - 1]))
                step(nc.vector.tensor_scalar(om[:], w["mu"], -1.0, 1.0, ALU.mult, ALU.add))
                for dst, at in ((xr, 0), (xk, KC)):
                    for k in range(KC):
                        step(nc.vector.tensor_scalar(dst[:, k, :], prev[:, k, :], om[:, at + k:at + k + 1], None, ALU.mult))
                        step(nc.vector.scalar_tensor_tensor(out=dst[:, k, :], in0=xnT[:, k, :], scalar=w["mu"][:, at + k:at + k + 1],
                                                            in1=dst[:, k, :], op0=ALU.mult, op1=ALU.add))

        def square(m):
            def evac(ps, step):
                step(nc.vector.tensor_scalar(relu[:, m, :], ps, 0.0, None, ALU.max))
                return nc.vector.tensor_tensor(k2[:, m, :], relu[:, m, :], relu[:, m, :], ALU.mult)
            return evac

        gemms(nc, K, project_T(w["k"], C, xk, square, "v")
              + project_rows(w["r"], C, xr, lambda t: (lambda ps, step: nc.scalar.activation(r[:, t, :], ps, ACT.Sigmoid)), "s"))

        def gate(t):
            def evac(ps, step):
                step(nc.vector.tensor_tensor(gated[:, t, :], ps, r[:, t, :], ALU.mult))
                return nc.vector.tensor_tensor(X[:, t, :], X[:, t, :], gated[:, t, :], ALU.add)
            return evac

        gemms(nc, K, project_rows(w["v"], C, k2, gate, "v"))


def routed_geglu(nc, K, X, arrays, specs):
    with pool(nc, "l0f") as p:
        w = Weights(nc, p, "L0_ffn", arrays, specs)
        xn = p.sb("xn", [P, NT, C])
        xnT = p.sb("xnT", [P, KC, NTOK])
        W1 = [p.sb(f"W1_{i}", [P, KC, FF]) for i in range(2)]
        W2 = [p.sb(f"W2_{i}", [P, KC, FF]) for i in range(2)]
        W3 = [p.sb(f"W3_{i}", [P, FC, C]) for i in range(2)]
        logits = p.sb("logits", [P, NT, E])
        best = p.sb("best", [P, NT])
        at = p.sb("at", [P, NT, E])
        first = p.sb("first", [P, NT])
        chosen = p.sb("chosen", [P, (E + 1) * NT])
        here = p.sb("here", [P, 2, NT])
        gel = p.sb("gel", [P, 2, NTOK])
        hT = p.sb("hT", [P, FC, NTOK])

        def sources(e):
            one = bass.ds(e, 1)
            return [arrays["W1"][one].rearrange("o (k p) n -> p (o k) n", p=P),
                    arrays["W2"][one].rearrange("o (k p) n -> p (o k) n", p=P),
                    arrays["W3"][one].rearrange("o (k p) n -> p (o k) n", p=P)]

        load(nc, list(zip((W1[0][:], W2[0][:], W3[0][:]), sources(0))))
        normalize(nc, K, X, xn, xnT, 1e-5)
        gemms(nc, K, project_rows(w["gate"], E, xnT, lambda t: vcopy(nc, logits[:, t, :]), "v"))
        with stage(nc, "dve_step") as (block, dve_step):
            @block.vector
            def _(dve):
                step = Steps(dve, dve_step)
                step(nc.vector.tensor_reduce(best[:], logits[:], AX.X, ALU.max))
                step(nc.vector.tensor_tensor(at[:], logits[:], best[:].unsqueeze(2).to_broadcast([P, NT, E]), ALU.is_equal))
                step(nc.vector.tensor_tensor(at[:], at[:], w["iota_less"].to_broadcast([P, NT, E]), ALU.mult))
                step(nc.vector.tensor_reduce(first[:], at[:], AX.X, ALU.min))
                for e in range(E):
                    step(nc.vector.tensor_scalar(chosen[:, e * NT:(e + 1) * NT], first[:], float(e - E), None, ALU.is_equal))
                step(nc.vector.memset(chosen[:, E * NT:], 1.0))

        def experts(e, n):
            with pool(nc, f"exp{nc.next_id()}") as p2:
                psA = p2.ps("psA", [P, 2, 512])
                psG = p2.ps("psG", [P, 2, 512])
                psY = p2.ps("psY", [P, NT, 512])
                with stage(nc, "chosen_ready", "loaded1", "loaded0", "inner_ready", "gelu_ready", "hidden_ready",
                           "y_ready", "y_taken") as \
                        (block, chosen_ready, loaded1, loaded0, inner_ready, gelu_ready, hidden_ready, y_ready, y_taken):
                    @block.sync
                    def _(sp):
                        if n == 2:
                            for dst, src in zip((W1[1][:], W2[1][:], W3[1][:]), sources(e + 1)):
                                sp.dma_start(dst, src).then_inc(loaded1, 16)
                            sp.wait_ge(y_ready, NT)
                            for dst, src in zip((W1[0][:], W2[0][:], W3[0][:]), sources(e + 2)):
                                sp.dma_start(dst, src).then_inc(loaded0, 16)
                            sp.wait_ge(loaded1, 48)
                            sp.wait_ge(loaded0, 48)

                    @block.tensor
                    def _(pe):
                        for i in range(n):
                            if i:
                                pe.wait_ge(loaded1, 48)
                            for f in range(FC):
                                m = i * FC + f
                                s = slice(f * P, (f + 1) * P)
                                if m >= 2:
                                    pe.wait_ge(hidden_ready, m - 1)
                                for k in range(KC):
                                    last = nc.tensor.matmul(psA[:, m % 2, :], W1[i][:, k, s], xnT[:, k, :], start=k == 0, stop=k == KC - 1)
                                last.then_inc(inner_ready, 1)
                                for k in range(KC):
                                    last = nc.tensor.matmul(psG[:, m % 2, :], W2[i][:, k, s], xnT[:, k, :], start=k == 0, stop=k == KC - 1)
                                last.then_inc(inner_ready, 1)
                            pe.wait_ge(hidden_ready, (i + 1) * FC)
                            for t in range(NT):
                                if i:
                                    pe.wait_ge(y_taken, t + 1)
                                for f in range(FC):
                                    last = nc.tensor.matmul(psY[:, t, 0:C], hT[:, f, t * P:(t + 1) * P], W3[i][:, f, :],
                                                            start=f == 0, stop=f == FC - 1)
                                last.then_inc(y_ready, 1)
                    @block.scalar
                    def _(act):
                        for m in range(n * FC):
                            act.wait_ge(inner_ready, 2 * m + 1)
                            if m >= 2:
                                act.wait_ge(hidden_ready, m - 1)
                            nc.scalar.activation(gel[:, m % 2, :], psA[:, m % 2, :], ACT.Gelu).then_inc(gelu_ready, 1)

                    @block.vector
                    def _(dve):
                        for i in range(n):
                            nc.vector.tensor_copy(here[:, i, :], chosen[:, bass.ds((e + i) * NT, NT)]).then_inc(chosen_ready, 1)
                        dve.wait_ge(chosen_ready, n)
                        for i in range(n):
                            if i:
                                dve.wait_ge(y_ready, NT)
                            for f in range(FC):
                                m = i * FC + f
                                dve.wait_ge(gelu_ready, m + 1)
                                dve.wait_ge(inner_ready, 2 * m + 2)
                                nc.vector.tensor_tensor(hT[:, f, :], psG[:, m % 2, :], gel[:, m % 2, :], ALU.mult).then_inc(hidden_ready, 1)
                            for t in range(NT):
                                dve.wait_ge(y_ready, i * NT + t + 1)
                                if i:
                                    dve.wait_ge(y_taken, t + 1)
                                nc.vector.scalar_tensor_tensor(out=X[:, t, :], in0=psY[:, t, 0:C], scalar=here[:, i, t:t + 1],
                                                               in1=X[:, t, :], op0=ALU.mult, op1=ALU.add).then_inc(y_taken, 1)

        with nc.Fori(0, E // 2) as pair:
            experts(pair * 2, 2)
        experts(E, 1)


def hyperbolic_attention(nc, K, X, arrays, specs):
    NQ = 2 * H
    with pool(nc, "l1a") as p:
        w = Weights(nc, p, "L1_attn", arrays, specs)
        gates = p.sb("gates", [P, NT, H + 1])
        spikes = p.sb("spikes", [P, NT])
        coef = p.sb("coef", [P, NT, H])
        v = p.sb("v", [P, NT, C])
        y = p.sb("y", [P, NT, C])
        turned = {n: p.sb(f"T_{n}", [P, 4, NTOK]) for n in ("qE", "kE", "qH", "kH")}
        with pool(nc, "l1b") as p1:
            xn = p1.sb("xn", [P, NT, C])
            xnT = p1.sb("xnT", [P, KC, NTOK])
            qk = p1.sb("qk", [P, NT, NQ, 16])
            qn = p1.sb("qn", [P, NT, NQ, 16])
            sq = p1.sb("sq", [P, NT, NQ, 16])
            a = p1.sb("a", [P, NT, NQ])
            m = p1.sb("m", [P, NT, NQ])
            ratio = p1.sb("ratio", [P, NT, NQ])
            time = p1.sb("time", [P, NT, NQ])
            safe = p1.sb("safe", [P, 1])
            curv = p1.sb("curv", [P, H])
            soft = p1.sb("soft", [P, H])
            expm = p1.sb("expm", [P, H])
            om = p1.sb("om", [P, NT, H])
            rows = {n: p1.sb(f"R_{n}", [P, NT, 512]) for n in ("qE", "kE", "qH", "kH")}
            normalize(nc, K, X, xn, xnT, 1e-5)
            ones = K["ones"][0:1, :]
            gemms(nc, K, project_rows(w["gates"], H + 1, xnT, lambda t: (lambda ps, step: nc.scalar.activation(gates[:, t, :], ps, ACT.Sigmoid)),
                                      "s", bias=w["bgates"], ones=ones)
                  + project_rows(w["qk"], 512, xnT, lambda t: vcopy(nc, qk[:, t, :, :].rearrange("p h d -> p (h d)")), "v", bias=w["bqk"], ones=ones)
                  + project_rows(w["v"], C, xnT, lambda t: vcopy(nc, v[:, t, :]), "v", bias=w["bv"], ones=ones))

            def over(x):
                return x.unsqueeze(3).to_broadcast([P, NT, NQ, 16])

            def by_rows(x):
                return x.rearrange("p t h d -> p (t h) d")

            def heads(n):
                return rows[n][:].rearrange("p t (h d) -> p t h d", h=H)

            with stage(nc, "dve_step", "squares_ready", "norms_ready", "space_ready", "time_ready", "act_step", "soft_ready",
                       "log_ready", "safe_ready") as \
                    (block, dve_step, squares_ready, norms_ready, space_ready, time_ready, act_step, soft_ready, log_ready,
                     safe_ready):
                @block.scalar
                def _(act):
                    nc.scalar.activation(safe[:], w["qk_scale"], ACT.Sigmoid).then_inc(safe_ready, 1)
                    nc.scalar.activation(soft[:], w["log_k"], ACT.Abs).then_inc(soft_ready, 1)
                    act.wait_ge(soft_ready, 1)
                    nc.scalar.activation(expm[:], soft[:], ACT.Exp, scale=-1.0).then_inc(act_step, 1)
                    act.wait_ge(act_step, 1)
                    nc.scalar.activation(expm[:], expm[:], ACT.Ln, bias=K["ones"][:, 0:1]).then_inc(log_ready, 1)
                    act.wait_ge(squares_ready, 1)
                    nc.scalar.activation(a[:], a[:], ACT.Sqrt).then_inc(norms_ready, 1)
                    act.wait_ge(space_ready, 1)
                    nc.scalar.activation(time[:], time[:], ACT.Sqrt, bias=K["ones"][:, 0:1]).then_inc(time_ready, 1)

                @block.vector
                def _(dve):
                    step = Steps(dve, dve_step)
                    V = nc.vector
                    for n in rows:
                        step(V.memset(rows[n][:], 0.0))
                    step(V.tensor_tensor(sq[:], qk[:], qk[:], ALU.mult))
                    V.tensor_reduce(a[:], sq[:], AX.X, ALU.add).then_inc(squares_ready, 1)
                    step(V.tensor_scalar(spikes[:], gates[:, :, H], w["threshold"], None, ALU.is_gt))
                    dve.wait_ge(log_ready, 1)
                    step(V.tensor_scalar(curv[:], w["log_k"], 0.0, None, ALU.max))
                    step(V.tensor_tensor(curv[:], curv[:], expm[:], ALU.add))
                    step(V.tensor_scalar(curv[:], curv[:], 1e-6, None, ALU.add))
                    step(V.reciprocal(curv[:], curv[:]))
                    step(V.tensor_scalar(curv[:], curv[:], -1.0, None, ALU.mult))
                    step(V.tensor_tensor(coef[:], gates[:, :, 0:H], curv[:].unsqueeze(1).to_broadcast([P, NT, H]), ALU.mult))
                    step(V.tensor_scalar(om[:], gates[:, :, 0:H], -0.25, 0.25, ALU.mult, ALU.add))
                    for t in range(NT):
                        step(V.tensor_tensor(heads("qE")[:, t, :, 0:16], qk[:, t, 0:H, :], om[:, t, :].unsqueeze(2).to_broadcast([P, H, 16]), ALU.mult))
                        step(V.tensor_copy(heads("kE")[:, t, :, 0:16], qk[:, t, H:NQ, :]))
                    dve.wait_ge(safe_ready, 1)
                    dve.wait_ge(norms_ready, 1)
                    step(V.tensor_scalar(a[:], a[:], 1e-12, None, ALU.max))
                    step(V.reciprocal(m[:], a[:]))
                    step(V.tensor_scalar(m[:], m[:], safe[:, 0:1], 1.5, ALU.mult, ALU.mult))
                    step(V.tensor_tensor(by_rows(qn[:]), by_rows(qk[:]), m[:].rearrange("p t h -> p (t h)").unsqueeze(2).to_broadcast([P, NT * NQ, 16]), ALU.mult))
                    step(V.tensor_tensor(sq[:], qn[:], qn[:], ALU.mult))
                    step(V.tensor_reduce(m[:], by_rows(sq[:])[:, :, 1:16], AX.X, ALU.add))
                    step(V.tensor_tensor(m[:].rearrange("p t h -> p (t h)"), m[:].rearrange("p t h -> p (t h)"), by_rows(sq[:])[:, :, 0], ALU.subtract))
                    step(V.tensor_scalar(m[:], m[:], 1e-8, None, ALU.max))
                    coefs = [1.0]
                    for k in range(1, 9):
                        coefs.append(coefs[-1] / (2 * k * (2 * k + 1)))
                    step(V.tensor_scalar(ratio[:], m[:], coefs[8], coefs[7], ALU.mult, ALU.add))
                    for k in range(6, -1, -1):
                        step(V.tensor_tensor(ratio[:], ratio[:], m[:], ALU.mult))
                        step(V.tensor_scalar(ratio[:], ratio[:], coefs[k], None, ALU.add))
                    step(V.tensor_tensor(by_rows(qn[:]), by_rows(qn[:]), ratio[:].rearrange("p t h -> p (t h)").unsqueeze(2).to_broadcast([P, NT * NQ, 16]), ALU.mult))
                    step(V.tensor_tensor(sq[:], qn[:], qn[:], ALU.mult))
                    V.tensor_reduce(time[:], by_rows(sq[:])[:, :, 1:16], AX.X, ALU.add).then_inc(space_ready, 1)
                    dve.wait_ge(time_ready, 1)
                    for t in range(NT):
                        step(V.tensor_copy(heads("qH")[:, t, :, 1:16], qn[:, t, 0:H, 1:16]))
                        step(V.tensor_scalar(heads("kH")[:, t, :, 1:16], qn[:, t, H:NQ, 1:16], -1.0, None, ALU.mult))
                        step(V.tensor_copy(heads("qH")[:, t, :, 0], time[:, t, 0:H]))
                        step(V.tensor_copy(heads("kH")[:, t, :, 0], time[:, t, H:NQ]))
            gemms(nc, K, [job for n in rows for job in turn_all(K, rows[n], NT, 512, lambda k, t0, n=n: vcopy(nc, turned[n][:, k, :]), "v")])
        with pool(nc, "l1c") as p1:
            A = p1.sb("A", [P, H, 512])
            R = p1.sb("R", [P, H, 512])
            top = p1.sb("top", [P, H, TB])
            tot = p1.sb("tot", [P, H, TB])
            probsT = p1.sb("probsT", [P, H, TB, T])
            for b in range(B):
                def products(q, k, evac):
                    jobs = []
                    for h in range(H):
                        r = slice(32 * (h % 4), 32 * (h % 4) + 32)
                        jobs.append((P, 512, [(turned[q][r, h // 4, (b * TB + t) * P:(b * TB + t + 1) * P],
                                               turned[k][r, h // 4, b * T:(b + 1) * T], t * 256, True, True) for t in range(TB)],
                                     evac(h), "v"))
                    return jobs

                def less_one(h):
                    def evac(ps, step):
                        step(nc.vector.tensor_scalar(A[:, h, :], ps, float(np.float32(1.0 + 1e-6)), 1.0, ALU.max, ALU.add))
                        return nc.vector.scalar_tensor_tensor(out=R[:, h, :], in0=A[:, h, :], scalar=-2.0, in1=A[:, h, :],
                                                              op0=ALU.add, op1=ALU.mult)
                    return evac

                gemms(nc, K, products("qH", "kH", less_one))
                with stage(nc, "root_ready", "sum_ready", "log_ready", "dve_step") as (block, root_ready, sum_ready, log_ready, dve_step):
                    @block.scalar
                    def _(act):
                        for i in range(4):
                            nc.scalar.activation(R[:, 4 * i:4 * i + 4, :], R[:, 4 * i:4 * i + 4, :], ACT.Sqrt).then_inc(root_ready, 1)
                        for i in range(4):
                            act.wait_ge(sum_ready, i + 1)
                            nc.scalar.activation(A[:, 4 * i:4 * i + 4, :], A[:, 4 * i:4 * i + 4, :], ACT.Ln).then_inc(log_ready, 1)

                    @block.vector
                    def _(dve):
                        for i in range(4):
                            s = slice(4 * i, 4 * i + 4)
                            dve.wait_ge(root_ready, i + 1)
                            nc.vector.scalar_tensor_tensor(out=A[:, s, :], in0=A[:, s, :], scalar=-1.0, in1=R[:, s, :],
                                                           op0=ALU.add, op1=ALU.add).then_inc(sum_ready, 1)
                        for i in range(4):
                            s = slice(4 * i, 4 * i + 4)
                            dve.wait_ge(log_ready, i + 1)
                            nc.vector.tensor_tensor(R[:, s, :], A[:, s, :], A[:, s, :], ALU.mult).then_inc(dve_step, 1)
                        dve.wait_ge(dve_step, 4)

                def mix(h):
                    def evac(ps, step):
                        for t in range(TB):
                            s = slice(t * 256, (t + 1) * 256)
                            step(nc.vector.scalar_tensor_tensor(out=A[:, h, s], in0=R[:, h, s], scalar=coef[:, b * TB + t, h:h + 1],
                                                                in1=ps[:, s], op0=ALU.mult, op1=ALU.add))
                        step(nc.vector.tensor_tensor(A[:, h, :], A[:, h, :], K["mask_q"].rearrange("p s n -> p (s n)"), ALU.add))
                        return nc.vector.tensor_reduce(top[:, h, :], A[:, h, :].rearrange("p (s n) -> p s n", s=TB), AX.X, ALU.max)
                    return evac

                gemms(nc, K, products("qE", "kE", mix))
                with stage(nc, "shifted", "exp_ready", "dve_step") as (block, shifted, exp_ready, dve_step):
                    @block.vector
                    def _(dve):
                        for i in range(4):
                            s = A[:, 4 * i:4 * i + 4, :].rearrange("p h (s n) -> p (h s) n", s=TB)
                            m = top[:, 4 * i:4 * i + 4, :].rearrange("p h s -> p (h s)").unsqueeze(2).to_broadcast([P, 4 * TB, T])
                            nc.vector.tensor_tensor(s, s, m, ALU.subtract).then_inc(shifted, 1)
                        for i in range(4):
                            dve.wait_ge(exp_ready, i + 1)
                            s = A[:, 4 * i:4 * i + 4, :].rearrange("p h (s n) -> p (h s) n", s=TB)
                            nc.vector.tensor_reduce(tot[:, 4 * i:4 * i + 4, :].rearrange("p h s -> p (h s)"), s, AX.X, ALU.add).then_inc(dve_step, 1)
                        dve.wait_ge(dve_step, 4)
                        nc.vector.reciprocal(tot[:], tot[:]).then_inc(dve_step, 1)
                        dve.wait_ge(dve_step, 5)
                        for t in range(TB):
                            nc.vector.tensor_scalar(tot[:, :, t], tot[:, :, t], spikes[:, b * TB + t:b * TB + t + 1], None, ALU.mult).then_inc(dve_step, 1)
                        dve.wait_ge(dve_step, 7)

                    @block.scalar
                    def _(act):
                        for i in range(4):
                            act.wait_ge(shifted, i + 1)
                            nc.scalar.activation(A[:, 4 * i:4 * i + 4, :], A[:, 4 * i:4 * i + 4, :], ACT.Exp).then_inc(exp_ready, 1)
                gemms(nc, K, [(P, 512, [("turn", A[:, h, t * T + kt * P:t * T + (kt + 1) * P], kt * T + t * P) for kt in range(TB) for t in range(TB)],
                               (vcopy if h % 2 else scopy)(nc, probsT[:, h, :, :].rearrange("p k q -> p (k q)")), "v" if h % 2 else "s") for h in range(H)])

                def scaled(t):
                    def evac(ps, step):
                        f = tot[:, :, t].unsqueeze(2).to_broadcast([P, H, 16])
                        return nc.vector.tensor_tensor(y[:, b * TB + t, :].rearrange("p (h d) -> p h d", h=H),
                                                       ps.rearrange("p (h d) -> p h d", h=H), f, ALU.mult)
                    return evac

                gemms(nc, K, [(P, C, [(probsT[:, h, kt, t * P:(t + 1) * P], v[:, b * TB + kt, h * 16:(h + 1) * 16], h * 16, kt == 0, kt == TB - 1)
                                      for h in range(H) for kt in range(TB)], scaled(t), "v") for t in range(TB)])
            yT = p1.sb("yT", [P, KC, NTOK])
            gemms(nc, K, turn_all(K, y, NT, C, lambda k, t0: vcopy(nc, yT[:, k, :]), "v"))
            add_to_residual(nc, K, X, w["o"], yT, KC, w["bo"])


def pooled_attention(nc, K, X, arrays, specs):
    with pool(nc, "l3x") as p:
        w = Weights(nc, p, "L3_xattn", arrays, specs)
        NKT = TB + ST
        xn = p.sb("xn", [P, NT, C])
        xnT = p.sb("xnT", [P, KC, NTOK])
        XT = p.sb("XT", [P, KC, NTOK])
        q1 = p.sb("q1", [P, KC, NTOK])
        q2 = p.sb("q2", [P, KC, NTOK])
        alpha = p.sb("alpha", [P, NT, C])
        zn = p.sb("zn", [P, NT, C])
        znT = p.sb("znT", [P, KC, NTOK])
        normalize(nc, K, X, xn, xnT, 1e-5)
        normalize(nc, K, xn, zn, znT, 1e-6, rms=True, w=w["norm_w"])
        gemms(nc, K, project_T(w["q"], C, znT, lambda m: vcopy(nc, q1[:, m, :]), "v")
              + project_rows(w["gate"], C, xnT, lambda t: (lambda ps, step: nc.scalar.activation(alpha[:, t, :], ps, ACT.Sigmoid)), "s",
                             bias=w["gate_b"], ones=K["ones"][0:1, :]))
        gemms(nc, K, project_T(w["k"], C, q1, lambda m: vcopy(nc, q2[:, m, :]), "v"))
        cx = p.sb("cx", [P, ST, C])
        cxT = p.sb("cxT", [P, KC, S])
        sc = p.sb("sc", [P, NKT * P])
        pT = p.sb("pT", [P, NKT, P])
        top = p.sb("top", [P, 1])
        tot = p.sb("tot", [P, 1])
        ht = p.sb("ht", [P, C])
        for b in range(B):
            load(nc, [(cx[:, n:n + 8, :], arrays["ctx"][b].rearrange("(p n) c -> p n c", p=P)[:, n:n + 8, :]) for n in range(0, ST, 8)])
            gemms(nc, K, [job for n in range(0, ST, 4) for job in (
                (P, 512, [("turn", cx[:, n + t, 0:P], t * P) for t in range(4)], vcopy(nc, cxT[:, 0, n * P:(n + 4) * P]), "v"),
                (P, 512, [("turn", cx[:, n + t, P:C], t * P) for t in range(4)], scopy(nc, cxT[:, 1, n * P:(n + 4) * P]), "s"))])
            for t in range(TB):
                tt = b * TB + t
                qs = slice(tt * P, (tt + 1) * P)
                jobs = [(P, T, [(q2[:, k, qs], znT[:, k, b * T:(b + 1) * T]) for k in range(KC)],
                         vadd(nc, sc[:, S:S + T], K["mask_q"][:, t, :]), "v")]
                for n in range(0, S, 512):
                    jobs.append((P, 512, [(q2[:, k, qs], cxT[:, k, n:n + 512]) for k in range(KC)],
                                 (vcopy if n % 1024 else scopy)(nc, sc[:, n:n + 512]), "v" if n % 1024 else "s"))
                gemms(nc, K, jobs)
                with stage(nc, "top_ready", "exp_ready") as (block, top_ready, exp_ready):
                    @block.vector
                    def _(dve):
                        nc.vector.tensor_reduce(top[:], sc[:], AX.X, ALU.max, negate=True).then_inc(top_ready, 1)
                        dve.wait_ge(top_ready, 1)
                        nc.vector.tensor_scalar(top[:], top[:], 1.0 / 16.0, None, ALU.mult).then_inc(top_ready, 1)
                        dve.wait_ge(exp_ready, 1)
                        nc.vector.reciprocal(tot[:], tot[:]).then_inc(top_ready, 1)
                        dve.wait_ge(top_ready, 3)

                    @block.scalar
                    def _(act):
                        act.wait_ge(top_ready, 2)
                        nc.scalar.activation(sc[:], sc[:], ACT.Exp, bias=top[:, 0:1], scale=1.0 / 16.0, accum_out=tot[:]).then_inc(exp_ready, 1)
                        act.wait_ge(exp_ready, 1)
                jobs = []
                for i, n in enumerate(range(0, NKT, 4)):
                    m = min(4, NKT - n)
                    jobs.append((P, m * P, [("turn", sc[:, (n + j) * P:(n + j + 1) * P], j * P) for j in range(m)],
                                 (vcopy if i % 2 else scopy)(nc, pT[:, n:n + m, :].rearrange("p t q -> p (t q)")), "v" if i % 2 else "s"))
                gemms(nc, K, jobs)

                def blend(ps, step, tt=tt):
                    step(nc.vector.scalar_tensor_tensor(out=ht[:], in0=ps, scalar=tot[:, 0:1], in1=xn[:, tt, :], op0=ALU.mult, op1=ALU.subtract))
                    step(nc.vector.tensor_tensor(ht[:], ht[:], alpha[:, tt, :], ALU.mult))
                    step(nc.vector.tensor_tensor(ht[:], ht[:], xn[:, tt, :], ALU.add))
                    return nc.vector.tensor_tensor(X[:, tt, :], X[:, tt, :], ht[:], ALU.add)

                gemms(nc, K, [(P, C, [(pT[:, n, :], cx[:, n, :]) for n in range(ST)]
                               + [(pT[:, ST + n, :], zn[:, b * TB + n, :]) for n in range(TB)], blend, "v")])


def state_space(nc, K, X, arrays, specs):
    DI = 2 * C
    CH = DI // P
    NS = 16
    with pool(nc, "l2s") as p:
        w = Weights(nc, p, "L2_attn", arrays, specs)
        xn = p.sb("xn", [P, NT, C])
        xnT = p.sb("xnT", [P, KC, NTOK])
        xi = p.sb("xi", [P, CH, NTOK])
        z = p.sb("z", [P, CH, NTOK])
        conv = p.sb("conv", [P, CH, NTOK])
        xs = p.sb("xs", [P, CH, NTOK])
        xp = p.sb("xp", [2 * NS + 1, NTOK])
        raw = p.sb("raw", [P, CH, NTOK])
        delta = p.sb("delta", [P, CH, NTOK])
        dx = p.sb("dx", [P, CH, NTOK])
        A = p.sb("A", [P, NS])
        yT = p.sb("yT", [P, CH, NTOK])
        normalize(nc, K, X, xn, xnT, 1e-5)
        gemms(nc, K, project_T(w["in"], DI, xnT, lambda m: vcopy(nc, xi[:, m, :]), "v")
              + project_T(w["in"][:, :, DI:], DI, xnT, lambda m: (lambda ps, step: nc.scalar.activation(z[:, m, :], ps, ACT.Silu)), "s"))
        with stage(nc, "dve_step", "conv_ready", "act_step", "act_done") as (block, dve_step, conv_ready, act_step, act_done):
            @block.vector
            def _(dve):
                step = Steps(dve, dve_step)
                for m in range(CH):
                    step(nc.vector.tensor_scalar(conv[:, m, :], xi[:, m, :], w["conv_w"][:, m, 3:4], w["conv_b"][:, m:m + 1], ALU.mult, ALU.add))
                    out, src = (x[:, m, :].rearrange("p (b t) -> p b t", b=B) for x in (conv, xi))
                    for s in range(1, 4):
                        step(nc.vector.scalar_tensor_tensor(out=out[:, :, s:T], in0=src[:, :, 0:T - s], scalar=w["conv_w"][:, m, 3 - s:4 - s],
                                                            in1=out[:, :, s:T], op0=ALU.mult, op1=ALU.add))
                dve.sem_inc(conv_ready, 1)

            @block.scalar
            def _(act):
                act.wait_ge(conv_ready, 1)
                nc.scalar.activation(xs[:], conv[:], ACT.Silu).then_inc(act_done, 1)
                nc.scalar.activation(A[:], w["A_log"], ACT.Exp).then_inc(act_done, 1)
                act.wait_ge(act_done, 2)
                nc.scalar.mul(A[:], A[:], -1.0).then_inc(act_done, 1)
                act.wait_ge(act_done, 3)
        gemms(nc, K, [(2 * NS + 1, NTOK, [(w["x"][:, m, :], xs[:, m, :]) for m in range(CH)], vcopy(nc, xp[:]), "v")])
        gemms(nc, K, [(P, NTOK, [(w["dt"][:, m * P:(m + 1) * P], xp[0:1, :])], vbias(nc, raw[:, m, :], w["b_dt"][:, m:m + 1]), "v") for m in range(CH)])
        with stage(nc, "act_step", "soft_ready", "dve_step") as (block, act_step, soft_ready, dve_step):
            @block.scalar
            def _(act):
                step = Steps(act, act_step)
                step(nc.scalar.activation(delta[:], raw[:], ACT.Abs))
                step(nc.scalar.activation(delta[:], delta[:], ACT.Exp, scale=-1.0))
                nc.scalar.activation(delta[:], delta[:], ACT.Ln, bias=K["ones"][:, 0:1]).then_inc(soft_ready, 1)

            @block.vector
            def _(dve):
                step = Steps(dve, dve_step)
                dve.wait_ge(act_step, 1)
                step(nc.vector.tensor_scalar(raw[:], raw[:], 0.0, None, ALU.max))
                dve.wait_ge(soft_ready, 1)
                step(nc.vector.tensor_tensor(delta[:], delta[:], raw[:], ALU.add))
                step(nc.vector.tensor_tensor(dx[:], delta[:], xs[:], ALU.mult))
        with pool(nc, "l2t") as p2:
            psB = p2.ps("psB", [P, 2, 512])
            psC = p2.ps("psC", [P, 2, 512])
            psY = p2.ps("psY", [P, CH, 512])
            decay = p2.sb("decay", [P, 3, NTOK])
            u = p2.sb("u", [P, 2, NTOK])
            h = p2.sb("h", [P, 2, NTOK])
            hc = p2.sb("hc", [P, 3, NTOK])
            with stage(nc, "spread", "input_ready", "decay_ready", "states_ready", "read_ready", "summed", "dve_step") as \
                    (block, spread, input_ready, decay_ready, states_ready, read_ready, summed, dve_step):
                @block.tensor
                def _(pe):
                    def spread_rows(s):
                        if s >= 2:
                            pe.wait_ge(read_ready, (s - 1) * CH)
                        n = 2 * NS + 1
                        for ps, r in ((psB, 1 + s), (psC, 1 + NS + s)):
                            last = nc.tensor.matmul(ps[:, s % 2, :], K["ident"][0:n, r:r + 1].to_broadcast([n, P]), xp[:, :], start=True, stop=True)
                        last.then_inc(spread, 1)

                    spread_rows(0)
                    for s in range(NS):
                        if s + 1 < NS:
                            spread_rows(s + 1)
                        for m in range(CH):
                            i = s * CH + m
                            pe.wait_ge(read_ready, i + 1)
                            nc.tensor.matmul(psY[:, m, :], K["ident"], hc[:, i % 3, :], start=s == 0, stop=s == NS - 1).then_inc(summed, 1)

                @block.scalar
                def _(act):
                    for i in range(NS * CH):
                        if i >= 3:
                            act.wait_ge(states_ready, 2 * (i - 2))
                        nc.scalar.activation(decay[:, i % 3, :], delta[:, i % CH, :], ACT.Exp, scale=A[:, i // CH:i // CH + 1]).then_inc(decay_ready, 1)

                @block.vector
                def _(dve):
                    N = NS * CH

                    def inputs(i):
                        s, m = i // CH, i % CH
                        dve.wait_ge(spread, s + 1)
                        if i >= 2:
                            dve.wait_ge(states_ready, 2 * (i - 1))
                        nc.vector.tensor_tensor(u[:, i % 2, :], psB[:, s % 2, :], dx[:, m, :], ALU.mult).then_inc(input_ready, 1)

                    inputs(0)
                    for i in range(N):
                        s, m = i // CH, i % CH
                        if i + 1 < N:
                            inputs(i + 1)
                        dve.wait_ge(decay_ready, i + 1)
                        dve.wait_ge(input_ready, i + 1)
                        if i >= 2:
                            dve.wait_ge(read_ready, i - 1)
                        for b in range(B):
                            c = slice(b * T, (b + 1) * T)
                            nc.vector.tensor_tensor_scan(h[:, i % 2, c], decay[:, i % 3, c], u[:, i % 2, c], 0.0, ALU.mult, ALU.add).then_inc(states_ready, 1)
                        dve.wait_ge(states_ready, 2 * (i + 1))
                        if i >= 3:
                            dve.wait_ge(summed, i - 2)
                        nc.vector.tensor_tensor(hc[:, i % 3, :], psC[:, s % 2, :], h[:, i % 2, :], ALU.mult).then_inc(read_ready, 1)
                    dve.wait_ge(summed, N)
                    step = Steps(dve, dve_step)
                    for m in range(CH):
                        step(nc.vector.scalar_tensor_tensor(out=yT[:, m, :], in0=xs[:, m, :], scalar=w["D"][:, m:m + 1], in1=psY[:, m, :],
                                                            op0=ALU.mult, op1=ALU.add))
                        step(nc.vector.tensor_tensor(yT[:, m, :], yT[:, m, :], z[:, m, :], ALU.mult))
        gemms(nc, K, project_rows(w["out"], C, yT, lambda t: vadd(nc, X[:, t, :], X[:, t, :]), "v", kc=CH))


def expert_choice(nc, K, X, arrays, specs):
    with pool(nc, "l2f") as p:
        w = Weights(nc, p, "L2_ffn", arrays, specs)
        xn = p.sb("xn", [P, NT, C])
        xnT = p.sb("xnT", [P, KC, NTOK])
        W1 = [p.sb(f"W1_{i}", [P, KC, FF]) for i in range(2)]
        W2 = [p.sb(f"W2_{i}", [P, FC, C]) for i in range(2)]
        score = p.sb("score", [P, E, NT])
        rank = p.sb("rank", [P, E * NT])
        over = p.sb("over", [P, E, NT])
        same = p.sb("same", [P, E, NT])
        scores = p.sb("scores", [P, E, NTOK])
        junk = p.sb("junk", [P, 2, NTOK])

        def sources(e):
            one = bass.ds(e, 1)
            return [arrays["M1"][one].rearrange("o (k p) n -> p (o k) n", p=P), arrays["M2"][one].rearrange("o (k p) n -> p (o k) n", p=P)]

        load(nc, list(zip((W1[0][:], W2[0][:]), sources(0))))
        normalize(nc, K, X, xn, xnT, 1e-5)
        gemms(nc, K, project_rows(w["gate"], E, xnT, lambda t: (lambda ps, step: nc.scalar.activation(score[:, :, t], ps, ACT.Sigmoid)), "s"))
        gemms(nc, K, [(P, NTOK, [("turn", score[:, e, t:t + 1].to_broadcast([P, P]), t * P) for t in range(NT)], scopy(nc, scores[:, e, :]), "s")
                      for e in range(E)])
        with stage(nc, "dve_step", "counted") as (block, dve_step, counted):
            @block.vector
            def _(dve):
                step = Steps(dve, dve_step)
                for n in range(E * NT):
                    e, t = n // NT, n % NT
                    if n:
                        dve.wait_ge(counted, 2 * n)
                    nc.vector.tensor_scalar(junk[:, 0, :], scores[:, e, :], score[:, e, t:t + 1], 0.0, ALU.is_gt, ALU.add,
                                            accum_out=over[:, e, t:t + 1]).then_inc(counted, 1)
                    nc.vector.scalar_tensor_tensor(out=junk[:, 1, :], in0=scores[:, e, :], scalar=score[:, e, t:t + 1], in1=w["before"][:, t, :],
                                                   op0=ALU.is_equal, op1=ALU.mult, accum_out=same[:, e, t:t + 1]).then_inc(counted, 1)
                dve.wait_ge(counted, 2 * E * NT)
                step(nc.vector.tensor_tensor(rank[:], over[:].rearrange("p e t -> p (e t)"), same[:].rearrange("p e t -> p (e t)"), ALU.add))
        rk = p.sb("rk", [P, 2 * NT])
        sc = p.sb("sc", [P, 2 * NT])
        b1 = p.sb("b1", [P, 2 * FC])
        b2 = p.sb("b2", [1, 2 * C])
        place = p.sb("place", [P, NT, P])
        placeT = p.sb("placeT", [P, NT, P])
        exT = p.sb("exT", [P, KC, P])
        hT = p.sb("hT", [P, FC, P])
        rows = p.sb("rows", [P, C])
        flat_score = score[:].rearrange("p e t -> p (e t)")
        with nc.Fori(0, E // 2) as pair:
            e = pair * 2
            with pool(nc, "l2e") as p2:
                psX = p2.ps("psX", [P, KC, P])
                psP = p2.ps("psP", [P, NT, P])
                psH = p2.ps("psH", [P, 2, 4, P])
                psR = p2.ps("psR", [P, C])
                psY = p2.ps("psY", [P, 2, 512])
                with stage(nc, "picked", "placed", "gathered", "turned", "gathered_copied", "turned_copied", "inner_ready",
                           "gelu_ready", "rows_ready", "rows_copied", "y_ready", "y_taken", "loaded1", "loaded0") as \
                        (block, picked, placed, gathered, turned, gathered_copied, turned_copied, inner_ready,
                         gelu_ready, rows_ready, rows_copied, y_ready, y_taken, loaded1, loaded0):
                    @block.sync
                    def _(sp):
                        for dst, src in zip((W1[1][:], W2[1][:]), sources(e + 1)):
                            sp.dma_start(dst, src).then_inc(loaded1, 16)
                        sp.wait_ge(rows_ready, 1)
                        for dst, src in zip((W1[0][:], W2[0][:]), sources(e + 2)):
                            sp.dma_start(dst, src).then_inc(loaded0, 16)
                        sp.wait_ge(loaded1, 32)
                        sp.wait_ge(loaded0, 32)

                    @block.tensor
                    def _(pe):
                        for i in range(2):
                            pe.wait_ge(placed, NT * (i + 1))
                            for k in range(KC):
                                for t in range(NT):
                                    last = nc.tensor.matmul(psX[:, k, :], xn[:, t, k * P:(k + 1) * P], place[:, t, :], start=t == 0, stop=t == NT - 1)
                            last.then_inc(gathered, 1)
                            for t in range(NT):
                                last = nc.tensor.transpose(psP[:, t, :], place[:, t, :], K["ident"])
                            last.then_inc(turned, 1)
                            pe.wait_ge(gathered_copied, i + 1)
                            if i:
                                pe.wait_ge(loaded1, 32)
                            for f in range(FC):
                                if i:
                                    pe.wait_ge(gelu_ready, f // 4 * 4 + 4)
                                for k in range(KC):
                                    last = nc.tensor.matmul(psH[:, f // 4, f % 4, :], W1[i][:, k, f * P:(f + 1) * P], exT[:, k, :], start=k == 0, stop=k == KC - 1)
                                if f % 4 == 3:
                                    last.then_inc(inner_ready, 1)
                            pe.wait_ge(gelu_ready, FC * (i + 1))
                            for f in range(FC):
                                nc.tensor.matmul(psR[:, :], hT[:, f, :], W2[i][:, f, :], start=f == 0, stop=False)
                            nc.tensor.matmul(psR[:, :], K["ones"][0:1, :], b2[0:1, i * C:(i + 1) * C], start=False, stop=True).then_inc(rows_ready, 1)
                            pe.wait_ge(rows_copied, i + 1)
                            pe.wait_ge(turned_copied, i + 1)
                            for t in range(NT):
                                if i * NT + t >= 2:
                                    pe.wait_ge(y_taken, i * NT + t - 1)
                                nc.tensor.matmul(psY[:, t % 2, 0:C], placeT[:, t, :], rows[:], start=True, stop=True).then_inc(y_ready, 1)

                    @block.scalar
                    def _(act):
                        act.wait_ge(picked, 4)
                        for i in range(2):
                            act.wait_ge(turned, i + 1)
                            if i:
                                act.wait_ge(y_ready, NT)
                            nc.scalar.copy(placeT[:], psP[:]).then_inc(turned_copied, 1)
                            for f in range(FC):
                                act.wait_ge(inner_ready, 2 * i + f // 4 + 1)
                                if i:
                                    act.wait_ge(rows_ready, i)
                                nc.scalar.activation(hT[:, f, :], psH[:, f // 4, f % 4, :], ACT.Gelu,
                                                     bias=b1[:, i * FC + f:i * FC + f + 1]).then_inc(gelu_ready, 1)

                    @block.vector
                    def _(dve):
                        nc.vector.tensor_copy(rk[:], rank[:, bass.ds(e * NT, 2 * NT)]).then_inc(picked, 1)
                        nc.vector.tensor_copy(sc[:], flat_score[:, bass.ds(e * NT, 2 * NT)]).then_inc(picked, 1)
                        nc.vector.tensor_copy(b1[:], w["b1"][:, bass.ds(e * FC, 2 * FC)]).then_inc(picked, 1)
                        nc.vector.tensor_copy(b2[:], w["b2"][:, bass.ds(e * C, 2 * C)]).then_inc(picked, 1)
                        dve.wait_ge(picked, 4)
                        for i in range(2):
                            if i:
                                dve.wait_ge(gathered, i)
                                dve.wait_ge(turned, i)
                            for t in range(NT):
                                nc.vector.tensor_scalar(place[:, t, :], w["iota"], rk[:, i * NT + t:i * NT + t + 1], None, ALU.is_equal).then_inc(placed, 1)
                            dve.wait_ge(gathered, i + 1)
                            if i:
                                dve.wait_ge(inner_ready, 2 * i)
                            nc.vector.tensor_copy(exT[:], psX[:]).then_inc(gathered_copied, 1)
                            dve.wait_ge(rows_ready, i + 1)
                            if i:
                                dve.wait_ge(y_ready, NT * i)
                            nc.vector.tensor_copy(rows[:], psR[:]).then_inc(rows_copied, 1)
                            for t in range(NT):
                                n = i * NT + t
                                dve.wait_ge(y_ready, n + 1)
                                if n >= NT:
                                    dve.wait_ge(y_taken, n - NT + 1)
                                nc.vector.scalar_tensor_tensor(out=X[:, t, :], in0=psY[:, t % 2, 0:C], scalar=sc[:, n:n + 1], in1=X[:, t, :],
                                                               op0=ALU.mult, op1=ALU.add).then_inc(y_taken, 1)


def rope_and_groups(nc, K, X, arrays, specs):
    HID = 512
    HC = HID // P
    with pool(nc, "l3f") as p:
        w = Weights(nc, p, "L3_ffn", arrays, specs)
        xn = p.sb("xn", [P, NT, C])
        s1 = p.sb("s1", [P, NT, C])
        x1 = p.sb("x1", [P, NT, C])
        x1T = p.sb("x1T", [P, KC, NTOK])
        with pool(nc, "l3g") as p1:
            xnT = p1.sb("xnT", [P, KC, NTOK])
            lowk = p1.sb("lowk", [64, 1, NTOK])
            lowv = p1.sb("lowv", [64, 1, NTOK])
            qT = p1.sb("qT", [P, 4, NTOK])
            kT = p1.sb("kT", [P, 4, NTOK])
            v = p1.sb("v", [P, NT, 512])
            attT = p1.sb("attT", [P, 4, NTOK])
            other = p1.sb("other", [P, 8, NTOK])
            normalize(nc, K, X, xn, xnT, 1e-5)
            gemms(nc, K, [(64, NTOK, [(w[n][:, k, :], xnT[:, k, :]) for k in range(KC)], vcopy(nc, dst[:, 0, :]), "v")
                          for n, dst in (("kc", lowk), ("vc", lowv))])

            def straight(dst, bias):
                def at(m):
                    def evac(ps, step):
                        if bias is None:
                            return nc.vector.tensor_tensor(dst[:, m, :], ps, w["cos"], ALU.mult)
                        step(nc.vector.tensor_tensor(dst[:, m, :], ps, w["cos"], ALU.mult))
                        return nc.vector.tensor_scalar(dst[:, m, :], dst[:, m, :], bias, None, ALU.add)
                    return evac
                return at

            def crossed(dst, base):
                def at(m):
                    def evac(ps, step):
                        step(nc.vector.tensor_tensor(other[:, base + m, :], ps, w["sin"], ALU.mult))
                        return nc.vector.tensor_tensor(dst[:, m, :], dst[:, m, :], other[:, base + m, :], ALU.add)
                    return evac
                return at

            gemms(nc, K, project_T(w["q"], 512, xnT, straight(qT, None), "v") + project_T(w["k"], 512, lowk, straight(kT, w["ones_row"]), "v", kc=1)
                  + project_T(w["qx"], 512, xnT, crossed(qT, 0), "v") + project_T(w["kx"], 512, lowk, crossed(kT, 4), "v", kc=1)
                  + project_rows(w["v"], 512, lowv, lambda t: scopy(nc, v[:, t, :]), "s", kc=1, bias=w["bv"], ones=K["ones"][0:1, :]))
            self_attend(nc, K, qT, kT, v, attT, 4, False)
            gemms(nc, K, project_rows(w["o"], C, attT, lambda t: vadd(nc, s1[:, t, :], xn[:, t, :]), "v", kc=4))
        normalize(nc, K, s1, x1, x1T, 1e-6, rms=True, w=w["norm1_w"])
        acc = p.sb("acc", [P, NT, C])
        sil = p.sb("sil", [P, 2 * HC, NTOK])
        hT = p.sb("hT", [P, 2 * HC, NTOK])
        logit = p.sb("logit", [P, NT, 2 + E])
        gate = p.sb("gate", [P, NT, E])
        gemms(nc, K, [(P, NTOK, [(w[n][:, k, m * P:(m + 1) * P], x1T[:, k, :]) for k in range(KC)],
                       (lambda ps, step, i=i, m=m: nc.scalar.activation(sil[:, i * HC + m, :], ps, ACT.Silu)), "s")
                      for i, n in enumerate(("in", "w1")) for m in range(HC)]
              + project_rows(w["gates"], 2 + E, x1T, lambda t: vcopy(nc, logit[:, t, :]), "v", bias=w["bgates"], ones=K["ones"][0:1, :]))
        gemms(nc, K, [(P, NTOK, [(w[n][:, k, HID + m * P:HID + (m + 1) * P], x1T[:, k, :]) for k in range(KC)],
                       (lambda ps, step, i=i, m=m: nc.vector.tensor_tensor(hT[:, i * HC + m, :], ps, sil[:, i * HC + m, :], ALU.mult)), "v")
                      for i, n in enumerate(("in", "w1")) for m in range(HC)])
        group_weights(nc, p, logit, gate)
        gemms(nc, K, project_rows(w["out"], C, hT, lambda t: vadd(nc, acc[:, t, :], x1[:, t, :]), "v", kc=HC)
              + [(P, C, [(hT[:, HC + k, t * P:(t + 1) * P], w["w2"][:, e * HC + k, :]) for k in range(HC)],
                  (lambda ps, step, e=e, t=t: nc.vector.scalar_tensor_tensor(out=acc[:, t, :], in0=ps, scalar=gate[:, t, e:e + 1], in1=acc[:, t, :],
                                                                            op0=ALU.mult, op1=ALU.add)), "v")
                 for e in range(E) for t in range(NT)])
        normalize(nc, K, acc, s1, None, 1e-6, rms=True, w=w["norm2_w"])
        with stage(nc, "added") as (block, added):
            @block.vector
            def _(dve):
                nc.vector.tensor_tensor(X[:], X[:], s1[:], ALU.add).then_inc(added, 1)
                dve.wait_ge(added, 1)


def group_weights(nc, p, logit, gate):
    G, EG = 2, E // 2
    names = ("gmax", "gsum", "gp", "emax", "esum", "ep", "prob", "rank", "cmp")
    shapes = ((P, NT), (P, NT), (P, NT, G), (P, NT, G), (P, NT, G), (P, NT, E), (P, NT, E), (P, NT, E), (P, NT, E))
    gmax, gsum, gp, emax, esum, ep, prob, rank, cmp = (p.sb(n, list(s)) for n, s in zip(names, shapes))
    with stage(nc, "dve_step", "shifted", "exp_ready") as (block, dve_step, shifted, exp_ready):
        @block.scalar
        def _(act):
            act.wait_ge(shifted, 2)
            nc.scalar.activation(gp[:], gp[:], ACT.Exp).then_inc(exp_ready, 1)
            nc.scalar.activation(ep[:], ep[:], ACT.Exp).then_inc(exp_ready, 1)

        @block.vector
        def _(dve):
            V = nc.vector
            step = Steps(dve, dve_step)

            def by_group(x):
                return x[:].rearrange("p t (g e) -> p (t g) e", g=G)

            def each(x, n):
                return x.unsqueeze(2).to_broadcast([P, x.shape[1], n])

            def flat(x):
                return x[:].rearrange("p t g -> p (t g)")

            step(V.tensor_reduce(gmax[:], logit[:, :, 0:G], AX.X, ALU.max))
            V.tensor_tensor(gp[:], logit[:, :, 0:G], each(gmax[:], G), ALU.subtract).then_inc(shifted, 1)
            step(V.tensor_copy(ep[:], logit[:, :, G:G + E]))
            step(V.tensor_reduce(flat(emax), by_group(ep), AX.X, ALU.max))
            V.tensor_tensor(by_group(ep), by_group(ep), each(flat(emax), EG), ALU.subtract).then_inc(shifted, 1)
            dve.wait_ge(exp_ready, 2)
            step(V.tensor_reduce(gsum[:], gp[:], AX.X, ALU.add))
            step(V.reciprocal(gsum[:], gsum[:]))
            step(V.tensor_tensor(gp[:], gp[:], each(gsum[:], G), ALU.mult))
            step(V.tensor_reduce(flat(esum), by_group(ep), AX.X, ALU.add))
            step(V.reciprocal(esum[:], esum[:]))
            step(V.tensor_tensor(by_group(prob), by_group(ep), each(flat(esum), EG), ALU.mult))
            step(V.tensor_tensor(emax[:, :, 1], gp[:, :, 1], gp[:, :, 0], ALU.is_gt))
            step(V.tensor_scalar(emax[:, :, 0], emax[:, :, 1], -1.0, 1.0, ALU.mult, ALU.add))
            step(V.tensor_tensor(gp[:], gp[:], emax[:], ALU.mult))
            step(V.tensor_tensor(by_group(prob), by_group(prob), each(flat(gp), EG), ALU.mult))
            step(V.memset(rank[:], 0.0))
            for e in range(E):
                it = prob[:, :, e:e + 1].to_broadcast([P, NT, E])
                step(V.tensor_tensor(cmp[:], it, prob[:], ALU.is_gt))
                step(V.tensor_tensor(rank[:], rank[:], cmp[:], ALU.add))
                if e + 1 < E:
                    n = E - 1 - e
                    it = prob[:, :, e:e + 1].to_broadcast([P, NT, n])
                    step(V.tensor_tensor(cmp[:, :, e + 1:], it, prob[:, :, e + 1:], ALU.is_equal))
                    step(V.tensor_tensor(rank[:, :, e + 1:], rank[:, :, e + 1:], cmp[:, :, e + 1:], ALU.add))
            step(V.tensor_scalar(rank[:], rank[:], 2.0, None, ALU.is_lt))
            step(V.tensor_tensor(gate[:], prob[:], rank[:], ALU.mult))


LAYERS = [
    ("L0_xattn", lambda nc, K, X, a, s: cross_attention(nc, K, X, a, s, "L0_xattn")),
    ("L0_attn", alibi_attention),
    ("L0_ffn", routed_geglu),
    ("L1_xattn", lambda nc, K, X, a, s: cross_attention(nc, K, X, a, s, "L1_xattn")),
    ("L1_attn", hyperbolic_attention),
    ("L1_ffn", channel_mix),
    ("L2_xattn", lora_attention),
    ("L2_attn", state_space),
    ("L2_ffn", expert_choice),
    ("L3_xattn", pooled_attention),
    ("L3_attn", complex_attention),
    ("L3_ffn", rope_and_groups),
]


def build(nc, x, out, arrays, specs, layers=None):
    with pool(nc, "top") as p:
        X = p.sb("X", [P, NT, C])
        const = Weights(nc, p, "consts", arrays, specs)
        K = {k: const[k] for k in specs["consts"]}
        K["sel"] = {32: K["sel32"], 64: K["sel64"]}
        ident16 = p.sb("ident16", [P, P], BF16)
        K["ident16"] = ident16[:]
        with stage(nc, "converted") as (block, converted):
            @block.vector
            def _(dve):
                nc.vector.tensor_copy(ident16[:], K["ident"]).then_inc(converted, 1)
                dve.wait_ge(converted, 1)
        load(nc, [(X[:, t, :], x[t // TB, (t % TB) * P:(t % TB + 1) * P, :]) for t in range(NT)])
        for name, layer in LAYERS:
            if layers is None or name in layers:
                layer(nc, K, X, arrays, specs)
        with stage(nc, "stored") as (block, stored):
            @block.sync
            def _(sp):
                for t in range(NT):
                    sp.dma_start(out[t // TB, (t % TB) * P:(t % TB + 1) * P, :], X[:, t, :]).then_inc(stored, 16)
                sp.wait_ge(stored, 16 * NT)


def chunks(w):
    k, n = w.shape
    if k <= P:
        return w.reshape(k, 1, n)
    return w.reshape(k // P, P, n).transpose(1, 0, 2)


def pad_heads(w, d=16, fill=0.0):
    lead = w.shape[:-1]
    out = np.zeros(lead + (w.shape[-1] // d, 2 * d), np.float32)
    out[..., :d] = w.reshape(lead + (-1, d))
    out[..., d] = fill
    return out.reshape(lead + (-1,))


def column(v):
    return v.reshape(-1, P).T


def row(v):
    return v.reshape(1, -1)


def swap_pairs(w):
    return w.reshape(w.shape[0], -1, 2)[:, :, ::-1].reshape(w.shape)


def rotary_tables():
    inv = (1.0 / 10000.0 ** (np.arange(0, 16, 2, dtype=np.float32) / 16)).astype(np.float32)
    ang = (np.arange(T, dtype=np.float32)[None, :] * inv[:, None]).astype(np.float32)
    cos, sin = np.zeros((2, P // 32, 32, B, T), np.float32)
    cos[:, 0:16] = np.repeat(np.cos(ang), 2, axis=0)[None, :, None, :]
    sin[:, 0:16:2] = -np.sin(ang)[None, :, None, :]
    sin[:, 1:16:2] = np.sin(ang)[None, :, None, :]
    return cos.reshape(P, NTOK), sin.reshape(P, NTOK)


def everywhere(v):
    return np.broadcast_to(v.reshape(1, -1), (P, v.size))


def constants():
    i = np.arange(P)
    q, k = np.arange(T)[:, None], np.arange(T)[None, :]
    mask_q = np.where(k <= q, 0.0, MASKED).astype(np.float32)
    return {
        "ident": np.eye(P, dtype=np.float32),
        "sel32": (i[:, None] == i[None, :] // 32 * 32 + 16).astype(np.float32),
        "sel64": (i[:, None] == i[None, :] // 64 * 64 + 32).astype(np.float32),
        "ones": np.ones((P, P), np.float32),
        "comb": (i[:, None] % 32 == i[None, :32]).astype(np.float32),
        "comb0": ((i[:, None] % 32 == i[None, :32]) & (i[:, None] < 64)).astype(np.float32),
        "comb1": ((i[:, None] % 32 == i[None, :32]) & (i[:, None] >= 64)).astype(np.float32),
        "mask_q": chunks(mask_q),
        "mask_k": chunks(np.ascontiguousarray(mask_q.T)),
    }


def alibi_tables():
    slopes = np.array([2.0 ** (-8.0 / H) * (2.0 ** (-8.0 / H)) ** i for i in range(H)], np.float32)
    pos = np.tile(np.arange(T, dtype=np.float32), B)
    q = np.zeros((H, 32, NTOK), np.float32)
    k = np.zeros((H, 32, NTOK), np.float32)
    q[:, 17] = 4 * slopes[:, None]
    k[:, 17] = pos
    q[:, 18] = -4 * slopes[:, None] * pos
    k[:, 18] = 1
    return chunks(q.reshape(-1, NTOK)), chunks(k.reshape(-1, NTOK))


def layouts(i):
    q_table, k_table = alibi_tables()
    cos, sin = rotary_tables()
    zero = np.zeros
    return {
        "consts": constants(),
        "L0_attn": {
            "q": chunks(pad_heads(i["L0_attn_q_w"].T)), "k": chunks(pad_heads(i["L0_attn_k_w"].T)),
            "v": chunks(pad_heads(i["L0_attn_v_w"].T)), "o": chunks(pad_heads(i["L0_attn_o_w"]).T),
            "bq": column(pad_heads(i["L0_attn_q_b"])), "bk": column(pad_heads(i["L0_attn_k_b"], fill=1.0)),
            "bv": row(pad_heads(i["L0_attn_v_b"], fill=1.0)), "bo": row(i["L0_attn_o_b"]),
            "q_table": q_table, "k_table": k_table,
        },
        "L0_xattn": {
            "q": chunks(i["L0_xattn_Wq"]), "k": chunks(i["L0_xattn_Wk"]), "v": chunks(i["L0_xattn_Wv"]), "o": chunks(pad_heads(i["L0_xattn_Wp"].T).T),
            "bq": column(i["L0_xattn_bq"]), "bk": column(i["L0_xattn_bk"]), "bv": row(i["L0_xattn_bv"]), "bo": row(i["L0_xattn_bp"]),
        },
        "L1_xattn": {
            "q": chunks(i["L1_xattn_w_q"].T), "k": chunks(i["L1_xattn_w_k"].T), "v": chunks(i["L1_xattn_w_v"].T), "o": chunks(pad_heads(i["L1_xattn_w_o"]).T),
            "bq": column(i["L1_xattn_b_q"]), "bk": column(i["L1_xattn_b_k"]), "bv": row(i["L1_xattn_b_v"]), "bo": row(i["L1_xattn_b_o"]),
        },
        "L0_ffn": {
            "gate": chunks(i["L0_ffn_Wg"]), "iota_less": np.broadcast_to(np.arange(E, dtype=np.float32) - E, (P, 1, E)),
        },
        "L1_attn": {
            "qk": chunks(i["L1_attn_Wqkv"][:2 * C].T), "v": chunks(i["L1_attn_Wqkv"][2 * C:].T), "o": chunks(i["L1_attn_Wout"].T),
            "gates": chunks(np.concatenate([i["L1_attn_Walpha"], i["L1_attn_Wimp"]]).T),
            "bqk": row(i["L1_attn_bqkv"][:2 * C]), "bv": row(i["L1_attn_bqkv"][2 * C:]), "bo": row(i["L1_attn_bout"]),
            "bgates": row(np.concatenate([i["L1_attn_balpha"], i["L1_attn_bimp"]])),
            "threshold": everywhere(i["L1_attn_spike_threshold"]), "qk_scale": everywhere(i["L1_attn_qk_scale"]),
            "log_k": everywhere(i["L1_attn_log_k"]),
        },
        "L3_xattn": {
            "q": chunks(i["L3_xattn_q_w"].T), "k": chunks(i["L3_xattn_k_w"]), "gate": chunks(i["L3_xattn_gate_w"].T),
            "gate_b": row(i["L3_xattn_gate_b"]), "norm_w": everywhere(i["L3_xattn_norm_w"]),
        },
        "L2_attn": {
            "in": chunks(i["L2_attn_W_in"]), "x": chunks(i["L2_attn_W_x"]), "out": chunks(i["L2_attn_W_out"]),
            "conv_w": chunks(i["L2_attn_conv_w"][:, 0, :]), "conv_b": column(i["L2_attn_conv_b"]), "dt": row(i["L2_attn_W_dt"]),
            "b_dt": column(i["L2_attn_b_dt"]), "A_log": everywhere(i["L2_attn_A_log"]), "D": column(i["L2_attn_D"]),
        },
        "L2_ffn": {
            "gate": chunks(i["L2_ffn_Wg"]), "iota": everywhere(np.arange(P, dtype=np.float32)),
            "before": chunks((np.arange(NTOK)[None, :] < np.arange(NTOK)[:, None]).astype(np.float32)),
            "b1": i["L2_ffn_b1"].reshape(E * FC, P).T, "b2": row(i["L2_ffn_b2"]),
        },
        "L3_ffn": {
            "q": chunks(pad_heads(i["L3_ffn_Wq"])), "qx": chunks(pad_heads(swap_pairs(i["L3_ffn_Wq"]))),
            "kc": chunks(i["L3_ffn_Wk_c"]), "vc": chunks(i["L3_ffn_Wv_c"]),
            "k": chunks(pad_heads(i["L3_ffn_Wk"])), "kx": chunks(pad_heads(swap_pairs(i["L3_ffn_Wk"]))),
            "v": chunks(pad_heads(i["L3_ffn_Wv"])), "o": chunks(pad_heads(i["L3_ffn_Wo"].T).T),
            "bv": row(pad_heads(zero(256, np.float32), fill=1.0)), "cos": cos, "sin": sin,
            "ones_row": (np.arange(P) % 32 == 16).astype(np.float32)[:, None],
            "in": chunks(i["L3_ffn_W_shared_in"]), "w1": chunks(i["L3_ffn_W1_shared"]), "out": chunks(i["L3_ffn_W_shared_out"]),
            "w2": chunks(i["L3_ffn_W2_experts"].reshape(-1, C)),
            "gates": chunks(np.concatenate([i["L3_ffn_Wg_gate"], i["L3_ffn_We_gate"]], axis=1)),
            "bgates": row(np.concatenate([i["L3_ffn_group_bias"], i["L3_ffn_expert_bias"]])),
            "norm1_w": everywhere(i["L3_ffn_norm1_w"]), "norm2_w": everywhere(i["L3_ffn_norm2_w"]),
        },
        "L1_ffn": {
            "r": chunks(i["L1_ffn_W_r"].T), "k": chunks(i["L1_ffn_W_k"].T), "v": chunks(i["L1_ffn_W_v"].T),
            "mu": np.concatenate([column(i["L1_ffn_mu_r"]), column(i["L1_ffn_mu_k"])], axis=1),
        },
        "L2_xattn": {
            "q": chunks(pad_heads(i["L2_xattn_Wq"].T)), "k": chunks(pad_heads(i["L2_xattn_Wf"][:C].T)),
            "v": chunks(pad_heads(i["L2_xattn_Wf"][C:].T)), "o": chunks(pad_heads(i["L2_xattn_Wp"]).T),
            "bq": column(pad_heads(i["L2_xattn_bq"])), "bk": column(pad_heads(i["L2_xattn_bf"][:C], fill=1.0)),
            "bv": row(pad_heads(i["L2_xattn_bf"][C:], fill=1.0)), "bo": row(i["L2_xattn_bp"]),
            "Aq": chunks(i["L2_xattn_Aq"].T), "Af": chunks(i["L2_xattn_Af"].T), "Ap": chunks(pad_heads(i["L2_xattn_Ap"]).T),
            "Bq": chunks(pad_heads(i["L2_xattn_Bq"].T)), "Bk": chunks(pad_heads(i["L2_xattn_Bf"][:C].T)),
            "Bv": chunks(pad_heads(i["L2_xattn_Bf"][C:].T)), "Bp": chunks(i["L2_xattn_Bp"].T),
        },
        "L3_attn": {
            "q": chunks(pad_heads(i["L3_attn_Wq"], 32)), "k": chunks(pad_heads(i["L3_attn_Wk"], 32)),
            "v": chunks(pad_heads(i["L3_attn_Wv"], 32)), "o": chunks(pad_heads(i["L3_attn_Wo"].T, 32).T),
            "bk": column(pad_heads(zero(512, np.float32), 32, 1.0)), "bv": row(pad_heads(zero(512, np.float32), 32, 1.0)),
        },
    }


def pack(blocks):
    n = sum(int(np.prod(b.shape[1:])) for b in blocks.values())
    packed = np.zeros((P, n), np.float32)
    at, spec = 0, {}
    for name, b in blocks.items():
        m = int(np.prod(b.shape[1:]))
        packed[:b.shape[0], at:at + m] = b.reshape(b.shape[0], m)
        spec[name] = (at, b.shape)
        at += m
    return packed, spec


def lay_out(inputs, layers=None):
    arrays, specs = {}, {}
    for name, blocks in layouts(inputs).items():
        if layers is not None and name not in layers and name != "consts":
            continue
        arrays[name], specs[name] = pack(blocks)
    arrays.update(big_arrays(inputs))
    return arrays, specs


def big_arrays(i):
    return {
        "x": i["x"], "ctx": i["ctx_1024"], "fside": i["fside_BxSxS_0"],
        "W1": np.concatenate([i["L0_ffn_W1"], i["L0_ffn_w1s"][None]]),
        "W2": np.concatenate([i["L0_ffn_W2"], i["L0_ffn_w2s"][None]]),
        "W3": np.concatenate([i["L0_ffn_W3"], i["L0_ffn_w3s"][None]]),
        "M1": np.concatenate([i["L2_ffn_W1"], i["L2_ffn_W1"][:1]]),
        "M2": np.concatenate([i["L2_ffn_W2"], i["L2_ffn_W2"][:1]]),
    }


def kernel(**inputs):
    import numpy as _np
    import concourse.bacc as _bacc
    from concourse import mybir as _mybir
    from concourse.bass_utils import run_bass_kernel_spmd as _run

    nc = _bacc.Bacc("TRN2", target_bir_lowering=False, num_devices=1)
    arrays, specs = lay_out({k: _np.asarray(v) for k, v in inputs.items()})
    aps = {n: nc.dram_tensor(f"in_{n}", a.shape, _mybir.dt.float32, kind="ExternalInput").ap() for n, a in arrays.items()}
    out = nc.dram_tensor("out_x", (B, T, C), _mybir.dt.float32, kind="ExternalOutput").ap()
    build(nc, aps["x"], out, aps, specs)
    r = _run(nc, [{f"in_{n}": _np.ascontiguousarray(a) for n, a in arrays.items()}], core_ids=[0])
    return r.results[0]["out_x"]
```

```python
from contextlib import ExitStack, contextmanager

import concourse.bass as bass
import numpy as np
from concourse import mybir

F32 = mybir.dt.float32
ACT = mybir.ActivationFunctionType
ALU = mybir.AluOpType
AX = mybir.AxisListType
P = 128
B = 2
T = 256
C = 256
H = 16
KC = C // P
NT = B * T // P
NTOK = B * T
TB = T // P
S = 4096
ST = S // P
E = 8
FF = 1024
FC = FF // P
MASKED = -1.0e30


BEFORE = {}


def release(nc):
    if id(nc) in BEFORE:
        BEFORE.pop(id(nc)).close()


@contextmanager
def stage(nc, *names):
    es = ExitStack()
    k = nc.next_id()
    sems = [es.enter_context(nc.semaphore(f"{n}_{k}")) for n in names]
    with nc.Block() as block:
        yield (block, *sems)
    nums = [s.num for s in sems]
    run = [nums[0]]
    for n in nums[1:] + [None]:
        if n is None or n != run[-1] + 1:
            nc.gpsimd.sem_clear(range(run[0], run[-1] + 1))
            run = []
        run.append(n)
    release(nc)
    BEFORE[id(nc)] = es


@contextmanager
def turns(nc, n):
    with nc.Fori(0, n) as i:
        yield i
        nc.all_engine_barrier()


class Steps:

    def __init__(self, engine, done):
        self.engine, self.done, self.n = engine, done, 0

    def __call__(self, instruction):
        self.n += 1
        instruction.then_inc(self.done, 1)
        self.engine.wait_ge(self.done, self.n)


class Pool:

    def __init__(self, nc, es, prefix):
        self.nc, self.es, self.prefix = nc, es, prefix

    def sb(self, name, shape, dt=F32):
        return self.es.enter_context(self.nc.sbuf_tensor(f"{self.prefix}_{name}", shape, dt))

    def ps(self, name, shape, dt=F32):
        return self.es.enter_context(self.nc.psum_tensor(f"{self.prefix}_{name}", shape, dt))


@contextmanager
def pool(nc, prefix):
    with ExitStack() as es:
        yield Pool(nc, es, prefix)


def load(nc, pairs, vector=None, pool_engine=None):
    vector, pool_engine = vector or [], pool_engine or []
    with stage(nc, "loaded_sp", "loaded_act", "dve_done", "pool_done") as (block, loaded_sp, loaded_act, dve_done, pool_done):
        @block.sync
        def _(sp):
            for dst, src in pairs[0::2]:
                sp.dma_start(dst, src).then_inc(loaded_sp, 16)
            sp.wait_ge(loaded_sp, 16 * len(pairs[0::2]))

        @block.scalar
        def _(act):
            for dst, src in pairs[1::2]:
                act.dma_start(dst, src).then_inc(loaded_act, 16)
            if pairs[1::2]:
                act.wait_ge(loaded_act, 16 * len(pairs[1::2]))

        @block.vector
        def _(dve):
            for n, one in enumerate(vector):
                one().then_inc(dve_done, 1)
                dve.wait_ge(dve_done, n + 1)

        @block.gpsimd
        def _(gp):
            for n, one in enumerate(pool_engine):
                one().then_inc(pool_done, 1)
                gp.wait_ge(pool_done, n + 1)


def normalize(nc, K, X, xn, xnT, eps, rms=False, w=None):
    with pool(nc, f"nrm{nc.next_id()}") as p:
        stats = p.sb("stats", [P, NT, 6])
        mv = p.sb("mv", [P, NT, 2])
        var = p.sb("var", [P, NT])
        sd = p.sb("sd", [P, NT])
        rstd = p.sb("rstd", [P, NT])
        shift = p.sb("shift", [P, NT])
        sq = p.sb("sq", [P, C])
        psT = p.ps("psT", [P, KC, 512])
        with stage(nc, "dve_step", "var_ready", "sd_ready", "rows_ready", "turned", "stored") as \
                (block, dve_step, var_ready, sd_ready, rows_ready, turned, stored):
            @block.vector
            def _(dve):
                step = Steps(dve, dve_step)
                for t in range(NT):
                    nc.vector.bn_stats(stats[:, t, :], X[:, t, :]).then_inc(dve_step, 1)
                step.n = NT
                dve.wait_ge(dve_step, step.n)
                for t in range(NT):
                    nc.vector.bn_aggr(mv[:, t, :], stats[:, t, :]).then_inc(dve_step, 1)
                step.n += NT
                dve.wait_ge(dve_step, step.n)
                if rms:
                    step(nc.vector.tensor_tensor(shift[:], mv[:, :, 0], mv[:, :, 0], ALU.mult))
                    step(nc.vector.tensor_tensor(shift[:], shift[:], mv[:, :, 1], ALU.add))
                    nc.vector.tensor_scalar(var[:], shift[:], eps, None, ALU.add).then_inc(var_ready, 1)
                else:
                    nc.vector.tensor_scalar(var[:], mv[:, :, 1], eps, None, ALU.add).then_inc(var_ready, 1)
                dve.wait_ge(sd_ready, 1)
                step(nc.vector.reciprocal(rstd[:], sd[:]))
                for t in range(NT):
                    if rms:
                        step(nc.vector.tensor_scalar(xn[:, t, :], X[:, t, :], rstd[:, t:t + 1], None, ALU.mult))
                        nc.vector.tensor_tensor(xn[:, t, :], xn[:, t, :], w[:, :], ALU.mult).then_inc(rows_ready, 1)
                    else:
                        nc.vector.tensor_scalar(xn[:, t, :], X[:, t, :], mv[:, t, 0:1], rstd[:, t:t + 1],
                                                ALU.subtract, ALU.mult).then_inc(rows_ready, 1)
                if xnT is not None:
                    dve.wait_ge(turned, 1)
                    nc.vector.tensor_copy(xnT[:, :, :], psT[:, :, :]).then_inc(stored, 1)

            @block.scalar
            def _(act):
                act.wait_ge(var_ready, 1)
                nc.scalar.activation(sd[:], var[:], ACT.Sqrt).then_inc(sd_ready, 1)

            @block.tensor
            def _(pe):
                if xnT is None:
                    return
                for t in range(NT):
                    pe.wait_ge(rows_ready, t + 1)
                    for k in range(KC):
                        last = nc.tensor.transpose(psT[:, k, t * P:(t + 1) * P], xn[:, t, k * P:(k + 1) * P], K["ident"])
                last.then_inc(turned, 1)


def gemms(nc, K, jobs, ring=4):
    with pool(nc, f"gem{nc.next_id()}") as p:
        banks = p.ps("banks", [P, ring, 512])
        turn = [sum(1 for j in jobs[:n] if j[4] == jobs[n][4]) for n in range(len(jobs))]
        with stage(nc, "product_ready", "dve_took", "act_took", "dve_step", "act_step") as \
                (block, product_ready, dve_took, act_took, dve_step, act_step):
            took = {"v": dve_took, "s": act_took}

            def view(n):
                return banks[0:jobs[n][0], n % ring, 0:jobs[n][1]]

            @block.tensor
            def _(pe):
                for n, (_, _, terms, _, _) in enumerate(jobs):
                    if n >= ring:
                        pe.wait_ge(took[jobs[n - ring][4]], turn[n - ring] + 1)
                    for i, term in enumerate(terms):
                        if term[0] == "turn":
                            _, rows, at = term
                            last = nc.tensor.transpose(view(n)[:, at:at + rows.shape[0]], rows, K["ident"])
                        elif len(term) > 2:
                            lhsT, rhs, at, first, final = term
                            last = nc.tensor.matmul(view(n)[:, at:at + rhs.shape[1]], lhsT, rhs, start=first, stop=final)
                        else:
                            last = nc.tensor.matmul(view(n), *term, start=i == 0, stop=i == len(terms) - 1)
                    last.then_inc(product_ready, 1)

            @block.vector
            def _(dve):
                step = Steps(dve, dve_step)
                for n, job in enumerate(jobs):
                    if job[4] == "v":
                        dve.wait_ge(product_ready, n + 1)
                        job[3](view(n), step).then_inc(dve_took, 1)

            @block.scalar
            def _(act):
                step = Steps(act, act_step)
                for n, job in enumerate(jobs):
                    if job[4] == "s":
                        act.wait_ge(product_ready, n + 1)
                        job[3](view(n), step).then_inc(act_took, 1)


def vcopy(nc, dst):
    return lambda ps, step: nc.vector.tensor_copy(dst, ps)


def scopy(nc, dst):
    return lambda ps, step: nc.scalar.copy(dst, ps)


def vadd(nc, dst, other):
    return lambda ps, step: nc.vector.tensor_tensor(dst, ps, other, ALU.add)


def vbias(nc, dst, bias):
    return lambda ps, step: nc.vector.tensor_scalar(dst, ps, bias, None, ALU.add)


def sbias(nc, dst, bias):
    return lambda ps, step: nc.scalar.activation(dst, ps, ACT.Identity, bias=bias)


def project_T(W, n_out, xT, evac, engine, cols=NTOK, kc=KC):
    return [(P, cols, [(W[:, k, m * P:(m + 1) * P], xT[:, k, 0:cols]) for k in range(kc)], evac(m), engine)
            for m in range(n_out // P)]


def project_rows(W, n_out, xT, evac, engine, bias=None, tiles=NT, kc=KC, ones=None):
    extra = [(ones, bias)] if bias is not None else []
    return [(P, n_out, [(xT[:, k, t * P:(t + 1) * P], W[:, k, 0:n_out]) for k in range(kc)] + extra, evac(t), engine)
            for t in range(tiles)]


def over_heads(x, nh):
    return x.unsqueeze(1).to_broadcast([P, nh, x.shape[1]])


BF16 = mybir.dt.bfloat16
Q_PARTS = (0, 0, 0, 1, 1, 2)
K_PARTS = (0, 1, 2, 0, 1, 0)
D = C // H
STACK = 6 * D
SHIFT = STACK
PLAIN_ROWS = STACK + 3


def store_parts(nc, K, jobs, SLOTS=6, pool_engine=()):
    with pool(nc, f"prt{nc.next_id()}") as p:
        RING = 4
        banks = p.ps("banks", [P, RING, 512])
        left = p.sb("left", [P, 2, 512])
        parts = p.sb("parts", [P, SLOTS, 3, 512], BF16)
        with stage(nc, "product_ready", "first_ready", "rest_ready", "second_ready", "third_ready", "pool_done",
                   *[f"stored{i}" for i in range(SLOTS)]) as \
                (block, product_ready, first_ready, rest_ready, second_ready, third_ready, pool_done, *stored):
            @block.tensor
            def _(pe):
                for n, (m, w, terms, _, _) in enumerate(jobs):
                    if n >= RING:
                        pe.wait_ge(rest_ready, n - RING + 1)
                    for i, term in enumerate(terms):
                        if term[0] == "turn":
                            _, rows, at = term
                            last = nc.tensor.transpose(banks[0:m, n % RING, at:at + rows.shape[0]], rows, K["ident"])
                        else:
                            last = nc.tensor.matmul(banks[0:m, n % RING, 0:w], *term, start=i == 0, stop=i == len(terms) - 1)
                    last.then_inc(product_ready, 1)

            @block.scalar
            def _(act):
                def second(n):
                    m, w = jobs[n][0:2]
                    act.wait_ge(rest_ready, n + 1)
                    nc.scalar.copy(parts[0:m, n % SLOTS, 1, 0:w], left[0:m, n % 2, 0:w]).then_inc(second_ready, 1)

                for n, (m, w, _, bias, _) in enumerate(jobs):
                    act.wait_ge(product_ready, n + 1)
                    if n >= SLOTS:
                        act.wait_ge(stored[n % SLOTS], 16 * (n // SLOTS))
                    dst, src = parts[0:m, n % SLOTS, 0, 0:w], banks[0:m, n % RING, 0:w]
                    if bias is None:
                        nc.scalar.copy(dst, src).then_inc(first_ready, 1)
                    else:
                        nc.scalar.activation(dst, src, ACT.Identity, bias=bias).then_inc(first_ready, 1)
                    if n:
                        second(n - 1)
                second(len(jobs) - 1)

            @block.vector
            def _(dve):
                def third(n):
                    m, w = jobs[n][0:2]
                    dve.wait_ge(second_ready, n + 1)
                    nc.vector.tensor_tensor(parts[0:m, n % SLOTS, 2, 0:w], left[0:m, n % 2, 0:w], parts[0:m, n % SLOTS, 1, 0:w],
                                            ALU.subtract).then_inc(third_ready, 1)

                for n, (m, w, _, bias, _) in enumerate(jobs):
                    dve.wait_ge(first_ready, n + 1)
                    if n >= 2:
                        dve.wait_ge(third_ready, n - 1)
                    dst, src, first = left[0:m, n % 2, 0:w], banks[0:m, n % RING, 0:w], parts[0:m, n % SLOTS, 0, 0:w]
                    if bias is None:
                        nc.vector.tensor_tensor(dst, src, first, ALU.subtract).then_inc(rest_ready, 1)
                    else:
                        nc.vector.scalar_tensor_tensor(out=dst, in0=src, scalar=bias, in1=first, op0=ALU.add, op1=ALU.subtract).then_inc(rest_ready, 1)
                    if n:
                        third(n - 1)
                third(len(jobs) - 1)

            @block.gpsimd
            def _(gp):
                for n, one in enumerate(pool_engine):
                    one().then_inc(pool_done, 1)
                    gp.wait_ge(pool_done, n + 1)

            @block.sync
            def _(sp):
                for n, (m, w, _, _, dst) in enumerate(jobs):
                    sp.wait_ge(third_ready, n + 1)
                    sp.dma_start(dst, parts[0:m, n % SLOTS, :, 0:w]).then_inc(stored[n % SLOTS], 16)
                for i in range(min(SLOTS, len(jobs))):
                    sp.wait_ge(stored[i], 16 * len(range(i, len(jobs), SLOTS)))


def key_pieces(dst, scratch, h, cols):
    return [(dst[i * D:(i + 1) * D], scratch[part, h * D:(h + 1) * D, cols]) for i, part in enumerate(K_PARTS)]


def stack_pieces(dst, scratch, parts, cols=slice(0, NTOK), c=0, chunks=1):
    return [(dst[i * D:(i + 1) * D], scratch[part, :, cols].rearrange("(h c d) n -> c d h n", c=chunks, d=D)[c])
            for i, part in enumerate(parts)]


def split_maxima(nc, step, neg, rest, m):
    step(nc.gpsimd.tensor_copy(m[:, :, 0], neg))
    step(nc.gpsimd.tensor_tensor(rest, neg, m[:, :, 0], ALU.subtract))
    step(nc.gpsimd.tensor_copy(m[:, :, 1], rest))
    return nc.gpsimd.tensor_tensor(m[:, :, 2], rest, m[:, :, 1], ALU.subtract)


class LongItem:
    heads = 1

    def __init__(self, n, key_tiles, q, k, v):
        self.n, self.key_tiles, self.q, self.k, self.v = n, key_tiles, q, k, v
        self.full = key_tiles // 8
        self.tail = key_tiles % 8
        self.units = -(-key_tiles // 4)
        self.parts = self.full + (1 if self.tail else 0)

    def maxima(self, s):
        if s < TB * self.full:
            t, c = s // self.full, s % self.full
            q = self.q[:, t * P:(t + 1) * P]
            mms = [(i * 512, q, self.k[:, c * 1024 + i * 512:c * 1024 + (i + 1) * 512]) for i in range(2)]
            return mms, (lambda ps: ps, lambda parts: parts[:, t, c:c + 1])
        w = self.tail * P
        mms = [(t * 512, self.q[:, t * P:(t + 1) * P], self.k[:, self.full * 1024:self.full * 1024 + w]) for t in range(TB)]
        return mms, (lambda ps: ps.rearrange("p (t n) -> p t n", t=TB)[:, :, 0:w], lambda parts: parts[:, :, self.full])

    def tiles(self, s):
        return range(4 * s, min(4 * s + 4, self.key_tiles))

    def scores(self, s):
        return [(i * T, self.k[:, kt * P:(kt + 1) * P], self.q) for i, kt in enumerate(self.tiles(s))]

    def values(self, s):
        return [(i * T, self.v(kt), kt % 4, kt < 4, kt >= self.key_tiles - 4) for i, kt in enumerate(self.tiles(s))]

    def combine(self):
        return [("comb", self.n % 4)]


def long_attention(nc, K, items, outs, scale, key_loads, next_loads, lead=2):
    N, n = len(items), items[0].units
    G = N * n
    COLS = items[0].heads * TB
    PARTS = items[0].parts
    GROUP = 4 // items[0].heads
    R = items[0].q.shape[0]
    SLOTS, NP, MR, NR = 3, 3, 4, 2
    ahead = n + lead
    order = [("max", a) for a in range(min(ahead, G))]
    for g in range(G):
        if g + ahead < G:
            order.append(("max", g + ahead))
        order.append(("score", g))
    place = {unit: i for i, unit in enumerate(order)}
    with pool(nc, f"sta{nc.next_id()}") as p:
        psS = p.ps("psS", [P, SLOTS, 1024])
        psO = p.ps("psO", [P, 2, T])
        psM = p.ps("psM", [P, 512])
        parts = p.sb("parts", [P, 2, COLS, PARTS])
        neg = p.sb("neg", [P, 2, COLS])
        rest = p.sb("rest", [P, COLS])
        split = p.sb("split", [P, MR, COLS, 3], BF16)
        probs = p.sb("probs", [P, NP, 1024])
        OT = p.sb("OT", [P, T])
        num = p.sb("num", [P, NR, T])
        den = p.sb("den", [P, NR, T])
        with stage(nc, "pool_step", "unit_ready", "max_taken", "max_ready", "max_split", "max_turned", "shifted", "probs_ready",
                   "probs_used", "o_copied", "combined", "n_copied", "sums_ready", "sums_read", "inverted", "out_ready",
                   "next_loaded", "keys0", "keys1", "keys2") as \
                (block, pool_step, unit_ready, max_taken, max_ready, max_split, max_turned, shifted, probs_ready,
                 probs_used, o_copied, combined, n_copied, sums_ready, sums_read, inverted, out_ready,
                 next_loaded, *keys):

            @block.sync
            def _(sp):
                for i in range(N):
                    if i >= 3:
                        sp.wait_ge(unit_ready, place["score", (i - 2) * n - 1] + 1)
                    for dst, src in key_loads(i):
                        sp.dma_start(dst, src).then_inc(keys[i % 3], 16)
                    if i == 2:
                        for dst, src in next_loads:
                            sp.dma_start(dst, src).then_inc(next_loaded, 16)
                sp.wait_ge(next_loaded, 16 * len(next_loads))

            @block.tensor
            def _(pe):
                def free_slot(at):
                    if at >= SLOTS:
                        kind, u = order[at - SLOTS]
                        pe.wait_ge(max_taken if kind == "max" else probs_ready, u + 1)

                def emit(kind, u):
                    at = place[kind, u]
                    free_slot(at)
                    item, s = items[u // n], u % n
                    mms = item.maxima(s)[0] if kind == "max" else item.scores(s)
                    for col, lhsT, rhs in mms:
                        last = nc.tensor.matmul(psS[:, at % SLOTS, col:col + rhs.shape[1]], lhsT, rhs, start=True, stop=True)
                    last.then_inc(unit_ready, 1)

                def maxima(u):
                    if u % n == 0:
                        i = u // n
                        pe.wait_ge(keys[i % 3], 16 * len(key_loads(i)) * (i // 3 + 1))
                    emit("max", u)

                def values(u):
                    pe.wait_ge(probs_ready, u + 1)
                    for col, v, group, first, final in items[u // n].values(u % n):
                        last = nc.tensor.matmul(psO[32 * group:32 * group + 32, 0, :], v, probs[:, u % NP, col:col + T],
                                                start=first, stop=final)
                    last.then_inc(probs_used, 1)

                def combine(h):
                    pe.wait_ge(o_copied, h + 1)
                    for comb, row in items[h].combine():
                        last = nc.tensor.matmul(psO[32 * row:32 * row + 32, 1, :], K[comb], OT[:], start=True, stop=True)
                    last.then_inc(combined, 1)
                    if (h + 1) % GROUP == 0:
                        pe.wait_ge(n_copied, (h + 1) // GROUP)

                def sums(g):
                    nc.tensor.matmul(psM[:, 0:T], K["sel32"], num[:, g % NR, :], start=True, stop=True).then_inc(sums_ready, 1)

                def turn(h):
                    pe.wait_ge(max_split, h + 1)
                    if (h - 1) // GROUP > 0:
                        pe.wait_ge(sums_read, (h - 1) // GROUP)
                    if h:
                        pe.wait_ge(shifted, h)
                    for c in range(COLS):
                        last = nc.tensor.matmul(psM[SHIFT:SHIFT + 3, c * P:(c + 1) * P], split[:, h % MR, c, :], K["ident16"], start=True, stop=True)
                    last.then_inc(max_turned, 1)

                for u in range(min(ahead, G)):
                    maxima(u)
                turn(0)
                for g in range(G):
                    if g + ahead < G:
                        maxima(g + ahead)
                    if g % n == 0:
                        pe.wait_ge(shifted, g // n + 1)
                    if g > n and (g - 2) % n == 0 and (g - 2) // n % GROUP == 0:
                        sums((g - 2) // n // GROUP - 1)
                    emit("score", g)
                    if g >= 1:
                        h = (g - 1) // n
                        if (g - 1) % n == 0 and h:
                            combine(h - 1)
                        values(g - 1)
                    if (g + 1) % n == 0 and (g + 1) // n < N:
                        turn((g + 1) // n)
                values(G - 1)
                combine(N - 1)
                sums(N // GROUP - 1)

            @block.vector
            def _(dve):
                def take(u):
                    at = place["max", u]
                    dve.wait_ge(unit_ready, at + 1)
                    item = items[u // n]
                    view, into = item.maxima(u % n)[1]
                    src = psS[:, at % SLOTS, :]
                    nc.vector.tensor_reduce(into(parts[:, u // n % 2]), view(src), AX.X, ALU.max).then_inc(max_taken, 1)
                    if (u + 1) % n == 0:
                        h = u // n
                        dve.wait_ge(max_taken, u + 1)
                        if h >= 2:
                            dve.wait_ge(max_split, h - 1)
                        nc.vector.tensor_reduce(neg[:, h % 2, :], parts[:, h % 2], AX.X, ALU.max, negate=True).then_inc(max_ready, 1)

                def shift(h):
                    dve.wait_ge(max_turned, h + 1)
                    nc.vector.tensor_copy(items[h].q[SHIFT:SHIFT + 3, :], psM[SHIFT:SHIFT + 3, 0:COLS * P]).then_inc(shifted, 1)

                def invert(g):
                    dve.wait_ge(sums_read, g + 1)
                    nc.vector.reciprocal(den[:, g % NR, :], den[:, g % NR, :]).then_inc(inverted, 1)

                for u in range(min(ahead, G)):
                    take(u)
                shift(0)
                for g in range(G):
                    if g + ahead < G:
                        take(g + ahead)
                    if g > n and (g - 2) % n == 0 and (g - 2) // n % GROUP == 0:
                        invert((g - 2) // n // GROUP - 1)
                    if (g + 1) % n == 0 and (g + 1) // n < N:
                        shift((g + 1) // n)
                invert(N // GROUP - 1)

            @block.scalar
            def _(act):
                def copy_o(h):
                    act.wait_ge(probs_used, (h + 1) * n)
                    if h:
                        act.wait_ge(combined, h)
                    nc.scalar.copy(OT[:], psO[:, 0, :]).then_inc(o_copied, 1)

                def copy_numerators(g):
                    act.wait_ge(combined, (g + 1) * GROUP)
                    if g >= NR:
                        act.wait_ge(out_ready, g - NR + 1)
                    nc.scalar.copy(num[:, g % NR, :], psO[:, 1, :]).then_inc(n_copied, 1)

                def copy_denominators(g):
                    act.wait_ge(sums_ready, g + 1)
                    nc.scalar.copy(den[:, g % NR, :], psM[:, 0:T]).then_inc(sums_read, 1)

                for g in range(G):
                    h = (g - 1) // n
                    ends = g >= 1 and (g - 1) % n == 0 and h
                    if ends:
                        copy_o(h - 1)
                    if g > n and (g - 2) % n == 0 and (g - 2) // n % GROUP == 0:
                        copy_denominators((g - 2) // n // GROUP - 1)
                    if g >= NP:
                        act.wait_ge(probs_used, g - NP + 1)
                    cols = T * len(items[g // n].values(g % n))
                    act.wait_ge(unit_ready, place["score", g] + 1)
                    nc.scalar.activation(probs[:, g % NP, 0:cols], psS[:, place["score", g] % SLOTS, 0:cols],
                                         ACT.Exp, scale=scale).then_inc(probs_ready, 1)
                    if ends and h % GROUP == 0:
                        copy_numerators(h // GROUP - 1)
                copy_o(N - 1)
                copy_numerators(N // GROUP - 1)
                copy_denominators(N // GROUP - 1)

            @block.gpsimd
            def _(gp):
                step = Steps(gp, pool_step)

                def divide(g):
                    gp.wait_ge(inverted, g + 1)
                    nc.gpsimd.tensor_tensor(outs[g], num[:, g % NR, :], den[:, g % NR, :], ALU.mult).then_inc(out_ready, 1)

                for h in range(N):
                    gp.wait_ge(max_ready, h + 1)
                    if h >= MR:
                        gp.wait_ge(max_turned, h - MR + 1)
                    split_maxima(nc, step, neg[:, h % 2, :], rest[:], split[:, h % MR, :, :]).then_inc(max_split, 1)
                    gp.wait_ge(max_split, h + 1)
                    if h >= GROUP + 2 and (h - 2) % GROUP == 0:
                        divide((h - 2) // GROUP - 1)
                for g in range((N - 3) // GROUP, N // GROUP):
                    divide(g)
                gp.wait_ge(out_ready, N // GROUP)


def short_attention(nc, K, q, k, values, outs, scale, mask, HP=2 * D, next_loads=()):
    CHUNKS = HP // (2 * D)
    PAIRS = H // 2
    N = B * PAIRS
    GROUP = P // HP // 2
    SLOTS, NP, MR, NR, LEAD = 3, 3, 4, 4, 3
    order = [("max", u) for u in range(LEAD)]
    for u in range(N):
        if u + LEAD < N:
            order.append(("max", u + LEAD))
        order.append(("score", u))
    place = {unit: i for i, unit in enumerate(order)}
    heads = [[(u // PAIRS, u % PAIRS * 2 + j) for j in range(2)] for u in range(N)]

    def products(left, right, masks, u):
        out = []
        for j, (b, h) in enumerate(heads[u]):
            if mask:
                out.append((j * 512, K["ident16"], masks, True, False))
            for t in range(TB):
                for c in range(CHUNKS):
                    out.append((j * 512 + t * T, left(c, b, h)[:, t * P:(t + 1) * P], right(c, b, h), not mask and c == 0,
                                c == CHUNKS - 1 and (not mask or t == TB - 1)))
        return out

    with pool(nc, f"sht{nc.next_id()}") as p:
        psS = p.ps("psS", [P, SLOTS, 1024])
        psO = p.ps("psO", [P, 512])
        psM = p.ps("psM", [P, 512])
        neg = p.sb("neg", [P, 2, 2 * TB])
        rest = p.sb("rest", [P, 2 * TB])
        split = p.sb("split", [P, MR, 2 * TB, 3], BF16)
        probs = p.sb("probs", [P, NP, 1024])
        num = p.sb("num", [P, NR, T])
        den = p.sb("den", [P, NR, T])
        with stage(nc, "pool_step", "unit_ready", "max_taken", "max_split", "max_turned", "shifted", "probs_ready",
                   "probs_used", "n_copied", "sums_ready", "sums_read", "inverted", "out_ready", "next_loaded") as \
                (block, pool_step, unit_ready, max_taken, max_split, max_turned, shifted, probs_ready,
                 probs_used, n_copied, sums_ready, sums_read, inverted, out_ready, next_loaded):
            @block.sync
            def _(sp):
                for dst, src in next_loads:
                    sp.dma_start(dst, src).then_inc(next_loaded, 16)
                if next_loads:
                    sp.wait_ge(next_loaded, 16 * len(next_loads))

            @block.tensor
            def _(pe):
                def emit(kind, u):
                    at = place[kind, u]
                    if at >= SLOTS:
                        before, v = order[at - SLOTS]
                        pe.wait_ge(max_taken if before == "max" else probs_ready, v + 1)
                    for col, lhsT, rhs, first, final in (products(q, k, K["mask16_q"], u) if kind == "max" else products(k, q, K["mask16_k"], u)):
                        last = nc.tensor.matmul(psS[:, at % SLOTS, col:col + rhs.shape[-1]], lhsT, rhs, start=first, stop=final)
                    last.then_inc(unit_ready, 1)

                def turn(u):
                    pe.wait_ge(max_split, u + 1)
                    if u:
                        pe.wait_ge(shifted, u)
                    if (u - 2) // GROUP > 0:
                        pe.wait_ge(sums_read, (u - 2) // GROUP)
                    for c in range(2 * TB):
                        last = nc.tensor.matmul(psM[SHIFT:SHIFT + 3, c * P:(c + 1) * P], split[:, u % MR, c, :], K["ident16"], start=True, stop=True)
                    last.then_inc(max_turned, 1)

                def values_product(u):
                    pe.wait_ge(probs_ready, u + 1)
                    if u % GROUP == 0 and u:
                        pe.wait_ge(n_copied, u // GROUP)
                    for kt in range(TB):
                        for j, (b, h) in enumerate(heads[u]):
                            row = HP * (h % (P // HP))
                            last = nc.tensor.matmul(psO[row:row + HP, 0:T], values(b, h, kt), probs[:, u % NP, j * 512 + kt * T:j * 512 + (kt + 1) * T],
                                                    start=kt == 0, stop=kt == TB - 1)
                    last.then_inc(probs_used, 1)

                def sums(g):
                    pe.wait_ge(n_copied, g + 1)
                    nc.tensor.matmul(psM[:, 0:T], K["sel"][HP], num[:, g % NR, :], start=True, stop=True).then_inc(sums_ready, 1)

                for u in range(LEAD):
                    emit("max", u)
                turn(0)
                for u in range(N):
                    if u + LEAD < N:
                        emit("max", u + LEAD)
                    pe.wait_ge(shifted, u + 1)
                    if u >= 2 and (u - 1) % GROUP == 0:
                        sums((u - 1) // GROUP - 1)
                    emit("score", u)
                    if u:
                        values_product(u - 1)
                    if u + 1 < N:
                        turn(u + 1)
                if (N - 1) % GROUP == 0:
                    sums((N - 1) // GROUP - 1)
                values_product(N - 1)
                sums(N // GROUP - 1)

            @block.vector
            def _(dve):
                def take(u):
                    dve.wait_ge(unit_ready, place["max", u] + 1)
                    if u >= 2:
                        dve.wait_ge(max_split, u - 1)
                    nc.vector.tensor_reduce(neg[:, u % 2, :], psS[:, place["max", u] % SLOTS, :].rearrange("p (i n) -> p i n", n=T),
                                            AX.X, ALU.max, negate=True).then_inc(max_taken, 1)

                def shift(u):
                    dve.wait_ge(max_turned, u + 1)
                    for j, (b, h) in enumerate(heads[u]):
                        last = nc.vector.tensor_copy(q(0, b, h)[SHIFT:SHIFT + 3, :], psM[SHIFT:SHIFT + 3, j * T:(j + 1) * T])
                    last.then_inc(shifted, 1)

                def invert(g):
                    dve.wait_ge(sums_read, g + 1)
                    nc.vector.reciprocal(den[:, g % NR, :], den[:, g % NR, :]).then_inc(inverted, 1)

                for u in range(LEAD):
                    take(u)
                shift(0)
                inverse = 0
                for u in range(N):
                    if u + LEAD < N:
                        take(u + LEAD)
                    if u + 1 < N and GROUP > 1:
                        shift(u + 1)
                    if u >= 3 and (u - 2) % GROUP == 0:
                        invert((u - 2) // GROUP - 1)
                        inverse += 1
                    if u + 1 < N and GROUP == 1:
                        shift(u + 1)
                for g in range(inverse, N // GROUP):
                    invert(g)

            @block.scalar
            def _(act):
                def copy_numerators(g):
                    act.wait_ge(probs_used, (g + 1) * GROUP)
                    if g >= NR:
                        act.wait_ge(out_ready, g - NR + 1)
                    nc.scalar.copy(num[:, g % NR, :], psO[:, 0:T]).then_inc(n_copied, 1)

                def copy_denominators(g):
                    act.wait_ge(sums_ready, g + 1)
                    nc.scalar.copy(den[:, g % NR, :], psM[:, 0:T]).then_inc(sums_read, 1)

                for u in range(N):
                    ends = u >= 2 and (u - 1) % GROUP == 0
                    if ends:
                        copy_numerators((u - 1) // GROUP - 1)
                        copy_denominators((u - 1) // GROUP - 1)
                    if u >= NP:
                        act.wait_ge(probs_used, u - NP + 1)
                    act.wait_ge(unit_ready, place["score", u] + 1)
                    nc.scalar.activation(probs[:, u % NP, :], psS[:, place["score", u] % SLOTS, :], ACT.Exp, scale=scale).then_inc(probs_ready, 1)
                if (N - 1) % GROUP == 0:
                    copy_numerators((N - 1) // GROUP - 1)
                    copy_denominators((N - 1) // GROUP - 1)
                copy_numerators(N // GROUP - 1)
                copy_denominators(N // GROUP - 1)

            @block.gpsimd
            def _(gp):
                step = Steps(gp, pool_step)

                def divide(g):
                    gp.wait_ge(inverted, g + 1)
                    nc.gpsimd.tensor_tensor(outs(g), num[:, g % NR, :], den[:, g % NR, :], ALU.mult).then_inc(out_ready, 1)

                for u in range(N):
                    gp.wait_ge(max_taken, u + 1)
                    if u >= MR:
                        gp.wait_ge(max_turned, u - MR + 1)
                    split_maxima(nc, step, neg[:, u % 2, :], rest[:], split[:, u % MR, :, :]).then_inc(max_split, 1)
                    gp.wait_ge(max_split, u + 1)
                    if u >= GROUP + 6 and (u - 6) % GROUP == 0:
                        divide((u - 6) // GROUP - 1)
                for g in range((N - 7) // GROUP, N // GROUP):
                    divide(g)
                gp.wait_ge(out_ready, N // GROUP)


class Stacks:

    def __init__(self, nc, p, name, chunks=1, rows=PLAIN_ROWS):
        self.nc, self.chunks, self.rows = nc, chunks, rows
        self.scratch = [nc.dram_tensor(f"{name}_{n}_parts", (3, H * D * chunks, NTOK), BF16, kind="Internal").ap() for n in "qk"]
        self.tiles = [[p.sb(f"{n}S{c}", [rows if c == 0 else STACK, H, NTOK], BF16) for c in range(chunks)] for n in "qk"]

    def into(self, which, m):
        return self.scratch[which][:, m * P:(m + 1) * P, :].rearrange("s p n -> p s n")

    def load(self, K, tables=None):
        nc = self.nc
        qS, kS = self.tiles[0][0], self.tiles[1][0]
        pairs = [pair for which, parts in enumerate((Q_PARTS, K_PARTS)) for c in range(self.chunks)
                 for pair in stack_pieces(self.tiles[which][c], self.scratch[which], parts, c=c, chunks=self.chunks)]
        if tables is None:
            pairs += [(qS[SHIFT:], K["zeros_dram"].rearrange("s (h n) -> s h n", h=H)),
                      (kS[SHIFT:], K["ones_dram"].rearrange("s (h n) -> s h n", h=H))]
            load(nc, pairs)
        else:
            m = self.rows - SHIFT
            seqs = [slice(b * T, (b + 1) * T) for b in range(B)]
            load(nc, pairs,
                 [lambda s=s: nc.vector.tensor_copy(qS[SHIFT:, :, s], tables[SHIFT:self.rows, 0:H, :]) for s in seqs]
                 + [lambda s=s: nc.vector.tensor_copy(kS[SHIFT:, :, s], tables[SHIFT:self.rows, H:H + 1, :].to_broadcast([m, H, T])) for s in seqs])

    def attend(self, K, v, attT, scale, mask, next_loads=()):
        HP = 2 * D * self.chunks
        per = P // HP
        groups = H // per
        short_attention(self.nc, K,
                        lambda c, b, h: self.tiles[0][c][:, h, b * T:(b + 1) * T], lambda c, b, h: self.tiles[1][c][:, h, b * T:(b + 1) * T],
                        lambda b, h, kt: v[:, b * TB + kt, h * HP:(h + 1) * HP],
                        lambda g: attT[:, g % groups, g // groups * T:(g // groups + 1) * T], scale, mask, HP, next_loads)


class Weights:

    def __init__(self, nc, p, name, arrays, specs, also=(), vector=None, pool_engine=None, now=True):
        self.specs = specs[name]
        n = sum(int(np.prod(shape[1:])) for _, shape in self.specs.values())
        self.tile = p.sb(name + "_weights", [P, n])
        cut = [n * i // 4 for i in range(5)]
        self.loads = [(self.tile[:, a:b], arrays[name][:, a:b]) for a, b in zip(cut, cut[1:]) if b > a]
        if now:
            load(nc, self.loads + list(also), vector, pool_engine)

    def __getitem__(self, key):
        at, shape = self.specs[key]
        n = int(np.prod(shape[1:]))
        view = self.tile[0:shape[0], at:at + n]
        if len(shape) == 3:
            view = view.rearrange("p (k n) -> p k n", k=shape[1])
        return view


def add_to_residual(nc, K, X, W, attT, kc, bias):
    gemms(nc, K, project_rows(W, C, attT, lambda t: vadd(nc, X[:, t, :], X[:, t, :]), "v",
                           bias=bias, kc=kc, ones=K["ones"][0:1, :]))


def alibi_attention(nc, K, X, arrays, specs):
    with pool(nc, "l0a") as p:
        xn = p.sb("xn", [P, NT, C])
        xnT = p.sb("xnT", [P, KC, NTOK])
        v = p.sb("v", [P, NT, 512])
        attT = p.sb("attT", [P, 4, NTOK])
        tables = p.sb("tables", [ALIBI_ROWS, H + 1, T])
        stacks = Stacks(nc, p, "L0_attn", rows=ALIBI_ROWS)
        w = Weights(nc, p, "L0_attn", arrays, specs, [(tables[SHIFT:], arrays["alibi"])])
        normalize(nc, K, X, xn, xnT, 1e-5)
        store_parts(nc, K, part_jobs(w["q"], C, xnT, w["bq"], stacks, 0) + part_jobs(w["k"], C, xnT, w["bk"], stacks, 1))
        gemms(nc, K, project_rows(w["v"], 512, xnT, lambda t: scopy(nc, v[:, t, :]), "s", bias=w["bv"], ones=K["ones"][0:1, :]))
        stacks.load(K, tables)
        stacks.attend(K, v, attT, 0.25, True)
        add_to_residual(nc, K, X, w["o"], attT, 4, w["bo"])


ALIBI_ROWS = PLAIN_ROWS + 6


def part_jobs(W, n_out, xT, bias, stacks, which, kc=KC, extra=None):
    return [(P, NTOK, [(W[:, k, m * P:(m + 1) * P], xT[:, k, :]) for k in range(kc)] + ([extra(m)] if extra else []),
             None if bias is None else bias[:, m:m + 1], stacks.into(which, m)) for m in range(n_out // P)]


def turn_all(K, rows, tiles, width, evac, engine):
    return [(P, P * min(4, tiles), [("turn", rows[:, t0 + t, k * P:(k + 1) * P], t * P) for t in range(min(4, tiles))],
             evac(k, t0), engine) for t0 in range(0, tiles, 4) for k in range(width // P)]


def cross_attention(nc, K, X, arrays, specs, name):
    raw = name == "L0_xattn"
    KT = ST + (TB if raw else 0)
    scrq = nc.dram_tensor(f"{name}_queries", (3, C, NTOK), BF16, kind="Internal").ap()
    scrk = nc.dram_tensor(f"{name}_keys", (3, C, KT * P), BF16, kind="Internal").ap()
    with pool(nc, name) as p:
        V = p.sb("V", [P, KT, 512])
        V4 = V[:].rearrange("p t (h d) -> p t h d", h=H)
        cx = p.sb("cx", [P, ST, C])

        def context_loads(b):
            ctx_b = arrays["ctx"][b].rearrange("(p n) c -> p n c", p=P)
            return [(cx[:, n:n + 8, :], ctx_b[:, n:n + 8, :]) for n in range(0, ST, 8)]

        half = KT * 5 // 8
        w = Weights(nc, p, name, arrays, specs, context_loads(0),
                    [lambda: nc.vector.memset(V[:, 0:half], 0.0), lambda: nc.vector.memset(V4[:, 0:half, :, D], 1.0)],
                    [lambda: nc.gpsimd.memset(V[:, half:], 0.0), lambda: nc.gpsimd.memset(V4[:, half:, :, D], 1.0)])
        attT = p.sb("attT", [P, 4 * NTOK])
        qS = p.sb("qS", [PLAIN_ROWS, H, T], BF16)
        oc = p.sb("oc", [P, 4, T])
        with pool(nc, name + "q") as p1:
            xn = p1.sb("xn", [P, NT, C])
            xnT = p1.sb("xnT", [P, KC, NTOK])
            normalize(nc, K, X, xn, xnT, 1e-5)
            store_parts(nc, K, [(P, NTOK, [(w["q"][:, k, m * P:(m + 1) * P], xnT[:, k, :]) for k in range(KC)], w["bq"][:, m:m + 1],
                                 scrq[:, m * P:(m + 1) * P, :].rearrange("s p n -> p s n")) for m in range(KC)])
        with turns(nc, B) as b:
            with pool(nc, name + "b") as p1:
                loads = [(qS[SHIFT:], K["zeros_dram"][:, 0:H * T].rearrange("s (h n) -> s h n", h=H))]
                if raw:
                    side = p1.sb("side", [P, TB, C])
                    sideT = p1.sb("sideT", [P, KC, T])
                    loads.append((side[:], arrays["fside"][bass.ds(b, 1)].rearrange("o (t p) c -> p (o t) c", p=P)))
                cols = bass.ds(b * T, T)
                load(nc, loads + stack_pieces(qS, scrq, Q_PARTS, cols))

                def keys_at(k, n, m):
                    return scrk[:, k * P:(k + 1) * P, n * P:(n + m) * P].rearrange("s p n -> p s n")

                def into_values(t):
                    return lambda ps, step: nc.vector.tensor_tensor(V4[:, t, :, 0:D], ps.rearrange("p (h d) -> p h d", h=H),
                                                                    w["bv"].rearrange("p (h d) -> p h d", h=H), ALU.add)

                if raw:
                    gemms(nc, K, turn_all(K, side, TB, C, lambda k, t0: vcopy(nc, sideT[:, k, :]), "v"))
                    gemms(nc, K, project_rows(w["v"], C, sideT, lambda t: into_values(ST + t), "v", tiles=TB))
                    def values_piece(t0):
                        s = slice(t0, t0 + 8)
                        return lambda: nc.gpsimd.tensor_copy(V4[:, s, :, 0:D], cx[:, s, :].rearrange("p t (h d) -> p t h d", h=H))

                    store_parts(nc, K, [(P, 512, [("turn", cx[:, n + t, k * P:(k + 1) * P], t * P) for t in range(4)], None, keys_at(k, n, 4))
                                        for n in range(0, ST, 4) for k in range(KC)]
                                + [(P, T, [(w["k"][:, k, m * P:(m + 1) * P], sideT[:, k, :]) for k in range(KC)], w["bk"][:, m:m + 1],
                                    keys_at(m, ST, TB)) for m in range(KC)],
                                pool_engine=[values_piece(t0) for t0 in range(0, ST, 8)])
                else:
                    cxT = p1.sb("cxT", [P, KC, S])
                    gemms(nc, K, [job for n in range(0, ST, 4) for job in (
                        (P, 512, [("turn", cx[:, n + t, 0:P], t * P) for t in range(4)], vcopy(nc, cxT[:, 0, n * P:(n + 4) * P]), "v"),
                        (P, 512, [("turn", cx[:, n + t, P:C], t * P) for t in range(4)], scopy(nc, cxT[:, 1, n * P:(n + 4) * P]), "s"))])
                    gemms(nc, K, project_rows(w["v"], C, cxT, into_values, "v", tiles=ST))
                    store_parts(nc, K, [(P, 512, [(w["k"][:, k, m * P:(m + 1) * P], cxT[:, k, n * P:(n + 4) * P]) for k in range(KC)],
                                         w["bk"][:, m:m + 1], keys_at(m, n, 4)) for n in range(0, ST, 4) for m in range(KC)], SLOTS=4)
            with pool(nc, name + "a") as p1:
                kst = [p1.sb(f"kst{i}", [PLAIN_ROWS, KT * P], BF16) for i in range(3)]
                items = [LongItem(h, KT, qS[:, h, :], kst[h % 3],
                                  lambda kt, h=h: V[:, kt, 32 * h:32 * h + 32]) for h in range(H)]
                long_attention(nc, K, items, [oc[:, g, :] for g in range(4)], 0.25,
                               lambda i: key_pieces(kst[i % 3], scrk, i, slice(0, KT * P)) + [(kst[i % 3][SHIFT:], K["ones_dram"][:, 0:KT * P])],
                               context_loads(B - 1))
            with stage(nc, "kept") as (block, kept):
                @block.vector
                def _(dve):
                    for g in range(4):
                        nc.vector.tensor_copy(attT[:, bass.ds(b * T + g * NTOK, T)], oc[:, g, :]).then_inc(kept, 1)
                    dve.wait_ge(kept, 4)
        add_to_residual(nc, K, X, w["o"], attT[:].rearrange("p (c n) -> p c n", c=4), 4, w["bo"])


def lora_attention(nc, K, X, arrays, specs):
    with pool(nc, "l2x") as p:
        xn = p.sb("xn", [P, NT, C])
        xnT = p.sb("xnT", [P, KC, NTOK])
        side = p.sb("side", [P, NT, C])
        sideT = p.sb("sideT", [P, KC, NTOK])
        v = p.sb("v", [P, NT, 512])
        attT = p.sb("attT", [P, 4, NTOK])
        stacks = Stacks(nc, p, "L2_xattn")
        lowq = p.sb("lowq", [16, NTOK])
        lowf = p.sb("lowf", [16, NTOK])
        lowp = p.sb("lowp", [16, NTOK])
        w = Weights(nc, p, "L2_xattn", arrays, specs,
                    [(side[:, t, :], arrays["ctx"][t // TB, (t % TB) * P:(t % TB + 1) * P, :]) for t in range(NT)])
        normalize(nc, K, X, xn, xnT, 1e-5)
        gemms(nc, K, turn_all(K, side, NT, C, lambda k, t0: vcopy(nc, sideT[:, k, :]), "v"))

        def low(dst, A, xT, kc):
            return (16, NTOK, [(A[:, k, :], xT[:, k, :]) for k in range(kc)],
                    lambda ps, step: nc.scalar.mul(dst[:], ps, 1.0 / 16.0), "s")

        gemms(nc, K, [low(lowq, w["Aq"], xnT, KC), low(lowf, w["Af"], sideT, KC)])
        store_parts(nc, K, part_jobs(w["q"], C, xnT, w["bq"], stacks, 0, extra=lambda m: (w["Bq"][:, 0, m * P:(m + 1) * P], lowq[:]))
                    + part_jobs(w["k"], C, sideT, w["bk"], stacks, 1, extra=lambda m: (w["Bk"][:, 0, m * P:(m + 1) * P], lowf[:])))
        gemms(nc, K, [(P, 512, [(sideT[:, k, t * P:(t + 1) * P], w["v"][:, k, :]) for k in range(KC)]
                       + [(lowf[:, t * P:(t + 1) * P], w["Bv"][:, 0, :]), (K["ones"][0:1, :], w["bv"])], scopy(nc, v[:, t, :]), "s")
                      for t in range(NT)])
        stacks.load(K)
        stacks.attend(K, v, attT, 0.25, True)
        gemms(nc, K, [low(lowp, w["Ap"], attT, 4)])
        gemms(nc, K, [(P, C, [(attT[:, k, t * P:(t + 1) * P], w["o"][:, k, :]) for k in range(4)]
                       + [(lowp[:, t * P:(t + 1) * P], w["Bp"][:, 0, :]), (K["ones"][0:1, :], w["bo"])],
                       vadd(nc, X[:, t, :], X[:, t, :]), "v") for t in range(NT)])


def complex_attention(nc, K, X, arrays, specs):
    with pool(nc, "l3a") as p:
        w = Weights(nc, p, "L3_attn", arrays, specs)
        xn = p.sb("xn", [P, NT, C])
        xnT = p.sb("xnT", [P, KC, NTOK])
        stacks = Stacks(nc, p, "L3_attn", chunks=2)
        v = p.sb("v", [P, NT, 1024])
        attT = p.sb("attT", [P, 8, NTOK])
        normalize(nc, K, X, xn, xnT, 1e-5)
        store_parts(nc, K, part_jobs(w["q"], 2 * C, xnT, None, stacks, 0) + part_jobs(w["k"], 2 * C, xnT, None, stacks, 1))
        gemms(nc, K, [(P, 512, [(xnT[:, k, t * P:(t + 1) * P], w["v"][:, k, n * 512:(n + 1) * 512]) for k in range(KC)]
                       + [(K["ones"][0:1, :], w["bv"][:, n * 512:(n + 1) * 512])], scopy(nc, v[:, t, n * 512:(n + 1) * 512]), "s")
                      for t in range(NT) for n in range(2)])
        stacks.load(K)
        stacks.attend(K, v, attT, 0.25, True)
        gemms(nc, K, project_rows(w["o"], C, attT, lambda t: vadd(nc, X[:, t, :], X[:, t, :]), "v", kc=8))


def channel_mix(nc, K, X, arrays, specs):
    with pool(nc, "l1f") as p:
        w = Weights(nc, p, "L1_ffn", arrays, specs)
        xn = p.sb("xn", [P, NT, C])
        xnT = p.sb("xnT", [P, KC, NTOK])
        prev = p.sb("prev", [P, KC, NTOK])
        xr = p.sb("xr", [P, KC, NTOK])
        xk = p.sb("xk", [P, KC, NTOK])
        om = p.sb("om", [P, 2 * KC])
        r = p.sb("r", [P, NT, C])
        relu = p.sb("relu", [P, KC, NTOK])
        k2 = p.sb("k2", [P, KC, NTOK])
        gated = p.sb("gated", [P, NT, C])
        normalize(nc, K, X, xn, xnT, 1e-5)
        with stage(nc, "dve_step") as (block, dve_step):
            @block.vector
            def _(dve):
                step = Steps(dve, dve_step)
                step(nc.vector.memset(prev[:].rearrange("p k (b t) -> p k b t", b=B)[:, :, :, 0], 0.0))
                for k in range(KC):
                    step(nc.vector.tensor_copy(prev[:, k, :].rearrange("p (b t) -> p b t", b=B)[:, :, 1:T],
                                               xnT[:, k, :].rearrange("p (b t) -> p b t", b=B)[:, :, 0:T - 1]))
                step(nc.vector.tensor_scalar(om[:], w["mu"], -1.0, 1.0, ALU.mult, ALU.add))
                for dst, at in ((xr, 0), (xk, KC)):
                    for k in range(KC):
                        step(nc.vector.tensor_scalar(dst[:, k, :], prev[:, k, :], om[:, at + k:at + k + 1], None, ALU.mult))
                        step(nc.vector.scalar_tensor_tensor(out=dst[:, k, :], in0=xnT[:, k, :], scalar=w["mu"][:, at + k:at + k + 1],
                                                            in1=dst[:, k, :], op0=ALU.mult, op1=ALU.add))

        def square(m):
            def evac(ps, step):
                step(nc.vector.tensor_scalar(relu[:, m, :], ps, 0.0, None, ALU.max))
                return nc.vector.tensor_tensor(k2[:, m, :], relu[:, m, :], relu[:, m, :], ALU.mult)
            return evac

        gemms(nc, K, project_T(w["k"], C, xk, square, "v")
              + project_rows(w["r"], C, xr, lambda t: (lambda ps, step: nc.scalar.activation(r[:, t, :], ps, ACT.Sigmoid)), "s"))

        def gate(t):
            def evac(ps, step):
                step(nc.vector.tensor_tensor(gated[:, t, :], ps, r[:, t, :], ALU.mult))
                return nc.vector.tensor_tensor(X[:, t, :], X[:, t, :], gated[:, t, :], ALU.add)
            return evac

        gemms(nc, K, project_rows(w["v"], C, k2, gate, "v"))


def routed_geglu(nc, K, X, arrays, specs):
    with pool(nc, "l0f") as p:
        xn = p.sb("xn", [P, NT, C])
        xnT = p.sb("xnT", [P, KC, NTOK])
        W1 = [p.sb(f"W1_{i}", [P, KC, FF]) for i in range(2)]
        W2 = [p.sb(f"W2_{i}", [P, KC, FF]) for i in range(2)]
        W3 = [p.sb(f"W3_{i}", [P, FC, C]) for i in range(2)]
        logits = p.sb("logits", [P, NT, E])
        best = p.sb("best", [P, NT])
        at = p.sb("at", [P, NT, E])
        first = p.sb("first", [P, NT])
        chosen = p.sb("chosen", [P, (E + 1) * NT])
        here = p.sb("here", [P, 2, NT])
        gel = p.sb("gel", [P, 2, NTOK])
        hT = p.sb("hT", [P, FC, NTOK])

        def sources(e):
            one = bass.ds(e, 1)
            return [arrays["W1"][one].rearrange("o (k p) n -> p (o k) n", p=P),
                    arrays["W2"][one].rearrange("o (k p) n -> p (o k) n", p=P),
                    arrays["W3"][one].rearrange("o (k p) n -> p (o k) n", p=P)]

        w = Weights(nc, p, "L0_ffn", arrays, specs, zip((W1[0][:], W2[0][:], W3[0][:]), sources(0)))
        normalize(nc, K, X, xn, xnT, 1e-5)
        gemms(nc, K, project_rows(w["gate"], E, xnT, lambda t: vcopy(nc, logits[:, t, :]), "v"))
        with stage(nc, "dve_step") as (block, dve_step):
            @block.vector
            def _(dve):
                step = Steps(dve, dve_step)
                step(nc.vector.tensor_reduce(best[:], logits[:], AX.X, ALU.max))
                step(nc.vector.tensor_tensor(at[:], logits[:], best[:].unsqueeze(2).to_broadcast([P, NT, E]), ALU.is_equal))
                step(nc.vector.tensor_tensor(at[:], at[:], w["iota_less"].to_broadcast([P, NT, E]), ALU.mult))
                step(nc.vector.tensor_reduce(first[:], at[:], AX.X, ALU.min))
                for e in range(E):
                    step(nc.vector.tensor_scalar(chosen[:, e * NT:(e + 1) * NT], first[:], float(e - E), None, ALU.is_equal))
                step(nc.vector.memset(chosen[:, E * NT:], 1.0))

        def experts(e, n):
            with pool(nc, f"exp{nc.next_id()}") as p2:
                psA = p2.ps("psA", [P, 2, 512])
                psG = p2.ps("psG", [P, 2, 512])
                psY = p2.ps("psY", [P, NT, 512])
                with stage(nc, "chosen_ready", "loaded1", "loaded0", "inner_ready", "gelu_ready", "hidden_ready",
                           "y_ready", "y_taken") as \
                        (block, chosen_ready, loaded1, loaded0, inner_ready, gelu_ready, hidden_ready, y_ready, y_taken):
                    @block.sync
                    def _(sp):
                        if n == 2:
                            for dst, src in zip((W1[1][:], W2[1][:], W3[1][:]), sources(e + 1)):
                                sp.dma_start(dst, src).then_inc(loaded1, 16)
                            sp.wait_ge(y_ready, NT)
                            for dst, src in zip((W1[0][:], W2[0][:], W3[0][:]), sources(e + 2)):
                                sp.dma_start(dst, src).then_inc(loaded0, 16)
                            sp.wait_ge(loaded1, 48)
                            sp.wait_ge(loaded0, 48)

                    @block.tensor
                    def _(pe):
                        for i in range(n):
                            if i:
                                pe.wait_ge(loaded1, 48)
                            for f in range(FC):
                                m = i * FC + f
                                s = slice(f * P, (f + 1) * P)
                                if m >= 2:
                                    pe.wait_ge(hidden_ready, m - 1)
                                for k in range(KC):
                                    last = nc.tensor.matmul(psA[:, m % 2, :], W1[i][:, k, s], xnT[:, k, :], start=k == 0, stop=k == KC - 1)
                                last.then_inc(inner_ready, 1)
                                for k in range(KC):
                                    last = nc.tensor.matmul(psG[:, m % 2, :], W2[i][:, k, s], xnT[:, k, :], start=k == 0, stop=k == KC - 1)
                                last.then_inc(inner_ready, 1)
                            pe.wait_ge(hidden_ready, (i + 1) * FC)
                            for t in range(NT):
                                if i:
                                    pe.wait_ge(y_taken, t + 1)
                                for f in range(FC):
                                    last = nc.tensor.matmul(psY[:, t, 0:C], hT[:, f, t * P:(t + 1) * P], W3[i][:, f, :],
                                                            start=f == 0, stop=f == FC - 1)
                                last.then_inc(y_ready, 1)
                    @block.scalar
                    def _(act):
                        for m in range(n * FC):
                            act.wait_ge(inner_ready, 2 * m + 1)
                            if m >= 2:
                                act.wait_ge(hidden_ready, m - 1)
                            nc.scalar.activation(gel[:, m % 2, :], psA[:, m % 2, :], ACT.Gelu).then_inc(gelu_ready, 1)

                    @block.vector
                    def _(dve):
                        for i in range(n):
                            nc.vector.tensor_copy(here[:, i, :], chosen[:, bass.ds((e + i) * NT, NT)]).then_inc(chosen_ready, 1)
                        dve.wait_ge(chosen_ready, n)
                        for i in range(n):
                            if i:
                                dve.wait_ge(y_ready, NT)
                            for f in range(FC):
                                m = i * FC + f
                                dve.wait_ge(gelu_ready, m + 1)
                                dve.wait_ge(inner_ready, 2 * m + 2)
                                nc.vector.tensor_tensor(hT[:, f, :], psG[:, m % 2, :], gel[:, m % 2, :], ALU.mult).then_inc(hidden_ready, 1)
                            for t in range(NT):
                                dve.wait_ge(y_ready, i * NT + t + 1)
                                if i:
                                    dve.wait_ge(y_taken, t + 1)
                                nc.vector.scalar_tensor_tensor(out=X[:, t, :], in0=psY[:, t, 0:C], scalar=here[:, i, t:t + 1],
                                                               in1=X[:, t, :], op0=ALU.mult, op1=ALU.add).then_inc(y_taken, 1)

        with turns(nc, E // 2) as pair:
            experts(pair * 2, 2)
        experts(E, 1)


def hyperbolic_attention(nc, K, X, arrays, specs):
    NQ = 2 * H
    with pool(nc, "l1a") as p:
        w = Weights(nc, p, "L1_attn", arrays, specs)
        gates = p.sb("gates", [P, NT, H + 1])
        spikes = p.sb("spikes", [P, NT])
        coef = p.sb("coef", [P, NT, H])
        v = p.sb("v", [P, NT, 512])
        y = p.sb("y", [P, NT, C])
        turned = {n: p.sb(f"T_{n}", [P, 4, NTOK]) for n in ("qE", "kE", "qH", "kH")}
        with pool(nc, "l1b") as p1:
            xn = p1.sb("xn", [P, NT, C])
            xnT = p1.sb("xnT", [P, KC, NTOK])
            qk = p1.sb("qk", [P, NT, NQ, 16])
            qn = p1.sb("qn", [P, NT, NQ, 16])
            sq = p1.sb("sq", [P, NT, NQ, 16])
            a = p1.sb("a", [P, NT, NQ])
            m = p1.sb("m", [P, NT, NQ])
            ratio = p1.sb("ratio", [P, NT, NQ])
            time = p1.sb("time", [P, NT, NQ])
            safe = p1.sb("safe", [P, 1])
            curv = p1.sb("curv", [P, H])
            soft = p1.sb("soft", [P, H])
            expm = p1.sb("expm", [P, H])
            om = p1.sb("om", [P, NT, H])
            rows = {n: p1.sb(f"R_{n}", [P, NT, 512]) for n in ("qE", "kE", "qH", "kH")}
            normalize(nc, K, X, xn, xnT, 1e-5)
            ones = K["ones"][0:1, :]
            gemms(nc, K, project_rows(w["gates"], H + 1, xnT, lambda t: (lambda ps, step: nc.scalar.activation(gates[:, t, :], ps, ACT.Sigmoid)),
                                      "s", bias=w["bgates"], ones=ones)
                  + project_rows(w["qk"], 512, xnT, lambda t: vcopy(nc, qk[:, t, :, :].rearrange("p h d -> p (h d)")), "v", bias=w["bqk"], ones=ones)
                  + project_rows(w["v"], 512, xnT, lambda t: scopy(nc, v[:, t, :]), "s", bias=w["bv"], ones=ones))

            def over(x):
                return x.unsqueeze(3).to_broadcast([P, NT, NQ, 16])

            def by_rows(x):
                return x.rearrange("p t h d -> p (t h) d")

            def heads(n):
                return rows[n][:].rearrange("p t (h d) -> p t h d", h=H)

            with stage(nc, "dve_step", "squares_ready", "norms_ready", "space_ready", "time_ready", "act_step", "soft_ready",
                       "log_ready", "safe_ready", "rows_cleared") as \
                    (block, dve_step, squares_ready, norms_ready, space_ready, time_ready, act_step, soft_ready, log_ready,
                     safe_ready, rows_cleared):
                @block.gpsimd
                def _(gp):
                    for n in ("qE", "kE", "qH", "kH"):
                        nc.gpsimd.memset(rows[n][:], 0.0).then_inc(rows_cleared, 1)

                @block.scalar
                def _(act):
                    nc.scalar.activation(safe[:], w["qk_scale"], ACT.Sigmoid).then_inc(safe_ready, 1)
                    nc.scalar.activation(soft[:], w["log_k"], ACT.Abs).then_inc(soft_ready, 1)
                    act.wait_ge(soft_ready, 1)
                    nc.scalar.activation(expm[:], soft[:], ACT.Exp, scale=-1.0).then_inc(act_step, 1)
                    act.wait_ge(act_step, 1)
                    nc.scalar.activation(expm[:], expm[:], ACT.Ln, bias=K["ones"][:, 0:1]).then_inc(log_ready, 1)
                    act.wait_ge(squares_ready, 1)
                    nc.scalar.activation(a[:], a[:], ACT.Sqrt).then_inc(norms_ready, 1)
                    act.wait_ge(space_ready, 1)
                    nc.scalar.activation(time[:], time[:], ACT.Sqrt, bias=K["ones"][:, 0:1]).then_inc(time_ready, 1)

                @block.vector
                def _(dve):
                    step = Steps(dve, dve_step)
                    V = nc.vector
                    step(V.tensor_tensor(sq[:], qk[:], qk[:], ALU.mult))
                    V.tensor_reduce(a[:], sq[:], AX.X, ALU.add).then_inc(squares_ready, 1)
                    step(V.tensor_scalar(spikes[:], gates[:, :, H], w["threshold"], None, ALU.is_gt))
                    dve.wait_ge(log_ready, 1)
                    step(V.tensor_scalar(curv[:], w["log_k"], 0.0, None, ALU.max))
                    step(V.tensor_tensor(curv[:], curv[:], expm[:], ALU.add))
                    step(V.tensor_scalar(curv[:], curv[:], 1e-6, None, ALU.add))
                    step(V.reciprocal(curv[:], curv[:]))
                    step(V.tensor_scalar(curv[:], curv[:], -1.0, None, ALU.mult))
                    step(V.tensor_tensor(coef[:], gates[:, :, 0:H], curv[:].unsqueeze(1).to_broadcast([P, NT, H]), ALU.mult))
                    step(V.tensor_scalar(om[:], gates[:, :, 0:H], -0.25, 0.25, ALU.mult, ALU.add))
                    dve.wait_ge(rows_cleared, 2)
                    for t in range(NT):
                        step(V.tensor_tensor(heads("qE")[:, t, :, 0:16], qk[:, t, 0:H, :], om[:, t, :].unsqueeze(2).to_broadcast([P, H, 16]), ALU.mult))
                        step(V.tensor_copy(heads("kE")[:, t, :, 0:16], qk[:, t, H:NQ, :]))
                    dve.wait_ge(safe_ready, 1)
                    dve.wait_ge(norms_ready, 1)
                    step(V.tensor_scalar(a[:], a[:], 1e-12, None, ALU.max))
                    step(V.reciprocal(m[:], a[:]))
                    step(V.tensor_scalar(m[:], m[:], safe[:, 0:1], 1.5, ALU.mult, ALU.mult))
                    step(V.tensor_tensor(by_rows(qn[:]), by_rows(qk[:]), m[:].rearrange("p t h -> p (t h)").unsqueeze(2).to_broadcast([P, NT * NQ, 16]), ALU.mult))
                    step(V.tensor_tensor(sq[:], qn[:], qn[:], ALU.mult))
                    step(V.tensor_reduce(m[:], by_rows(sq[:])[:, :, 1:16], AX.X, ALU.add))
                    step(V.tensor_tensor(m[:].rearrange("p t h -> p (t h)"), m[:].rearrange("p t h -> p (t h)"), by_rows(sq[:])[:, :, 0], ALU.subtract))
                    step(V.tensor_scalar(m[:], m[:], 1e-8, None, ALU.max))
                    coefs = [1.0]
                    for k in range(1, 9):
                        coefs.append(coefs[-1] / (2 * k * (2 * k + 1)))
                    step(V.tensor_scalar(ratio[:], m[:], coefs[8], coefs[7], ALU.mult, ALU.add))
                    for k in range(6, -1, -1):
                        step(V.tensor_tensor(ratio[:], ratio[:], m[:], ALU.mult))
                        step(V.tensor_scalar(ratio[:], ratio[:], coefs[k], None, ALU.add))
                    step(V.tensor_tensor(by_rows(qn[:]), by_rows(qn[:]), ratio[:].rearrange("p t h -> p (t h)").unsqueeze(2).to_broadcast([P, NT * NQ, 16]), ALU.mult))
                    step(V.tensor_tensor(sq[:], qn[:], qn[:], ALU.mult))
                    V.tensor_reduce(time[:], by_rows(sq[:])[:, :, 1:16], AX.X, ALU.add).then_inc(space_ready, 1)
                    dve.wait_ge(time_ready, 1)
                    dve.wait_ge(rows_cleared, 4)
                    for t in range(NT):
                        step(V.tensor_copy(heads("qH")[:, t, :, 1:16], qn[:, t, 0:H, 1:16]))
                        step(V.tensor_scalar(heads("kH")[:, t, :, 1:16], qn[:, t, H:NQ, 1:16], -1.0, None, ALU.mult))
                        step(V.tensor_copy(heads("qH")[:, t, :, 0], time[:, t, 0:H]))
                        step(V.tensor_copy(heads("kH")[:, t, :, 0], time[:, t, H:NQ]))
            gemms(nc, K, [job for n in rows for job in turn_all(K, rows[n], NT, 512, lambda k, t0, n=n: vcopy(nc, turned[n][:, k, :]), "v")])
        with pool(nc, "l1c") as p1:
            for b in range(B):
                hyperbolic_softmax(nc, K, b, turned, coef, spikes, v, y)
            yT = p1.sb("yT", [P, KC, NTOK])
            gemms(nc, K, turn_all(K, y, NT, C, lambda k, t0: vcopy(nc, yT[:, k, :]), "v"))
            add_to_residual(nc, K, X, w["o"], yT, KC, w["bo"])


def hyperbolic_softmax(nc, K, b, turned, coef, spikes, v, y):
    with pool(nc, f"hyp{b}") as p:
        Dm = p.sb("D", [P, H, 512])
        R = p.sb("R", [P, H, 512])
        probsT = p.sb("probsT", [P, H, 512])
        top = p.sb("top", [P, H, TB])
        tot = p.sb("tot", [P, H, TB])
        yP = p.sb("yP", [P, 4, T])
        banks = p.ps("banks", [P, 5, 512])
        psY = p.ps("psY", [P, 2, 512])
        RING = 5
        order = [(kind, h) for kind in ("hyper", "plain", "turn") for h in range(H)] + [("out", t) for t in range(TB)]
        with stage(nc, "unit_ready", "bank_read", "root_in", "root_ready", "sum_ready", "log_ready", "square_ready", "top_ready",
                   "exp_ready", "act_read", "y_ready", "y_copied", "dve_step", "scaled") as \
                (block, unit_ready, bank_read, root_in, root_ready, sum_ready, log_ready, square_ready, top_ready,
                 exp_ready, act_read, y_ready, y_copied, dve_step, scaled):

            def by_act(kind, h):
                return kind == "turn" and h % 2 == 0

            def read_by(n, act):
                return sum(1 for kind, h in order[:n + 1] if by_act(kind, h) == act)

            @block.tensor
            def _(pe):
                def values_product(g):
                    for h in range(4 * g, 4 * g + 4):
                        n = 2 * H + h
                        act = by_act("turn", h)
                        pe.wait_ge(act_read if act else bank_read, read_by(n, act))
                    for kt in range(TB):
                        for j in range(4):
                            h = 4 * g + j
                            last = nc.tensor.matmul(psY[32 * j:32 * j + 32, g // 2, g % 2 * T:(g % 2 + 1) * T], v[:, b * TB + kt, 32 * h:32 * h + 32],
                                                    probsT[:, h, kt * T:(kt + 1) * T], start=kt == 0, stop=kt == TB - 1)
                    last.then_inc(y_ready, 1)

                for n, (kind, h) in enumerate(order):
                    if n >= RING:
                        act = by_act(*order[n - RING])
                        pe.wait_ge(act_read if act else bank_read, read_by(n - RING, act))
                    bank = banks[:, n % RING, :]
                    r = slice(32 * (h % 4), 32 * (h % 4) + 32)
                    if kind in ("hyper", "plain"):
                        q, k = (turned["qH"], turned["kH"]) if kind == "hyper" else (turned["qE"], turned["kE"])
                        if kind == "plain":
                            nc.tensor.matmul(bank, K["ident16"], K["mask16_q"], start=True, stop=False)
                        for t in range(TB):
                            last = nc.tensor.matmul(bank[:, t * T:(t + 1) * T], q[r, h // 4, (b * TB + t) * P:(b * TB + t + 1) * P],
                                                    k[r, h // 4, b * T:(b + 1) * T], start=kind == "hyper", stop=kind == "hyper" or t == TB - 1)
                    elif kind == "turn":
                        pe.wait_ge(exp_ready, TB * (h + 1))
                        for kt in range(TB):
                            for t in range(TB):
                                last = nc.tensor.transpose(bank[:, kt * T + t * P:kt * T + (t + 1) * P], Dm[:, h, t * T + kt * P:t * T + (kt + 1) * P], K["ident"])
                    else:
                        if h == 0:
                            pe.wait_ge(y_copied, 2)
                        for g in range(4):
                            last = nc.tensor.transpose(bank[:, g * P:(g + 1) * P], yP[:, g, h * P:(h + 1) * P], K["ident"])
                    last.then_inc(unit_ready, 1)
                    if kind == "turn" and h % 4 == 0 and h:
                        values_product(h // 4 - 1)
                    if kind == "turn" and h == H - 1:
                        values_product(H // 4 - 1)

            @block.vector
            def _(dve):
                step = Steps(dve, dve_step)
                V = nc.vector
                for n, (kind, h) in enumerate(order):
                    if by_act(kind, h):
                        continue
                    bank = banks[:, n % RING, :]
                    if kind != "out":
                        dve.wait_ge(unit_ready, n + 1)
                    if kind == "hyper":
                        V.tensor_scalar(Dm[:, h, :], bank, float(np.float32(1.0 + 1e-6)), -1.0, ALU.max, ALU.add).then_inc(bank_read, 1)
                        dve.wait_ge(bank_read, h + 1)
                        V.scalar_tensor_tensor(out=R[:, h, :], in0=Dm[:, h, :], scalar=2.0, in1=Dm[:, h, :], op0=ALU.add, op1=ALU.mult).then_inc(root_in, 1)
                    elif kind == "plain":
                        dve.wait_ge(square_ready, h + 1)
                        s = slice(0, T)
                        step(V.scalar_tensor_tensor(out=Dm[:, h, s], in0=R[:, h, s], scalar=coef[:, b * TB, h:h + 1], in1=bank[:, s],
                                                    op0=ALU.mult, op1=ALU.add))
                        s = slice(T, 2 * T)
                        V.scalar_tensor_tensor(out=Dm[:, h, s], in0=R[:, h, s], scalar=coef[:, b * TB + 1, h:h + 1], in1=bank[:, s],
                                               op0=ALU.mult, op1=ALU.add).then_inc(bank_read, 1)
                        dve.wait_ge(bank_read, H + h + 1)
                        V.tensor_reduce(top[:, h, :], Dm[:, h, :].rearrange("p (s n) -> p s n", s=TB), AX.X, ALU.max, negate=True).then_inc(top_ready, 1)
                    elif kind == "turn":
                        V.tensor_copy(probsT[:, h, :], bank).then_inc(bank_read, 1)
                    else:
                        if h == 0:
                            dve.wait_ge(exp_ready, TB * H)
                            step(V.reciprocal(tot[:], tot[:]))
                            for t in range(TB):
                                step(V.tensor_scalar(tot[:, :, t], tot[:, :, t], spikes[:, b * TB + t:b * TB + t + 1], None, ALU.mult))
                        dve.wait_ge(unit_ready, n + 1)
                        V.tensor_tensor(y[:, b * TB + h, :].rearrange("p (h d) -> p h d", h=H), bank.rearrange("p (h d) -> p h d", h=H)[:, :, 0:16],
                                        tot[:, :, h].unsqueeze(2).to_broadcast([P, H, 16]), ALU.mult).then_inc(scaled, 1)
                dve.wait_ge(scaled, TB)

            @block.gpsimd
            def _(gp):
                for h in range(H):
                    gp.wait_ge(root_ready, h + 1)
                    nc.gpsimd.tensor_tensor(Dm[:, h, :], Dm[:, h, :], R[:, h, :], ALU.add).then_inc(sum_ready, 1)
                for h in range(H):
                    gp.wait_ge(log_ready, h + 1)
                    nc.gpsimd.tensor_tensor(R[:, h, :], Dm[:, h, :], Dm[:, h, :], ALU.mult).then_inc(square_ready, 1)

            @block.scalar
            def _(act):
                for h in range(H):
                    act.wait_ge(root_in, h + 1)
                    nc.scalar.activation(R[:, h, :], R[:, h, :], ACT.Sqrt).then_inc(root_ready, 1)
                for h in range(H):
                    act.wait_ge(sum_ready, h + 1)
                    nc.scalar.activation(Dm[:, h, :], Dm[:, h, :], ACT.Ln, bias=K["ones"][:, 0:1]).then_inc(log_ready, 1)
                for h in range(H):
                    act.wait_ge(top_ready, h + 1)
                    for t in range(TB):
                        s = slice(t * T, (t + 1) * T)
                        nc.scalar.activation(Dm[:, h, s], Dm[:, h, s], ACT.Exp, bias=top[:, h, t:t + 1], accum_out=tot[:, h, t:t + 1]).then_inc(exp_ready, 1)
                for h in range(0, H, 2):
                    n = 2 * H + h
                    act.wait_ge(unit_ready, n + 1)
                    nc.scalar.copy(probsT[:, h, :], banks[:, n % RING, :]).then_inc(act_read, 1)
                for i in range(2):
                    act.wait_ge(y_ready, 2 * i + 2)
                    nc.scalar.copy(yP[:, 2 * i:2 * i + 2, :], psY[:, i, :].rearrange("p (g n) -> p g n", g=2)).then_inc(y_copied, 1)


def pooled_attention(nc, K, X, arrays, specs):
    NKT = TB + ST
    with pool(nc, "l3x") as p:
        xn = p.sb("xn", [P, NT, C])
        q2 = p.sb("q2", [P, KC, NTOK])
        alpha = p.sb("alpha", [P, NT, C])
        zn = p.sb("zn", [P, NT, C])
        znT = p.sb("znT", [P, KC, NTOK])
        cx = p.sb("cx", [P, B, ST, C])

        def context_loads(b):
            ctx_b = arrays["ctx"][b].rearrange("(p n) c -> p n c", p=P)
            return [(cx[:, b, n:n + 8, :], ctx_b[:, n:n + 8, :]) for n in range(0, ST, 8)]

        with pool(nc, "l3y") as p1:
            w = Weights(nc, p1, "L3_xattn", arrays, specs, context_loads(0))
            xnT = p1.sb("xnT", [P, KC, NTOK])
            q1 = p1.sb("q1", [P, KC, NTOK])
            normalize(nc, K, X, xn, xnT, 1e-5)
            normalize(nc, K, xn, zn, znT, 1e-6, rms=True, w=w["norm_w"])
            gemms(nc, K, project_T(w["q"], C, znT, lambda m: vcopy(nc, q1[:, m, :]), "v")
                  + project_rows(w["gate"], C, xnT, lambda t: (lambda ps, step: nc.scalar.activation(alpha[:, t, :], ps, ACT.Sigmoid)), "s",
                                 bias=w["gate_b"], ones=K["ones"][0:1, :]))
            gemms(nc, K, project_T(w["k"], C, q1, lambda m: vcopy(nc, q2[:, m, :]), "v"))
        pooled_softmax(nc, K, X, xn, q2, alpha, zn, znT, cx, context_loads(1), NKT)


def pooled_softmax(nc, K, X, xn, q2, alpha, zn, znT, cx, next_loads, NKT):
    SU = S // 512
    PU = -(-NKT // 4)
    RING = 5
    order = []
    for i in range(NT + 1):
        if i < NT:
            if i % TB == 0:
                order += [("context", i // TB, u) for u in range(2 * ST // 4)]
            order += [("score", i, u) for u in range(SU + 1)]
        if i:
            order += [("probs", i - 1, u) for u in range(PU)]
    place = {unit: n for n, unit in enumerate(order)}

    def by_dve(kind, u):
        return u == SU if kind == "score" else u % 2 == 1

    def taken(n, dve):
        return sum(1 for kind, _, u in order[:n + 1] if by_dve(kind, u) == dve)

    with pool(nc, "l3z") as p:
        cxT = p.sb("cxT", [P, KC, S])
        sc = p.sb("sc", [P, 2, NKT * P])
        pT = p.sb("pT", [P, NKT, P])
        tops = p.sb("tops", [P, 2, SU + 1])
        top = p.sb("top", [P, 2])
        tot = p.sb("tot", [P, 2])
        ht = p.sb("ht", [P, 2, C])
        banks = p.ps("banks", [P, RING, 512])
        psH = p.ps("psH", [P, 2, 512])
        with stage(nc, "next_loaded", "unit_ready", "dve_took", "act_took", "top_step", "top_ready", "exp_ready", "h_ready",
                   "blend_step", "blended") as \
                (block, next_loaded, unit_ready, dve_took, act_took, top_step, top_ready, exp_ready, h_ready, blend_step, blended):
            @block.sync
            def _(sp):
                for dst, src in next_loads:
                    sp.dma_start(dst, src).then_inc(next_loaded, 16)
                sp.wait_ge(next_loaded, 16 * len(next_loads))

            @block.tensor
            def _(pe):
                for n, (kind, i, u) in enumerate(order):
                    if n >= RING:
                        last_kind, _, last_u = order[n - RING]
                        dve = by_dve(last_kind, last_u)
                        pe.wait_ge(dve_took if dve else act_took, taken(n - RING, dve))
                    bank = banks[:, n % RING, :]
                    if kind == "context":
                        if i and u == 0:
                            pe.wait_ge(next_loaded, 16 * len(next_loads))
                        for t in range(4):
                            last = nc.tensor.transpose(bank[:, t * P:(t + 1) * P], cx[:, i, u // 2 * 4 + t, u % 2 * P:(u % 2 + 1) * P], K["ident"])
                    elif kind == "score":
                        if u == 0 and i % TB == 0:
                            done = place["context", i // TB, 2 * ST // 4 - 1]
                            pe.wait_ge(dve_took, taken(done, True))
                            pe.wait_ge(act_took, taken(done, False))
                        for k in range(KC):
                            rhs = cxT[:, k, u * 512:(u + 1) * 512] if u < SU else znT[:, k, i // TB * T:(i // TB + 1) * T]
                            last = nc.tensor.matmul(bank[:, 0:rhs.shape[-1]], q2[:, k, i * P:(i + 1) * P], rhs, start=k == 0, stop=k == KC - 1)
                    else:
                        if u == 0:
                            pe.wait_ge(exp_ready, i + 1)
                        for j in range(4 * u, min(4 * u + 4, NKT)):
                            last = nc.tensor.transpose(bank[:, (j - 4 * u) * P:(j - 4 * u + 1) * P], sc[:, i % 2, j * P:(j + 1) * P], K["ident"])
                    last.then_inc(unit_ready, 1)
                    if kind == "probs" and u == PU - 1:
                        if i >= 2:
                            pe.wait_ge(blended, i - 1)
                        for j in range(NKT):
                            if j % 4 == 0:
                                m = place["probs", i, j // 4]
                                dve = by_dve("probs", j // 4)
                                pe.wait_ge(dve_took if dve else act_took, taken(m, dve))
                            v = cx[:, i // TB, j, :] if j < ST else zn[:, i // TB * TB + j - ST, :]
                            last = nc.tensor.matmul(psH[:, i % 2, 0:C], pT[:, j, :], v, start=j == 0, stop=j == NKT - 1)
                        last.then_inc(h_ready, 1)

            def destination(kind, i, u):
                if kind == "context":
                    return cxT[:, u % 2, u // 2 * 512:(u // 2 + 1) * 512]
                if kind == "score":
                    return sc[:, i % 2, u * 512:min((u + 1) * 512, S + T)]
                return pT[:, 4 * u:min(4 * u + 4, NKT), :].rearrange("p t q -> p (t q)")

            @block.scalar
            def _(act):
                for n, (kind, i, u) in enumerate(order):
                    if kind == "score" and u == 0 and i:
                        softmax_of = i - 1
                    elif kind == "probs" and u == 0 and i == NT - 1:
                        softmax_of = i
                    else:
                        softmax_of = None
                    if softmax_of is not None:
                        j = softmax_of
                        act.wait_ge(top_ready, j + 1)
                        if j >= 2:
                            act.wait_ge(blended, j - 1)
                        nc.scalar.activation(sc[:, j % 2, :], sc[:, j % 2, :], ACT.Exp, bias=top[:, j % 2:j % 2 + 1], scale=1.0 / 16.0,
                                             accum_out=tot[:, j % 2:j % 2 + 1]).then_inc(exp_ready, 1)
                    if not by_dve(kind, u):
                        act.wait_ge(unit_ready, n + 1)
                        dst = destination(kind, i, u)
                        nc.scalar.copy(dst, banks[:, n % RING, 0:dst.shape[-1]]).then_inc(act_took, 1)

            @block.vector
            def _(dve):
                tops_done = Steps(dve, top_step)
                blend = Steps(dve, blend_step)
                for n, (kind, i, u) in enumerate(order):
                    dst = destination(kind, i, u)
                    if by_dve(kind, u):
                        dve.wait_ge(unit_ready, n + 1)
                        if kind == "score":
                            nc.vector.tensor_tensor(sc[:, i % 2, S:S + T], banks[:, n % RING, 0:T], K["mask_q"][:, i % TB, :], ALU.add).then_inc(dve_took, 1)
                            dve.wait_ge(dve_took, taken(n, True))
                        else:
                            nc.vector.tensor_copy(dst, banks[:, n % RING, 0:dst.shape[-1]]).then_inc(dve_took, 1)
                    if kind == "score":
                        src = dst if u < SU else sc[:, i % 2, S:S + T]
                        if u < SU:
                            dve.wait_ge(act_took, taken(n, False))
                        tops_done(nc.vector.tensor_reduce(tops[:, i % 2, u:u + 1], src, AX.X, ALU.max))
                        if u == SU:
                            if i >= 2:
                                dve.wait_ge(exp_ready, i - 1)
                            tops_done(nc.vector.tensor_reduce(top[:, i % 2:i % 2 + 1], tops[:, i % 2, :], AX.X, ALU.max, negate=True))
                            nc.vector.tensor_scalar(top[:, i % 2:i % 2 + 1], top[:, i % 2:i % 2 + 1], 1.0 / 16.0, None, ALU.mult).then_inc(top_ready, 1)
                    if kind == "probs" and u == PU - 1:
                        dve.wait_ge(h_ready, i + 1)
                        dve.wait_ge(exp_ready, i + 1)
                        one, h = tot[:, i % 2:i % 2 + 1], ht[:, i % 2, :]
                        blend(nc.vector.reciprocal(one, one))
                        blend(nc.vector.scalar_tensor_tensor(out=h, in0=psH[:, i % 2, 0:C], scalar=one, in1=xn[:, i, :], op0=ALU.mult, op1=ALU.subtract))
                        blend(nc.vector.tensor_tensor(h, h, alpha[:, i, :], ALU.mult))
                        blend(nc.vector.tensor_tensor(h, h, xn[:, i, :], ALU.add))
                        nc.vector.tensor_tensor(X[:, i, :], X[:, i, :], h, ALU.add).then_inc(blended, 1)
                dve.wait_ge(blended, NT)


def state_space(nc, K, X, arrays, specs):
    DI = 2 * C
    CH = DI // P
    NS = 16
    with pool(nc, "l2s") as p:
        w = Weights(nc, p, "L2_attn", arrays, specs)
        xn = p.sb("xn", [P, NT, C])
        xnT = p.sb("xnT", [P, KC, NTOK])
        xi = p.sb("xi", [P, CH, NTOK])
        z = p.sb("z", [P, CH, NTOK])
        conv = p.sb("conv", [P, CH, NTOK])
        xs = p.sb("xs", [P, CH, NTOK])
        xp = p.sb("xp", [2 * NS + 1, NTOK])
        raw = p.sb("raw", [P, CH, NTOK])
        delta = p.sb("delta", [P, CH, NTOK])
        dx = p.sb("dx", [P, CH, NTOK])
        A = p.sb("A", [P, NS])
        yT = p.sb("yT", [P, CH, NTOK])
        normalize(nc, K, X, xn, xnT, 1e-5)
        gemms(nc, K, project_T(w["in"], DI, xnT, lambda m: vcopy(nc, xi[:, m, :]), "v")
              + project_T(w["in"][:, :, DI:], DI, xnT, lambda m: (lambda ps, step: nc.scalar.activation(z[:, m, :], ps, ACT.Silu)), "s"))
        with stage(nc, "dve_step", "conv_ready", "act_step", "act_done") as (block, dve_step, conv_ready, act_step, act_done):
            @block.vector
            def _(dve):
                step = Steps(dve, dve_step)
                for m in range(CH):
                    step(nc.vector.tensor_scalar(conv[:, m, :], xi[:, m, :], w["conv_w"][:, m, 3:4], w["conv_b"][:, m:m + 1], ALU.mult, ALU.add))
                    out, src = (x[:, m, :].rearrange("p (b t) -> p b t", b=B) for x in (conv, xi))
                    for s in range(1, 4):
                        step(nc.vector.scalar_tensor_tensor(out=out[:, :, s:T], in0=src[:, :, 0:T - s], scalar=w["conv_w"][:, m, 3 - s:4 - s],
                                                            in1=out[:, :, s:T], op0=ALU.mult, op1=ALU.add))
                dve.sem_inc(conv_ready, 1)

            @block.scalar
            def _(act):
                act.wait_ge(conv_ready, 1)
                nc.scalar.activation(xs[:], conv[:], ACT.Silu).then_inc(act_done, 1)
                nc.scalar.activation(A[:], w["A_log"], ACT.Exp).then_inc(act_done, 1)
                act.wait_ge(act_done, 2)
                nc.scalar.mul(A[:], A[:], -1.0).then_inc(act_done, 1)
                act.wait_ge(act_done, 3)
        gemms(nc, K, [(2 * NS + 1, NTOK, [(w["x"][:, m, :], xs[:, m, :]) for m in range(CH)], vcopy(nc, xp[:]), "v")])
        gemms(nc, K, [(P, NTOK, [(w["dt"][:, m * P:(m + 1) * P], xp[0:1, :])], vbias(nc, raw[:, m, :], w["b_dt"][:, m:m + 1]), "v") for m in range(CH)])
        with stage(nc, "act_step", "soft_ready", "dve_step") as (block, act_step, soft_ready, dve_step):
            @block.scalar
            def _(act):
                step = Steps(act, act_step)
                step(nc.scalar.activation(delta[:], raw[:], ACT.Abs))
                step(nc.scalar.activation(delta[:], delta[:], ACT.Exp, scale=-1.0))
                nc.scalar.activation(delta[:], delta[:], ACT.Ln, bias=K["ones"][:, 0:1]).then_inc(soft_ready, 1)

            @block.vector
            def _(dve):
                step = Steps(dve, dve_step)
                dve.wait_ge(act_step, 1)
                step(nc.vector.tensor_scalar(raw[:], raw[:], 0.0, None, ALU.max))
                dve.wait_ge(soft_ready, 1)
                step(nc.vector.tensor_tensor(delta[:], delta[:], raw[:], ALU.add))
                step(nc.vector.tensor_tensor(dx[:], delta[:], xs[:], ALU.mult))
        with pool(nc, "l2t") as p2:
            psB = p2.ps("psB", [P, 2, 512])
            psC = p2.ps("psC", [P, 2, 512])
            psY = p2.ps("psY", [P, CH, 512])
            decay = p2.sb("decay", [P, 3, NTOK])
            u = p2.sb("u", [P, 2, NTOK])
            h = p2.sb("h", [P, 2, NTOK])
            hc = p2.sb("hc", [P, 3, NTOK])
            with stage(nc, "spread", "input_ready", "decay_ready", "states_ready", "read_ready", "summed", "dve_step") as \
                    (block, spread, input_ready, decay_ready, states_ready, read_ready, summed, dve_step):
                @block.tensor
                def _(pe):
                    def spread_rows(s):
                        if s >= 2:
                            pe.wait_ge(read_ready, (s - 1) * CH)
                        n = 2 * NS + 1
                        for ps, r in ((psB, 1 + s), (psC, 1 + NS + s)):
                            last = nc.tensor.matmul(ps[:, s % 2, :], K["ident"][0:n, r:r + 1].to_broadcast([n, P]), xp[:, :], start=True, stop=True)
                        last.then_inc(spread, 1)

                    spread_rows(0)
                    for s in range(NS):
                        if s + 1 < NS:
                            spread_rows(s + 1)
                        for m in range(CH):
                            i = s * CH + m
                            pe.wait_ge(read_ready, i + 1)
                            nc.tensor.matmul(psY[:, m, :], K["ident"], hc[:, i % 3, :], start=s == 0, stop=s == NS - 1).then_inc(summed, 1)

                @block.scalar
                def _(act):
                    for i in range(NS * CH):
                        if i >= 3:
                            act.wait_ge(states_ready, 2 * (i - 2))
                        nc.scalar.activation(decay[:, i % 3, :], delta[:, i % CH, :], ACT.Exp, scale=A[:, i // CH:i // CH + 1]).then_inc(decay_ready, 1)

                @block.vector
                def _(dve):
                    N = NS * CH

                    def inputs(i):
                        s, m = i // CH, i % CH
                        dve.wait_ge(spread, s + 1)
                        if i >= 2:
                            dve.wait_ge(states_ready, 2 * (i - 1))
                        nc.vector.tensor_tensor(u[:, i % 2, :], psB[:, s % 2, :], dx[:, m, :], ALU.mult).then_inc(input_ready, 1)

                    inputs(0)
                    for i in range(N):
                        s, m = i // CH, i % CH
                        if i + 1 < N:
                            inputs(i + 1)
                        dve.wait_ge(decay_ready, i + 1)
                        dve.wait_ge(input_ready, i + 1)
                        if i >= 2:
                            dve.wait_ge(read_ready, i - 1)
                        for b in range(B):
                            c = slice(b * T, (b + 1) * T)
                            nc.vector.tensor_tensor_scan(h[:, i % 2, c], decay[:, i % 3, c], u[:, i % 2, c], 0.0, ALU.mult, ALU.add).then_inc(states_ready, 1)
                        dve.wait_ge(states_ready, 2 * (i + 1))
                        if i >= 3:
                            dve.wait_ge(summed, i - 2)
                        nc.vector.tensor_tensor(hc[:, i % 3, :], psC[:, s % 2, :], h[:, i % 2, :], ALU.mult).then_inc(read_ready, 1)
                    dve.wait_ge(summed, N)
                    step = Steps(dve, dve_step)
                    for m in range(CH):
                        step(nc.vector.scalar_tensor_tensor(out=yT[:, m, :], in0=xs[:, m, :], scalar=w["D"][:, m:m + 1], in1=psY[:, m, :],
                                                            op0=ALU.mult, op1=ALU.add))
                        step(nc.vector.tensor_tensor(yT[:, m, :], yT[:, m, :], z[:, m, :], ALU.mult))
        gemms(nc, K, project_rows(w["out"], C, yT, lambda t: vadd(nc, X[:, t, :], X[:, t, :]), "v", kc=CH))


def expert_choice(nc, K, X, arrays, specs):
    with pool(nc, "l2f") as p:
        xn = p.sb("xn", [P, NT, C])
        xnT = p.sb("xnT", [P, KC, NTOK])
        W1 = [p.sb(f"W1_{i}", [P, KC, FF]) for i in range(2)]
        W2 = [p.sb(f"W2_{i}", [P, FC, C]) for i in range(2)]
        score = p.sb("score", [P, E, NT])
        rank = p.sb("rank", [P, E * NT])
        over = p.sb("over", [P, E, NT])
        same = p.sb("same", [P, E, NT])
        scores = p.sb("scores", [P, E, NTOK])
        junk = p.sb("junk", [P, 2, NTOK])

        def sources(e):
            one = bass.ds(e, 1)
            return [arrays["M1"][one].rearrange("o (k p) n -> p (o k) n", p=P), arrays["M2"][one].rearrange("o (k p) n -> p (o k) n", p=P)]

        w = Weights(nc, p, "L2_ffn", arrays, specs, zip((W1[0][:], W2[0][:]), sources(0)))
        normalize(nc, K, X, xn, xnT, 1e-5)
        gemms(nc, K, project_rows(w["gate"], E, xnT, lambda t: (lambda ps, step: nc.scalar.activation(score[:, :, t], ps, ACT.Sigmoid)), "s"))
        gemms(nc, K, [(P, NTOK, [("turn", score[:, e, t:t + 1].to_broadcast([P, P]), t * P) for t in range(NT)], scopy(nc, scores[:, e, :]), "s")
                      for e in range(E)])
        with stage(nc, "dve_step", "counted") as (block, dve_step, counted):
            @block.vector
            def _(dve):
                step = Steps(dve, dve_step)
                for n in range(E * NT):
                    e, t = n // NT, n % NT
                    if n:
                        dve.wait_ge(counted, 2 * n)
                    nc.vector.tensor_scalar(junk[:, 0, :], scores[:, e, :], score[:, e, t:t + 1], 0.0, ALU.is_gt, ALU.add,
                                            accum_out=over[:, e, t:t + 1]).then_inc(counted, 1)
                    nc.vector.scalar_tensor_tensor(out=junk[:, 1, :], in0=scores[:, e, :], scalar=score[:, e, t:t + 1], in1=w["before"][:, t, :],
                                                   op0=ALU.is_equal, op1=ALU.mult, accum_out=same[:, e, t:t + 1]).then_inc(counted, 1)
                dve.wait_ge(counted, 2 * E * NT)
                step(nc.vector.tensor_tensor(rank[:], over[:].rearrange("p e t -> p (e t)"), same[:].rearrange("p e t -> p (e t)"), ALU.add))
        rk = p.sb("rk", [P, 2 * NT])
        sc = p.sb("sc", [P, 2 * NT])
        b1 = p.sb("b1", [P, 2 * FC])
        b2 = p.sb("b2", [1, 2 * C])
        place = p.sb("place", [P, NT, P])
        placeT = p.sb("placeT", [P, NT, P])
        exT = p.sb("exT", [P, KC, P])
        hT = p.sb("hT", [P, FC, P])
        rows = p.sb("rows", [P, C])
        flat_score = score[:].rearrange("p e t -> p (e t)")
        with turns(nc, E // 2) as pair:
            e = pair * 2
            with pool(nc, "l2e") as p2:
                psX = p2.ps("psX", [P, KC, P])
                psP = p2.ps("psP", [P, NT, P])
                psH = p2.ps("psH", [P, 2, 4, P])
                psR = p2.ps("psR", [P, C])
                psY = p2.ps("psY", [P, 2, 512])
                with stage(nc, "picked", "placed", "gathered", "turned", "gathered_copied", "turned_copied", "inner_ready",
                           "gelu_ready", "rows_ready", "rows_copied", "y_ready", "y_taken", "loaded1", "loaded0") as \
                        (block, picked, placed, gathered, turned, gathered_copied, turned_copied, inner_ready,
                         gelu_ready, rows_ready, rows_copied, y_ready, y_taken, loaded1, loaded0):
                    @block.sync
                    def _(sp):
                        for dst, src in zip((W1[1][:], W2[1][:]), sources(e + 1)):
                            sp.dma_start(dst, src).then_inc(loaded1, 16)
                        sp.wait_ge(rows_ready, 1)
                        for dst, src in zip((W1[0][:], W2[0][:]), sources(e + 2)):
                            sp.dma_start(dst, src).then_inc(loaded0, 16)
                        sp.wait_ge(loaded1, 32)
                        sp.wait_ge(loaded0, 32)

                    @block.tensor
                    def _(pe):
                        for i in range(2):
                            pe.wait_ge(placed, NT * (i + 1))
                            for k in range(KC):
                                for t in range(NT):
                                    last = nc.tensor.matmul(psX[:, k, :], xn[:, t, k * P:(k + 1) * P], place[:, t, :], start=t == 0, stop=t == NT - 1)
                            last.then_inc(gathered, 1)
                            for t in range(NT):
                                last = nc.tensor.transpose(psP[:, t, :], place[:, t, :], K["ident"])
                            last.then_inc(turned, 1)
                            pe.wait_ge(gathered_copied, i + 1)
                            if i:
                                pe.wait_ge(loaded1, 32)
                            for f in range(FC):
                                if i:
                                    pe.wait_ge(gelu_ready, f // 4 * 4 + 4)
                                for k in range(KC):
                                    last = nc.tensor.matmul(psH[:, f // 4, f % 4, :], W1[i][:, k, f * P:(f + 1) * P], exT[:, k, :], start=k == 0, stop=k == KC - 1)
                                if f % 4 == 3:
                                    last.then_inc(inner_ready, 1)
                            pe.wait_ge(gelu_ready, FC * (i + 1))
                            for f in range(FC):
                                nc.tensor.matmul(psR[:, :], hT[:, f, :], W2[i][:, f, :], start=f == 0, stop=False)
                            nc.tensor.matmul(psR[:, :], K["ones"][0:1, :], b2[0:1, i * C:(i + 1) * C], start=False, stop=True).then_inc(rows_ready, 1)
                            pe.wait_ge(rows_copied, i + 1)
                            pe.wait_ge(turned_copied, i + 1)
                            for t in range(NT):
                                if i * NT + t >= 2:
                                    pe.wait_ge(y_taken, i * NT + t - 1)
                                nc.tensor.matmul(psY[:, t % 2, 0:C], placeT[:, t, :], rows[:], start=True, stop=True).then_inc(y_ready, 1)

                    @block.scalar
                    def _(act):
                        act.wait_ge(picked, 4)
                        for i in range(2):
                            act.wait_ge(turned, i + 1)
                            if i:
                                act.wait_ge(y_ready, NT)
                            nc.scalar.copy(placeT[:], psP[:]).then_inc(turned_copied, 1)
                            for f in range(FC):
                                act.wait_ge(inner_ready, 2 * i + f // 4 + 1)
                                if i:
                                    act.wait_ge(rows_ready, i)
                                nc.scalar.activation(hT[:, f, :], psH[:, f // 4, f % 4, :], ACT.Gelu,
                                                     bias=b1[:, i * FC + f:i * FC + f + 1]).then_inc(gelu_ready, 1)

                    @block.vector
                    def _(dve):
                        nc.vector.tensor_copy(rk[:], rank[:, bass.ds(e * NT, 2 * NT)]).then_inc(picked, 1)
                        nc.vector.tensor_copy(sc[:], flat_score[:, bass.ds(e * NT, 2 * NT)]).then_inc(picked, 1)
                        nc.vector.tensor_copy(b1[:], w["b1"][:, bass.ds(e * FC, 2 * FC)]).then_inc(picked, 1)
                        nc.vector.tensor_copy(b2[:], w["b2"][:, bass.ds(e * C, 2 * C)]).then_inc(picked, 1)
                        dve.wait_ge(picked, 4)
                        for i in range(2):
                            if i:
                                dve.wait_ge(gathered, i)
                                dve.wait_ge(turned, i)
                            for t in range(NT):
                                nc.vector.tensor_scalar(place[:, t, :], w["iota"], rk[:, i * NT + t:i * NT + t + 1], None, ALU.is_equal).then_inc(placed, 1)
                            dve.wait_ge(gathered, i + 1)
                            if i:
                                dve.wait_ge(inner_ready, 2 * i)
                            nc.vector.tensor_copy(exT[:], psX[:]).then_inc(gathered_copied, 1)
                            dve.wait_ge(rows_ready, i + 1)
                            if i:
                                dve.wait_ge(y_ready, NT * i)
                            nc.vector.tensor_copy(rows[:], psR[:]).then_inc(rows_copied, 1)
                            for t in range(NT):
                                n = i * NT + t
                                dve.wait_ge(y_ready, n + 1)
                                if n >= NT:
                                    dve.wait_ge(y_taken, n - NT + 1)
                                nc.vector.scalar_tensor_tensor(out=X[:, t, :], in0=psY[:, t % 2, 0:C], scalar=sc[:, n:n + 1], in1=X[:, t, :],
                                                               op0=ALU.mult, op1=ALU.add).then_inc(y_taken, 1)


def rope_and_groups(nc, K, X, arrays, specs):
    HID = 512
    HC = HID // P
    with pool(nc, "l3f") as p:
        w = Weights(nc, p, "L3_ffn", arrays, specs)
        we = Weights(nc, p, "L3_ffn_experts", arrays, specs, now=False)
        xn = p.sb("xn", [P, NT, C])
        s1 = p.sb("s1", [P, NT, C])
        x1 = p.sb("x1", [P, NT, C])
        x1T = p.sb("x1T", [P, KC, NTOK])
        with pool(nc, "l3g") as p1:
            xnT = p1.sb("xnT", [P, KC, NTOK])
            lowk = p1.sb("lowk", [64, 1, NTOK])
            lowv = p1.sb("lowv", [64, 1, NTOK])
            qT = p1.sb("qT", [P, KC, NTOK])
            kT = p1.sb("kT", [P, KC, NTOK])
            stacks = Stacks(nc, p1, "L3_ffn")
            v = p1.sb("v", [P, NT, 512])
            attT = p1.sb("attT", [P, 4, NTOK])
            other = p1.sb("other", [P, 2 * KC, NTOK])
            normalize(nc, K, X, xn, xnT, 1e-5)
            gemms(nc, K, [(64, NTOK, [(w[n][:, k, :], xnT[:, k, :]) for k in range(KC)], vcopy(nc, dst[:, 0, :]), "v")
                          for n, dst in (("kc", lowk), ("vc", lowv))])

            def straight(dst):
                return lambda m: (lambda ps, step: nc.vector.tensor_tensor(dst[:, m, :], ps, w["cos"], ALU.mult))

            def crossed(dst, base):
                def at(m):
                    def evac(ps, step):
                        step(nc.vector.tensor_tensor(other[:, base + m, :], ps, w["sin"], ALU.mult))
                        return nc.vector.tensor_tensor(dst[:, m, :], dst[:, m, :], other[:, base + m, :], ALU.add)
                    return evac
                return at

            gemms(nc, K, project_T(w["q"], C, xnT, straight(qT), "v") + project_T(w["k"], C, lowk, straight(kT), "v", kc=1)
                  + project_T(w["qx"], C, xnT, crossed(qT, 0), "v") + project_T(w["kx"], C, lowk, crossed(kT, KC), "v", kc=1)
                  + project_rows(w["v"], 512, lowv, lambda t: scopy(nc, v[:, t, :]), "s", kc=1, bias=w["bv"], ones=K["ones"][0:1, :]))
            store_parts(nc, K, [(P, NTOK, [(K["ident"], x[:, m, :])], None, stacks.into(which, m)) for which, x in enumerate((qT, kT)) for m in range(KC)])
            stacks.load(K)
            stacks.attend(K, v, attT, 0.25, False, we.loads)
            gemms(nc, K, project_rows(w["o"], C, attT, lambda t: vadd(nc, s1[:, t, :], xn[:, t, :]), "v", kc=4))
        normalize(nc, K, s1, x1, x1T, 1e-6, rms=True, w=w["norm1_w"])
        acc = p.sb("acc", [P, NT, C])
        sil = p.sb("sil", [P, 2 * HC, NTOK])
        hT = p.sb("hT", [P, 2 * HC, NTOK])
        logit = p.sb("logit", [P, NT, 2 + E])
        gate = p.sb("gate", [P, NT, E])
        gemms(nc, K, [(P, NTOK, [(we[n][:, k, m * P:(m + 1) * P], x1T[:, k, :]) for k in range(KC)],
                       (lambda ps, step, i=i, m=m: nc.scalar.activation(sil[:, i * HC + m, :], ps, ACT.Silu)), "s")
                      for i, n in enumerate(("in", "w1")) for m in range(HC)]
              + project_rows(we["gates"], 2 + E, x1T, lambda t: vcopy(nc, logit[:, t, :]), "v", bias=we["bgates"], ones=K["ones"][0:1, :]))
        gemms(nc, K, [(P, NTOK, [(we[n][:, k, HID + m * P:HID + (m + 1) * P], x1T[:, k, :]) for k in range(KC)],
                       (lambda ps, step, i=i, m=m: nc.vector.tensor_tensor(hT[:, i * HC + m, :], ps, sil[:, i * HC + m, :], ALU.mult)), "v")
                      for i, n in enumerate(("in", "w1")) for m in range(HC)])
        group_weights(nc, p, logit, gate)
        gemms(nc, K, project_rows(we["out"], C, hT, lambda t: vadd(nc, acc[:, t, :], x1[:, t, :]), "v", kc=HC)
              + [(P, C, [(hT[:, HC + k, t * P:(t + 1) * P], we["w2"][:, e * HC + k, :]) for k in range(HC)],
                  (lambda ps, step, e=e, t=t: nc.vector.scalar_tensor_tensor(out=acc[:, t, :], in0=ps, scalar=gate[:, t, e:e + 1], in1=acc[:, t, :],
                                                                            op0=ALU.mult, op1=ALU.add)), "v")
                 for e in range(E) for t in range(NT)])
        normalize(nc, K, acc, s1, None, 1e-6, rms=True, w=w["norm2_w"])
        with stage(nc, "added") as (block, added):
            @block.vector
            def _(dve):
                nc.vector.tensor_tensor(X[:], X[:], s1[:], ALU.add).then_inc(added, 1)
                dve.wait_ge(added, 1)


def group_weights(nc, p, logit, gate):
    G, EG = 2, E // 2
    names = ("gmax", "gsum", "gp", "emax", "esum", "ep", "prob", "rank", "cmp")
    shapes = ((P, NT), (P, NT), (P, NT, G), (P, NT, G), (P, NT, G), (P, NT, E), (P, NT, E), (P, NT, E), (P, NT, E))
    gmax, gsum, gp, emax, esum, ep, prob, rank, cmp = (p.sb(n, list(s)) for n, s in zip(names, shapes))
    with stage(nc, "dve_step", "shifted", "exp_ready") as (block, dve_step, shifted, exp_ready):
        @block.scalar
        def _(act):
            act.wait_ge(shifted, 2)
            nc.scalar.activation(gp[:], gp[:], ACT.Exp).then_inc(exp_ready, 1)
            nc.scalar.activation(ep[:], ep[:], ACT.Exp).then_inc(exp_ready, 1)

        @block.vector
        def _(dve):
            V = nc.vector
            step = Steps(dve, dve_step)

            def by_group(x):
                return x[:].rearrange("p t (g e) -> p (t g) e", g=G)

            def each(x, n):
                return x.unsqueeze(2).to_broadcast([P, x.shape[1], n])

            def flat(x):
                return x[:].rearrange("p t g -> p (t g)")

            step(V.tensor_reduce(gmax[:], logit[:, :, 0:G], AX.X, ALU.max))
            V.tensor_tensor(gp[:], logit[:, :, 0:G], each(gmax[:], G), ALU.subtract).then_inc(shifted, 1)
            step(V.tensor_copy(ep[:], logit[:, :, G:G + E]))
            step(V.tensor_reduce(flat(emax), by_group(ep), AX.X, ALU.max))
            V.tensor_tensor(by_group(ep), by_group(ep), each(flat(emax), EG), ALU.subtract).then_inc(shifted, 1)
            dve.wait_ge(exp_ready, 2)
            step(V.tensor_reduce(gsum[:], gp[:], AX.X, ALU.add))
            step(V.reciprocal(gsum[:], gsum[:]))
            step(V.tensor_tensor(gp[:], gp[:], each(gsum[:], G), ALU.mult))
            step(V.tensor_reduce(flat(esum), by_group(ep), AX.X, ALU.add))
            step(V.reciprocal(esum[:], esum[:]))
            step(V.tensor_tensor(by_group(prob), by_group(ep), each(flat(esum), EG), ALU.mult))
            step(V.tensor_tensor(emax[:, :, 1], gp[:, :, 1], gp[:, :, 0], ALU.is_gt))
            step(V.tensor_scalar(emax[:, :, 0], emax[:, :, 1], -1.0, 1.0, ALU.mult, ALU.add))
            step(V.tensor_tensor(gp[:], gp[:], emax[:], ALU.mult))
            step(V.tensor_tensor(by_group(prob), by_group(prob), each(flat(gp), EG), ALU.mult))
            step(V.memset(rank[:], 0.0))
            for e in range(E):
                it = prob[:, :, e:e + 1].to_broadcast([P, NT, E])
                step(V.tensor_tensor(cmp[:], it, prob[:], ALU.is_gt))
                step(V.tensor_tensor(rank[:], rank[:], cmp[:], ALU.add))
                if e + 1 < E:
                    n = E - 1 - e
                    it = prob[:, :, e:e + 1].to_broadcast([P, NT, n])
                    step(V.tensor_tensor(cmp[:, :, e + 1:], it, prob[:, :, e + 1:], ALU.is_equal))
                    step(V.tensor_tensor(rank[:, :, e + 1:], rank[:, :, e + 1:], cmp[:, :, e + 1:], ALU.add))
            step(V.tensor_scalar(rank[:], rank[:], 2.0, None, ALU.is_lt))
            step(V.tensor_tensor(gate[:], prob[:], rank[:], ALU.mult))


LAYERS = [
    ("L0_xattn", lambda nc, K, X, a, s: cross_attention(nc, K, X, a, s, "L0_xattn")),
    ("L0_attn", alibi_attention),
    ("L0_ffn", routed_geglu),
    ("L1_xattn", lambda nc, K, X, a, s: cross_attention(nc, K, X, a, s, "L1_xattn")),
    ("L1_attn", hyperbolic_attention),
    ("L1_ffn", channel_mix),
    ("L2_xattn", lora_attention),
    ("L2_attn", state_space),
    ("L2_ffn", expert_choice),
    ("L3_xattn", pooled_attention),
    ("L3_attn", complex_attention),
    ("L3_ffn", rope_and_groups),
]


def build(nc, x, out, arrays, specs, layers=None):
    with pool(nc, "top") as p:
        X = p.sb("X", [P, NT, C])
        const = Weights(nc, p, "consts", arrays, specs, now=False)
        K = {k: const[k] for k in specs["consts"]}
        K["sel"] = {32: K["sel32"], 64: K["sel64"]}
        K["ones_dram"] = nc.dram_tensor("ones_rows", (3, H * NTOK), BF16, kind="Internal").ap()
        K["zeros_dram"] = nc.dram_tensor("zeros_rows", (3, H * NTOK), BF16, kind="Internal").ap()
        ident16 = p.sb("ident16", [P, P], BF16)
        K["ident16"] = ident16[:]
        masks16 = p.sb("masks16", [P, 2, TB * T], BF16)
        K["mask16_q"], K["mask16_k"] = masks16[:, 0, :], masks16[:, 1, :]
        with pool(nc, "rows") as p1:
            fill = [p1.sb(f"fill{i}", [3, H * NTOK], BF16) for i in range(2)]
            load(nc, const.loads + [(X[:, t, :], x[t // TB, (t % TB) * P:(t % TB + 1) * P, :]) for t in range(NT)],
                 [lambda: nc.vector.memset(fill[0][:], 1.0)], [lambda: nc.gpsimd.memset(fill[1][:], 0.0)])
            load(nc, [(K["ones_dram"], fill[0][:]), (K["zeros_dram"], fill[1][:])],
                 [lambda: nc.vector.tensor_copy(ident16[:], K["ident"]),
                  lambda: nc.vector.tensor_copy(masks16[:, 0, :], K["mask_q"].rearrange("p s n -> p (s n)")),
                  lambda: nc.vector.tensor_copy(masks16[:, 1, :], K["mask_k"].rearrange("p s n -> p (s n)"))])
        for name, layer in LAYERS:
            if layers is None or name in layers:
                layer(nc, K, X, arrays, specs)
        with stage(nc, "stored") as (block, stored):
            @block.sync
            def _(sp):
                for t in range(NT):
                    sp.dma_start(out[t // TB, (t % TB) * P:(t % TB + 1) * P, :], X[:, t, :]).then_inc(stored, 16)
                sp.wait_ge(stored, 16 * NT)
        release(nc)


def chunks(w):
    k, n = w.shape
    if k <= P:
        return w.reshape(k, 1, n)
    return w.reshape(k // P, P, n).transpose(1, 0, 2)


def pad_heads(w, d=16, fill=0.0):
    lead = w.shape[:-1]
    out = np.zeros(lead + (w.shape[-1] // d, 2 * d), np.float32)
    out[..., :d] = w.reshape(lead + (-1, d))
    out[..., d] = fill
    return out.reshape(lead + (-1,))


def column(v):
    return v.reshape(-1, P).T


def row(v):
    return v.reshape(1, -1)


def swap_pairs(w):
    return w.reshape(w.shape[0], -1, 2)[:, :, ::-1].reshape(w.shape)


def rotary_tables():
    inv = (1.0 / 10000.0 ** (np.arange(0, 16, 2, dtype=np.float32) / 16)).astype(np.float32)
    ang = (np.arange(T, dtype=np.float32)[None, :] * inv[:, None]).astype(np.float32)
    cos, sin = np.zeros((2, P // D, D, B, T), np.float32)
    cos[:] = np.repeat(np.cos(ang), 2, axis=0)[None, :, None, :]
    sin[:, 0::2] = -np.sin(ang)[None, :, None, :]
    sin[:, 1::2] = np.sin(ang)[None, :, None, :]
    return cos.reshape(P, NTOK), sin.reshape(P, NTOK)


def everywhere(v):
    return np.broadcast_to(v.reshape(1, -1), (P, v.size))


def constants():
    i = np.arange(P)
    q, k = np.arange(T)[:, None], np.arange(T)[None, :]
    mask_q = np.where(k <= q, 0.0, MASKED).astype(np.float32)
    return {
        "ident": np.eye(P, dtype=np.float32),
        "sel32": (i[:, None] == i[None, :] // 32 * 32 + 16).astype(np.float32),
        "sel64": (i[:, None] == i[None, :] // 64 * 64 + 32).astype(np.float32),
        "ones": np.ones((P, P), np.float32),
        "comb": (i[:, None] % 32 == i[None, :32]).astype(np.float32),
        "comb0": ((i[:, None] % 32 == i[None, :32]) & (i[:, None] < 64)).astype(np.float32),
        "comb1": ((i[:, None] % 32 == i[None, :32]) & (i[:, None] >= 64)).astype(np.float32),
        "mask_q": chunks(mask_q),
        "mask_k": chunks(np.ascontiguousarray(mask_q.T)),
    }


def bfloat16_parts(x):
    out = []
    for _ in range(3):
        part = x.astype(np.float32)
        part = ((part.view(np.uint32) + 0x8000) & 0xFFFF0000).astype(np.uint32).view(np.float32)
        out.append(part)
        x = (x - part).astype(np.float32)
    return out


def alibi_tables():
    slopes = np.array([2.0 ** (-8.0 / H) * (2.0 ** (-8.0 / H)) ** i for i in range(H)], np.float32)
    pos = np.arange(T, dtype=np.float32)
    table = np.zeros((ALIBI_ROWS - SHIFT, H + 1, T), np.float32)
    table[3:6, :H] = np.stack(bfloat16_parts(4 * slopes))[:, :, None]
    table[6:9, :H] = bfloat16_parts(-4 * slopes[:, None] * pos)
    table[0:3, H] = 1
    table[3:6, H] = pos
    table[6:9, H] = 1
    return table


def layouts(i):
    cos, sin = rotary_tables()
    zero = np.zeros
    return {
        "consts": constants(),
        "L0_attn": {
            "q": chunks(i["L0_attn_q_w"].T), "k": chunks(i["L0_attn_k_w"].T),
            "v": chunks(pad_heads(i["L0_attn_v_w"].T)), "o": chunks(pad_heads(i["L0_attn_o_w"]).T),
            "bq": column(i["L0_attn_q_b"]), "bk": column(i["L0_attn_k_b"]),
            "bv": row(pad_heads(i["L0_attn_v_b"], fill=1.0)), "bo": row(i["L0_attn_o_b"]),
        },
        "L0_xattn": {
            "q": chunks(i["L0_xattn_Wq"]), "k": chunks(i["L0_xattn_Wk"]), "v": chunks(i["L0_xattn_Wv"]), "o": chunks(pad_heads(i["L0_xattn_Wp"].T).T),
            "bq": column(i["L0_xattn_bq"]), "bk": column(i["L0_xattn_bk"]), "bv": everywhere(i["L0_xattn_bv"]), "bo": row(i["L0_xattn_bp"]),
        },
        "L1_xattn": {
            "q": chunks(i["L1_xattn_w_q"].T), "k": chunks(i["L1_xattn_w_k"].T), "v": chunks(i["L1_xattn_w_v"].T), "o": chunks(pad_heads(i["L1_xattn_w_o"]).T),
            "bq": column(i["L1_xattn_b_q"]), "bk": column(i["L1_xattn_b_k"]), "bv": everywhere(i["L1_xattn_b_v"]), "bo": row(i["L1_xattn_b_o"]),
        },
        "L0_ffn": {
            "gate": chunks(i["L0_ffn_Wg"]), "iota_less": np.broadcast_to(np.arange(E, dtype=np.float32) - E, (P, 1, E)),
        },
        "L1_attn": {
            "qk": chunks(i["L1_attn_Wqkv"][:2 * C].T), "v": chunks(pad_heads(i["L1_attn_Wqkv"][2 * C:].T)), "o": chunks(i["L1_attn_Wout"].T),
            "gates": chunks(np.concatenate([i["L1_attn_Walpha"], i["L1_attn_Wimp"]]).T),
            "bqk": row(i["L1_attn_bqkv"][:2 * C]), "bv": row(pad_heads(i["L1_attn_bqkv"][2 * C:])), "bo": row(i["L1_attn_bout"]),
            "bgates": row(np.concatenate([i["L1_attn_balpha"], i["L1_attn_bimp"]])),
            "threshold": everywhere(i["L1_attn_spike_threshold"]), "qk_scale": everywhere(i["L1_attn_qk_scale"]),
            "log_k": everywhere(i["L1_attn_log_k"]),
        },
        "L3_xattn": {
            "q": chunks(i["L3_xattn_q_w"].T), "k": chunks(i["L3_xattn_k_w"]), "gate": chunks(i["L3_xattn_gate_w"].T),
            "gate_b": row(i["L3_xattn_gate_b"]), "norm_w": everywhere(i["L3_xattn_norm_w"]),
        },
        "L2_attn": {
            "in": chunks(i["L2_attn_W_in"]), "x": chunks(i["L2_attn_W_x"]), "out": chunks(i["L2_attn_W_out"]),
            "conv_w": chunks(i["L2_attn_conv_w"][:, 0, :]), "conv_b": column(i["L2_attn_conv_b"]), "dt": row(i["L2_attn_W_dt"]),
            "b_dt": column(i["L2_attn_b_dt"]), "A_log": everywhere(i["L2_attn_A_log"]), "D": column(i["L2_attn_D"]),
        },
        "L2_ffn": {
            "gate": chunks(i["L2_ffn_Wg"]), "iota": everywhere(np.arange(P, dtype=np.float32)),
            "before": chunks((np.arange(NTOK)[None, :] < np.arange(NTOK)[:, None]).astype(np.float32)),
            "b1": i["L2_ffn_b1"].reshape(E * FC, P).T, "b2": row(i["L2_ffn_b2"]),
        },
        "L3_ffn": {
            "q": chunks(i["L3_ffn_Wq"]), "qx": chunks(swap_pairs(i["L3_ffn_Wq"])),
            "kc": chunks(i["L3_ffn_Wk_c"]), "vc": chunks(i["L3_ffn_Wv_c"]),
            "k": chunks(i["L3_ffn_Wk"]), "kx": chunks(swap_pairs(i["L3_ffn_Wk"])),
            "v": chunks(pad_heads(i["L3_ffn_Wv"])), "o": chunks(pad_heads(i["L3_ffn_Wo"].T).T),
            "bv": row(pad_heads(zero(256, np.float32), fill=1.0)), "cos": cos, "sin": sin,
            "norm1_w": everywhere(i["L3_ffn_norm1_w"]), "norm2_w": everywhere(i["L3_ffn_norm2_w"]),
        },
        "L3_ffn_experts": {
            "in": chunks(i["L3_ffn_W_shared_in"]), "w1": chunks(i["L3_ffn_W1_shared"]), "out": chunks(i["L3_ffn_W_shared_out"]),
            "w2": chunks(i["L3_ffn_W2_experts"].reshape(-1, C)),
            "gates": chunks(np.concatenate([i["L3_ffn_Wg_gate"], i["L3_ffn_We_gate"]], axis=1)),
            "bgates": row(np.concatenate([i["L3_ffn_group_bias"], i["L3_ffn_expert_bias"]])),
        },
        "L1_ffn": {
            "r": chunks(i["L1_ffn_W_r"].T), "k": chunks(i["L1_ffn_W_k"].T), "v": chunks(i["L1_ffn_W_v"].T),
            "mu": np.concatenate([column(i["L1_ffn_mu_r"]), column(i["L1_ffn_mu_k"])], axis=1),
        },
        "L2_xattn": {
            "q": chunks(i["L2_xattn_Wq"].T), "k": chunks(i["L2_xattn_Wf"][:C].T),
            "v": chunks(pad_heads(i["L2_xattn_Wf"][C:].T)), "o": chunks(pad_heads(i["L2_xattn_Wp"]).T),
            "bq": column(i["L2_xattn_bq"]), "bk": column(i["L2_xattn_bf"][:C]),
            "bv": row(pad_heads(i["L2_xattn_bf"][C:], fill=1.0)), "bo": row(i["L2_xattn_bp"]),
            "Aq": chunks(i["L2_xattn_Aq"].T), "Af": chunks(i["L2_xattn_Af"].T), "Ap": chunks(pad_heads(i["L2_xattn_Ap"]).T),
            "Bq": chunks(i["L2_xattn_Bq"].T), "Bk": chunks(i["L2_xattn_Bf"][:C].T),
            "Bv": chunks(pad_heads(i["L2_xattn_Bf"][C:].T)), "Bp": chunks(i["L2_xattn_Bp"].T),
        },
        "L3_attn": {
            "q": chunks(i["L3_attn_Wq"]), "k": chunks(i["L3_attn_Wk"]),
            "v": chunks(pad_heads(i["L3_attn_Wv"], 32)), "o": chunks(pad_heads(i["L3_attn_Wo"].T, 32).T),
            "bv": row(pad_heads(zero(512, np.float32), 32, 1.0)),
        },
    }


def pack(blocks):
    n = sum(int(np.prod(b.shape[1:])) for b in blocks.values())
    packed = np.zeros((P, n), np.float32)
    at, spec = 0, {}
    for name, b in blocks.items():
        m = int(np.prod(b.shape[1:]))
        packed[:b.shape[0], at:at + m] = b.reshape(b.shape[0], m)
        spec[name] = (at, b.shape)
        at += m
    return packed, spec


def lay_out(inputs, layers=None):
    arrays, specs = {}, {}
    for name, blocks in layouts(inputs).items():
        if layers is not None and name.replace("_experts", "") not in layers and name != "consts":
            continue
        arrays[name], specs[name] = pack(blocks)
    arrays.update(big_arrays(inputs))
    return arrays, specs


def big_arrays(i):
    return {
        "x": i["x"], "ctx": i["ctx_1024"], "fside": i["fside_BxSxS_0"], "alibi": alibi_tables(),
        "W1": np.concatenate([i["L0_ffn_W1"], i["L0_ffn_w1s"][None]]),
        "W2": np.concatenate([i["L0_ffn_W2"], i["L0_ffn_w2s"][None]]),
        "W3": np.concatenate([i["L0_ffn_W3"], i["L0_ffn_w3s"][None]]),
        "M1": np.concatenate([i["L2_ffn_W1"], i["L2_ffn_W1"][:1]]),
        "M2": np.concatenate([i["L2_ffn_W2"], i["L2_ffn_W2"][:1]]),
    }


def kernel(**inputs):
    import numpy as _np
    import concourse.bacc as _bacc
    from concourse import mybir as _mybir
    from concourse.bass_utils import run_bass_kernel_spmd as _run

    nc = _bacc.Bacc("TRN2", target_bir_lowering=False, num_devices=1)
    arrays, specs = lay_out({k: _np.asarray(v) for k, v in inputs.items()})
    aps = {n: nc.dram_tensor(f"in_{n}", a.shape, _mybir.dt.float32, kind="ExternalInput").ap() for n, a in arrays.items()}
    out = nc.dram_tensor("out_x", (B, T, C), _mybir.dt.float32, kind="ExternalOutput").ap()
    build(nc, aps["x"], out, aps, specs)
    r = _run(nc, [{f"in_{n}": _np.ascontiguousarray(a) for n, a in arrays.items()}], core_ids=[0])
    return r.results[0]["out_x"]
```
